# Optimizing a Trainium2 kernel written in Bass

```python
import numpy as np
import jax
import jax.numpy as jnp

def _softmax(x, axis=-1):
    return jax.nn.softmax(x, axis=axis)

def _gelu(x):
    return jax.nn.gelu(x, approximate=True)

def _silu(x):
    return jax.nn.silu(x)

def _sigmoid(x):
    return jax.nn.sigmoid(x)

def _layernorm(x, axis=-1, eps=1e-05):
    m = jnp.mean(x, axis=axis, keepdims=True)
    v = jnp.var(x, axis=axis, keepdims=True)
    return (x - m) / jnp.sqrt(v + eps)

def _scatter_add(tgt, idx, src, axis=0):
    return tgt.at[idx].add(src)

def _segment_sum(src, seg, n):
    return jax.ops.segment_sum(src, seg, n)
kernel_name = 'mk_xattn_ffn_d2_seqx_r8_5f8f22'

def setup_inputs(seed: int=0):
    np.random.seed(seed)
    _w = jnp.asarray

    def _rec_inputs():
        import jax
        import jax.numpy as jnp
        _rk = jax.random.key(seed)
        x = -0.0002928 + 1 * jax.random.normal(jax.random.fold_in(_rk, 1), (8, 256, 128), jnp.float32)
        _lenS = 256 - jax.random.randint(jax.random.fold_in(_rk, 7), (8,), 0, max(1, 256 // 4) + 1, jnp.int32)
        _lenS2 = 256 - jax.random.randint(jax.random.fold_in(_rk, 8), (8,), 0, max(1, 256 // 4) + 1, jnp.int32)
        _ctx_1024P = jax.random.normal(jax.random.fold_in(_rk, 11), (8, 16, 128), jnp.float32)
        _ctx_1024c = jax.random.dirichlet(jax.random.fold_in(_rk, 511), 0.3 * jnp.ones((16,), jnp.float32), (8, 256))
        _ctx_1024t = jnp.einsum('bsk,bkd->bsd', _ctx_1024c, _ctx_1024P)
        _ctx_1024t = _ctx_1024t * jax.lax.rsqrt(jnp.mean(jnp.square(_ctx_1024t)) + 1e-12) * 0.953939
        ctx_1024 = -1.39393e-06 + 0.999914 * (_ctx_1024t + 0.3 * jax.random.normal(jax.random.fold_in(_rk, 611), (8, 256, 128), jnp.float32))
        return (x, ctx_1024)
    x, ctx_1024 = _rec_inputs()

    def _L0_xattn_setup():
        import jax, jax.numpy as jnp
        import numpy as np
        H, DK, DV = (16, 64, 64)
        MEM = 128
        D_MODEL = 128
        OUT_DIM = 128
        key = jax.random.key(seed)
        ks = jax.random.split(key, 12)
        B, S = (2, 256)
        scale = 1.0 / np.sqrt(D_MODEL)
        inp = {'queries': jax.random.normal(ks[0], (B, S, D_MODEL), jnp.float32), 'keys': jax.random.normal(ks[1], (B, S, D_MODEL), jnp.float32), 'values': jax.random.normal(ks[2], (B, S, D_MODEL), jnp.float32), 'wq_w': jax.random.normal(ks[3], (D_MODEL, H * DK), jnp.float32) * scale, 'wq_b': jnp.zeros((H * DK,), jnp.float32), 'wk_w': jax.random.normal(ks[4], (D_MODEL, H * DK), jnp.float32) * scale, 'wk_b': jnp.zeros((H * DK,), jnp.float32), 'wv_w': jax.random.normal(ks[5], (D_MODEL, H * DV), jnp.float32) * scale, 'wv_b': jnp.zeros((H * DV,), jnp.float32), 'mk': jax.random.normal(ks[6], (1, MEM, H * DK), jnp.float32) * (0.1 / DK), 'mv': jax.random.normal(ks[7], (1, MEM, H * DV), jnp.float32) * (0.1 / MEM), 'wo_w': jax.random.normal(ks[8], (H * DV, OUT_DIM), jnp.float32) * (1.0 / np.sqrt(H * DV)), 'wo_b': jnp.zeros((OUT_DIM,), jnp.float32)}
        return inp
    _L0_xattn_all = _L0_xattn_setup()
    _L0_xattn_in = {k: v for k, v in _L0_xattn_all.items() if k in ('wq_w', 'wq_b', 'wk_w', 'wk_b', 'wv_w', 'wv_b', 'mk', 'mv', 'wo_w', 'wo_b')}
    del _L0_xattn_all

    def _L0_ffn_setup():
        import jax, jax.numpy as jnp
        import numpy as np
        B, S, DIM, FFN, E = (4, 256, 128, 512, 8)
        key = jax.random.key(seed)
        k0, k1, k2, k3 = jax.random.split(key, 4)
        scale = 0.02
        return {'hidden_states': jax.random.normal(k0, (B, S, DIM), jnp.float32), 'router_w': jax.random.normal(k1, (DIM, E), jnp.float32) * scale, 'router_b': jnp.zeros((E,), jnp.float32), 'w1': jax.random.normal(k2, (E, DIM, 2 * FFN), jnp.float32) * scale, 'w2': jax.random.normal(k3, (E, FFN, DIM), jnp.float32) * scale}
    _L0_ffn_all = _L0_ffn_setup()
    _L0_ffn_in = {k: v for k, v in _L0_ffn_all.items() if k in ('router_w', 'router_b', 'w1', 'w2')}
    del _L0_ffn_all

    def _L1_xattn_setup():
        import jax, jax.numpy as jnp
        import numpy as np
        B, L, DM, H = (2, 512, 128, 16)
        D = DM // H

        def _split_heads(x):
            b, l, _ = x.shape
            return x.reshape(b, l, H, D).transpose(0, 2, 1, 3)
        key = jax.random.key(seed)
        ks = jax.random.split(key, 11)
        s = 1.0 / np.sqrt(DM)
        return {'query': jax.random.normal(ks[0], (B, L, DM), jnp.float32), 'key': jax.random.normal(ks[1], (B, L, DM), jnp.float32), 'value': jax.random.normal(ks[2], (B, L, DM), jnp.float32), 'Wq': jax.random.normal(ks[3], (DM, DM), jnp.float32) * s, 'bq': jnp.zeros((DM,), jnp.float32), 'Wk': jax.random.normal(ks[4], (DM, DM), jnp.float32) * s, 'bk': jnp.zeros((DM,), jnp.float32), 'Wv': jax.random.normal(ks[5], (DM, DM), jnp.float32) * s, 'bv': jnp.zeros((DM,), jnp.float32), 'Wo': jax.random.normal(ks[6], (DM, DM), jnp.float32) * s, 'bo': jnp.zeros((DM,), jnp.float32)}
    _L1_xattn_all = _L1_xattn_setup()
    _L1_xattn_in = {k: v for k, v in _L1_xattn_all.items() if k in ('Wq', 'bq', 'Wk', 'bk', 'Wv', 'bv', 'Wo', 'bo')}
    del _L1_xattn_all

    def _L1_ffn_setup():
        import jax, jax.numpy as jnp
        import numpy as np
        B, S, D, F, E = (4, 256, 128, 512, 8)
        key = jax.random.key(seed)
        ks = jax.random.split(key, 7)
        s1 = 1.0 / np.sqrt(D)
        s2 = 1.0 / np.sqrt(F)
        x = jax.random.normal(ks[0], (B, S, D), dtype=jnp.float32)
        W1 = jax.random.uniform(ks[1], (E, D, F), jnp.float32, -s1, s1)
        b1 = jax.random.uniform(ks[2], (E, F), jnp.float32, -s1, s1)
        W2 = jax.random.uniform(ks[3], (E, F, D), jnp.float32, -s2, s2)
        b2 = jax.random.uniform(ks[4], (E, D), jnp.float32, -s2, s2)
        Wr = jax.random.uniform(ks[5], (D, E), jnp.float32, -s1, s1)
        br = jax.random.uniform(ks[6], (E,), jnp.float32, -s1, s1)
        return {'x': x, 'W1': W1, 'b1': b1, 'W2': W2, 'b2': b2, 'Wr': Wr, 'br': br}
    _L1_ffn_all = _L1_ffn_setup()
    _L1_ffn_in = {k: v for k, v in _L1_ffn_all.items() if k in ('W1', 'b1', 'W2', 'b2', 'Wr', 'br')}
    del _L1_ffn_all
    return {'x': x, 'ctx_1024': ctx_1024, 'L0_xattn_wq_w': _L0_xattn_in['wq_w'], 'L0_xattn_wq_b': _L0_xattn_in['wq_b'], 'L0_xattn_wk_w': _L0_xattn_in['wk_w'], 'L0_xattn_wk_b': _L0_xattn_in['wk_b'], 'L0_xattn_wv_w': _L0_xattn_in['wv_w'], 'L0_xattn_wv_b': _L0_xattn_in['wv_b'], 'L0_xattn_mk': _L0_xattn_in['mk'], 'L0_xattn_mv': _L0_xattn_in['mv'], 'L0_xattn_wo_w': _L0_xattn_in['wo_w'], 'L0_xattn_wo_b': _L0_xattn_in['wo_b'], 'L0_ffn_router_w': _L0_ffn_in['router_w'], 'L0_ffn_router_b': _L0_ffn_in['router_b'], 'L0_ffn_w1': _L0_ffn_in['w1'], 'L0_ffn_w2': _L0_ffn_in['w2'], 'L1_xattn_Wq': _L1_xattn_in['Wq'], 'L1_xattn_bq': _L1_xattn_in['bq'], 'L1_xattn_Wk': _L1_xattn_in['Wk'], 'L1_xattn_bk': _L1_xattn_in['bk'], 'L1_xattn_Wv': _L1_xattn_in['Wv'], 'L1_xattn_bv': _L1_xattn_in['bv'], 'L1_xattn_Wo': _L1_xattn_in['Wo'], 'L1_xattn_bo': _L1_xattn_in['bo'], 'L1_ffn_W1': _L1_ffn_in['W1'], 'L1_ffn_b1': _L1_ffn_in['b1'], 'L1_ffn_W2': _L1_ffn_in['W2'], 'L1_ffn_b2': _L1_ffn_in['b2'], 'L1_ffn_Wr': _L1_ffn_in['Wr'], 'L1_ffn_br': _L1_ffn_in['br']}

def reference(x, ctx_1024, L0_xattn_wq_w, L0_xattn_wq_b, L0_xattn_wk_w, L0_xattn_wk_b, L0_xattn_wv_w, L0_xattn_wv_b, L0_xattn_mk, L0_xattn_mv, L0_xattn_wo_w, L0_xattn_wo_b, L0_ffn_router_w, L0_ffn_router_b, L0_ffn_w1, L0_ffn_w2, L1_xattn_Wq, L1_xattn_bq, L1_xattn_Wk, L1_xattn_bk, L1_xattn_Wv, L1_xattn_bv, L1_xattn_Wo, L1_xattn_bo, L1_ffn_W1, L1_ffn_b1, L1_ffn_W2, L1_ffn_b2, L1_ffn_Wr, L1_ffn_br):
    import jax
    import jax.numpy as jnp

    def _L0_xattn_ref(queries, keys, values, wq_w, wq_b, wk_w, wk_b, wv_w, wv_b, mk, mv, wo_w, wo_b):
        import jax, jax.numpy as jnp
        import numpy as np
        H, DK, DV = (16, 64, 64)
        MEM = 128
        D_MODEL = 128
        OUT_DIM = 128
        B, S, _ = queries.shape
        q = (queries @ wq_w + wq_b).reshape(B, S, H, DK).transpose(0, 2, 1, 3)
        k_proj = keys @ wk_w + wk_b
        v_proj = values @ wv_w + wv_b
        k_ext = jnp.concatenate([k_proj, jnp.broadcast_to(mk, (B, MEM, H * DK))], axis=1)
        v_ext = jnp.concatenate([v_proj, jnp.broadcast_to(mv, (B, MEM, H * DV))], axis=1)
        T = S + MEM
        k = k_ext.reshape(B, T, H, DK).transpose(0, 2, 1, 3)
        v = v_ext.reshape(B, T, H, DV).transpose(0, 2, 1, 3)
        scores = jnp.einsum('bhsd,bhtd->bhst', q, k) / jnp.sqrt(jnp.float32(DK))
        attn = jax.nn.softmax(scores, axis=-1)
        out = jnp.einsum('bhst,bhtd->bhsd', attn, v)
        out = out.transpose(0, 2, 1, 3).reshape(B, S, H * DV)
        return out @ wo_w + wo_b

    def _L0_ffn_ref(hidden_states, router_w, router_b, w1, w2):
        import jax, jax.numpy as jnp
        import numpy as np
        B, S, DIM, FFN, E = (4, 256, 128, 512, 8)
        b, s, d = hidden_states.shape
        x = hidden_states.reshape(-1, d)
        logits = x @ router_w + router_b
        route = jax.nn.softmax(logits, axis=1)
        max_prob = jnp.max(route, axis=1, keepdims=True)
        max_ind = jnp.argmax(route, axis=1)
        out = jnp.zeros_like(x)
        num_experts = w1.shape[0]
        for e in range(num_experts):
            h = x @ w1[e]
            a, g = jnp.split(h, 2, axis=1)
            y = jax.nn.silu(a) * g @ w2[e]
            out = jnp.where((max_ind == e)[:, None], y, out)
        out = out * max_prob
        return out.reshape(b, s, d)

    def _L1_xattn_ref(query, key, value, Wq, bq, Wk, bk, Wv, bv, Wo, bo):
        import jax, jax.numpy as jnp
        import numpy as np
        B, L, DM, H = (2, 512, 128, 16)
        D = DM // H

        def _split_heads(x):
            b, l, _ = x.shape
            return x.reshape(b, l, H, D).transpose(0, 2, 1, 3)
        q = _split_heads(query @ Wq + bq)
        k = _split_heads(key @ Wk + bk)
        v = _split_heads(value @ Wv + bv)
        q = jax.nn.elu(q) + 1.0
        k = jax.nn.elu(k) + 1.0
        S = jnp.einsum('bhle,bhld->bhed', k, q)
        out = jnp.einsum('bhme,bhed->bhmd', v, S)
        denom = jnp.einsum('bhld,bhld->bhl', q, k) + 1e-06
        out = out / denom[..., None]
        out = out.transpose(0, 2, 1, 3).reshape(out.shape[0], -1, DM)
        return out @ Wo + bo

    def _L1_ffn_ref(x, W1, b1, W2, b2, Wr, br):
        import jax, jax.numpy as jnp
        import numpy as np
        B, S, D, F, E = (4, 256, 128, 512, 8)
        b, s, d = x.shape
        e = Wr.shape[1]
        logits = x @ Wr + br
        idx = jnp.argmax(logits, axis=-1)
        probs = jax.nn.softmax(logits, axis=-1)
        gates = jnp.take_along_axis(probs, idx[..., None], axis=-1)[..., 0]
        xf = x.reshape(-1, d)
        idxf = idx.reshape(-1)
        gf = gates.reshape(-1)
        out = jnp.zeros_like(xf)
        for ei in range(e):
            h = jax.nn.gelu(xf @ W1[ei] + b1[ei], approximate=False)
            y = h @ W2[ei] + b2[ei]
            mask = (idxf == ei).astype(xf.dtype)
            out = out + y * (gf * mask)[:, None]
        return out.reshape(b, s, d)
    x = x + _L0_xattn_ref(_layernorm(x, axis=-1), ctx_1024, ctx_1024, L0_xattn_wq_w, L0_xattn_wq_b, L0_xattn_wk_w, L0_xattn_wk_b, L0_xattn_wv_w, L0_xattn_wv_b, L0_xattn_mk, L0_xattn_mv, L0_xattn_wo_w, L0_xattn_wo_b)
    x = x + _L0_ffn_ref(_layernorm(x, axis=-1), L0_ffn_router_w, L0_ffn_router_b, L0_ffn_w1, L0_ffn_w2)
    x = x + _L1_xattn_ref(_layernorm(x, axis=-1), ctx_1024, ctx_1024, L1_xattn_Wq, L1_xattn_bq, L1_xattn_Wk, L1_xattn_bk, L1_xattn_Wv, L1_xattn_bv, L1_xattn_Wo, L1_xattn_bo)
    x = x + _L1_ffn_ref(_layernorm(x, axis=-1), L1_ffn_W1, L1_ffn_b1, L1_ffn_W2, L1_ffn_b2, L1_ffn_Wr, L1_ffn_br)
    return x

_drawn_inputs = setup_inputs


def setup_inputs(seed=0):
    import zlib

    import numpy as np

    out = dict(_drawn_inputs(seed))
    spreads = {'L0_xattn_wq_b': (0.0, 0.8),
     'L0_xattn_wk_b': (0.0, 0.8),
     'L0_xattn_wv_b': (0.0, 0.1),
     'L0_xattn_wo_b': (0.0, 0.1),
     'L0_ffn_router_b': (0.0, 0.8),
     'L1_xattn_bq': (0.0, 0.1),
     'L1_xattn_bk': (0.0, 0.1),
     'L1_xattn_bv': (0.0, 0.1),
     'L1_xattn_bo': (0.0, 2.0)}
    factors = {'L0_xattn_mk': 200.0,
     'L0_xattn_mv': 200.0,
     'L0_ffn_router_w': 8.0,
     'L0_ffn_w1': 8.0,
     'L0_ffn_w2': 8.0,
     'L1_ffn_W1': 8.0,
     'L1_ffn_b1': 48.2,
     'L1_ffn_W2': 8.0,
     'L1_ffn_b2': 200.0,
     'L1_ffn_Wr': 8.0,
     'L1_ffn_br': 8.0}
    for name, (base, spread) in spreads.items():
        noise = np.random.default_rng([zlib.crc32(name.encode()), seed]).standard_normal(out[name].shape)
        drawn = base * np.exp(spread * noise) if base else spread * noise
        out[name] = jnp.asarray(drawn.astype(out[name].dtype))
    for name, factor in factors.items():
        out[name] = (out[name] * factor).astype(out[name].dtype)
    return out
```

```python
from contextlib import ExitStack

import concourse.bass as bass
from concourse import mybir

F32 = mybir.dt.float32
F32R = mybir.dt.float32r
BF16 = mybir.dt.bfloat16
I32 = mybir.dt.int32
U32 = mybir.dt.uint32
ACT = mybir.ActivationFunctionType
ALU = mybir.AluOpType
AX_X = mybir.AxisListType.X

P = 128
D = 128
B, S = 8, 256
NT = B * S // P
ST = S // P
H, DK = 16, 64
HP = H // 2
HD = H * DK
MEM = 128
T = S + MEM
KT = T // P
E = 8
FF = 512
FK = FF // P
SLOT_TILES = (B * S + E * (P - 1)) // P
H1, D1 = 16, 8
EPS = 1e-5
ROW = 2 * D + 2
RING = 4
NO_TOKEN = 1 << 20
G4 = NT // 4
PRING = 4


def f32(ap):
    return ap.bitcast(F32)


def build(nc, io):
    ctx = ExitStack()
    with ctx:
        def sb(name, shape, dt=F32):
            return ctx.enter_context(nc.sbuf_tensor(name, shape, dt))

        def sem(name):
            return ctx.enter_context(nc.semaphore(name))

        ident = sb("ident", [P, P])
        x_in = sb("x_in", [P, NT, D])
        x_res = sb("x_res", [P, NT, D])
        w1_0 = sb("w1_0", [P, E, 2 * FF])
        upper = sb("upper", [P, P], BF16)
        ones = sb("ones", [P, P], BF16)
        before = sb("before", [P, E, E])
        first = sb("first", [P, E])
        tile_no = sb("tile_no", [P, SLOT_TILES])
        block_mask = sb("block_mask", [P, D])
        first_i = sb("first_i", [P, E], I32)
        tile_no_i = sb("tile_no_i", [P, SLOT_TILES], I32)
        token_no = sb("token_no", [P, NT], I32)
        empty_row = sb("empty_row", [P, ROW])
        bias_row = sb("bias_row", [P, 2 + 3 + 2, D])
        bo0_bc = bias_row[:, 0, :]
        bq1_bc, bk1_bc, bo1_bc = (bias_row[:, i, :] for i in (1, 2, 3))
        router = sb("router", [P, 2, E])
        rb_bc = sb("rb_bc", [P, 2, E])
        bv1 = sb("bv1", [P, 1])
        w_attn1 = sb("w_attn1", [P, 4, D])
        stats = sb("stats", [P, NT, 6])
        meanvar = sb("meanvar", [P, NT, 2])
        rstd = sb("rstd", [P, NT])
        nt_a = sb("nt_a", [P, NT])
        nt_b = sb("nt_b", [P, NT])
        ctx_t = sb("ctx_t", [P, B, S])
        phase = ExitStack()

        def tmp(name, shape, dt=F32):
            return phase.enter_context(nc.sbuf_tensor(name, shape, dt))

        w_hi = tmp("w_hi", [P, 3, HD], F32R)
        w_lo = tmp("w_lo", [P, 3, HD], F32R)
        bqk = tmp("bqk", [P, 2, HP])
        bqk_s = tmp("bqk_s", [P, 2, HP])
        bv_bc = tmp("bv_bc", [P, HD])
        wo0 = tmp("wo0", [P, H, D])
        xn = tmp("xn", [P, ST, D])
        xt_hi = tmp("xt_hi", [P, S], F32R)
        xt_lo = tmp("xt_lo", [P, S], F32R)
        ct_hi = tmp("ct_hi", [P, S], F32R)
        ct_lo = tmp("ct_lo", [P, S], F32R)
        k_hi = tmp("k_hi", [P, HP, T], F32R)
        k_lo = tmp("k_lo", [P, HP, T], F32R)
        q_hi = tmp("q_hi", [P, 2, S], F32R)
        q_lo = tmp("q_lo", [P, 2, S], F32R)
        v_tmp = tmp("v_tmp", [P, ST * 2, 512])
        v_hl = tmp("v_hl", [P, KT, H, 2, DK], F32R)
        probs = tmp("probs", [P, PRING, ST, T])
        nmax = tmp("nmax", [P, PRING, ST])
        psums = tmp("psums", [P, PRING, ST])
        rsums = tmp("rsums", [P, PRING, ST])
        pt_hi = tmp("pt_hi", [P, 2, KT * S], F32R)
        pt_lo = tmp("pt_lo", [P, 2, KT * S], F32R)
        ot = tmp("ot", [P, H, S])
        wraw = ot[:, 0:12, :].rearrange("p (w a) c -> p w (a c)", w=3)
        mk_raw = ot[:, 12:16, :].rearrange("p a (b c) -> p (a b) c", c=MEM)

        phase.close()
        phase = ctx
        w2_0 = tmp("w2_0", [P, E, FK, D])
        w1_1 = tmp("w1_1", [P, E, FF])
        w2_1 = tmp("w2_1", [P, E, FK, D])
        b1_bc = tmp("b1_bc", [P, E, FF])
        b2_bc = tmp("b2_bc", [P, E, D])
        rows = tmp("rows", [P, NT, ROW])
        onehot = tmp("onehot", [P, NT + 1, E], BF16)
        logits = tmp("logits", [P, NT, E])
        chosen = tmp("chosen", [P, NT, E])
        scr = tmp("scr", [P, NT, E])
        col = [tmp(f"col{i}", [P, NT]) for i in range(3)]
        counts = tmp("counts", [P, E])
        counts_i = tmp("counts_i", [P, E], I32)
        tiles_f = tmp("tiles_f", [P, E])
        base = tmp("base", [P, E])
        sq = tmp("sq", [P, E, E])
        cmp_t = tmp("cmp_t", [P, SLOT_TILES, E])
        texp_f = tmp("texp_f", [P, SLOT_TILES])
        texp = [tmp(f"texp{i}", [P, SLOT_TILES], I32) for i in range(2)]
        slot_f = tmp("slot_f", [P, NT])
        slot = [tmp(f"slot{i}", [P, NT], I32) for i in range(2)]
        xt4 = tmp("xt4", [P, 2, 4, P])
        xg = tmp("xg", [P, RING, ROW])
        xgt = tmp("xgt", [P, 2, P])
        act_t = tmp("act_t", [P, 2, FF])
        gm = tmp("gm", [P, 2, FF])
        gt = tmp("gt", [P, 2, FF])
        yb = tmp("yb", [P, 2, D])
        yo = tmp("yo", [P, RING, D])
        k1 = tmp("k1", [P, NT, D])
        q1 = rows[:, :, D:2 * D]
        v1t = tmp("v1t", [P, NT, P])
        z1 = tmp("z1", [P, 2, 4, D])
        e1 = tmp("e1", [P, 2, 4, D])
        s1 = tmp("s1", [P, B, D])
        den = tmp("den", [P, NT, H1])

        s_all = ctx.enter_context(nc.psum_tensor("s_all", [P, 4, 512], F32))
        s_ps = [s_all[:, i, :] for i in range(4)]
        pta = ctx.enter_context(nc.psum_tensor("pta", [P, 512], F32))
        ptb = ctx.enter_context(nc.psum_tensor("ptb", [P, 512], F32))
        o_ps = ctx.enter_context(nc.psum_tensor("o_ps", [P, 512], F32))
        m_ps = ctx.enter_context(nc.psum_tensor("m_ps", [P, 512], F32))

        bank = [s_all[:, i, :] for i in range(4)] + [pta[:], ptb[:], o_ps[:], m_ps[:]]

        slots = [nc.dram_tensor(f"slots{i}", [SLOT_TILES * P, ROW], F32, kind="Internal").ap() for i in range(2)]
        x2_dram = nc.dram_tensor("x2_dram", [B * S, D], F32, kind="Internal").ap()

        sems = {}

        names = ("x_loaded ctx_loaded w_loaded small_loaded ident_made xb_made prepared "
                 "stats_done ln_done dve_self pool_self split_hi split_done "
                 "xn_ready ct_ready xt_ps xt_hi_done xt_done v_ps v_tmp_done v_hi_done v_done "
                 "k_ps k_hi_done k_done q_ps q_hi_done q_done "
                 "scores_ps max_done exp_done recip_done probs0_done probs1_done pta_ps ptb_ps pta_hi ptb_hi pta_done ptb_done "
                 "o_ps_done ot_done wo_ps x1_done stored").split()
        for n in names:
            sems[n] = sem(n)

        for i in range(3):
            for n in "ln_var ln_rs ln_out".split():
                sems[f"{n}{i}"] = sem(f"{n}{i}")
        for i in range(2):
            for n in ("xt4_ps xt4_done logits_ps onehot_done shifted exps_done ranks_ps gates_done rows_x rows_id texp_done "
                      "slot_done scattered tx_ps xgt_done ha_ps hb_ps act_done gm_done gt_ps gt_done y_ps yb_done "
                      "yo_done").split():
                sems[f"{n}{i}"] = sem(f"{n}{i}")
            for c in range(RING):
                for n in "xg_loaded y_stored".split():
                    sems[f"{n}{i}_{c}"] = sem(f"{n}{i}_{c}")
        for n in ("r_loaded w1_loaded w2_loaded l1_loaded empty_made prefilled consts_made act_self x2_loaded xb1_done "
                  "kq_ps mn_done ex1_done kq_done v1_ps v1_done s1_ps s1_done o1_ps o1_done ot1_ps ot1_done wo1_ps x3_done "
                  "xta_ps xta_done").split():
            sems[n] = sem(n)
        sem_of = sems.__getitem__

        class Tile:

            def __init__(self, lap, c):
                self.lap, self.c = (lap + c // RING, c % RING)
                self.n = self.lap * RING + self.c

            def at(self, k):
                return Tile(self.lap, self.c + k)

        def wait(eng, name, value):
            if not isinstance(value, int) or value > 0:
                eng.wait_ge(sem_of(name), value)

        def expert_steps(eng, step):
            laps = SLOT_TILES // RING
            for c in range(RING):
                step(Tile(0, c))
            with eng.Fori(1, laps) as lap:
                for c in range(RING):
                    step(Tile(lap, c))
            for n in range(laps * RING, SLOT_TILES + 1):
                step(Tile(n // RING, n % RING))

        block = ctx.enter_context(nc.Block())

        @block.sync
        def _(sp):
            sp.dma_start(x_in[:], io["x"].rearrange("(t p) d -> p t d", p=P)).then_inc(sems["x_loaded"], 16)
            sp.dma_start(bo0_bc, io["bo0"].broadcast_to([P, D])).then_inc(sems["small_loaded"], 16)
            sp.dma_start(wraw[:, 0, :], io["wq0"]).then_inc(sems["w_loaded"], 16)
            sp.dma_start(wraw[:, 1, :], io["wk0"]).then_inc(sems["w_loaded"], 16)
            sp.dma_start(wraw[:, 2, :], io["wv0"]).then_inc(sems["w_loaded"], 16)
            sp.dma_start(mk_raw, io["mk0"]).then_inc(sems["w_loaded"], 16)
            sp.dma_start(wo0[0:DK], io["wo0"]).then_inc(sems["small_loaded"], 16)
            sp.dma_start(wo0[DK:P], io["wo0"]).then_inc(sems["small_loaded"], 16)
            for i, n in enumerate(("wr0", "wr1")):
                sp.dma_start(router[:, i, :], io[n]).then_inc(sems["r_loaded"], 16)
            for i, n in enumerate(("br0", "br1")):
                sp.dma_start(rb_bc[:, i, :], io[n].broadcast_to([P, E])).then_inc(sems["r_loaded"], 16)
            for i, n in enumerate(("bq1", "bk1", "bo1")):
                sp.dma_start(bias_row[:, 1 + i, :], io[n].broadcast_to([P, D])).then_inc(sems["r_loaded"], 16)
            for i, n in enumerate(("wq1", "wk1", "wv1", "wo1")):
                sp.dma_start(w_attn1[:, i, :], io[n]).then_inc(sems["r_loaded"], 16)
            sp.dma_start(bv1[:], io["bv1"]).then_inc(sems["r_loaded"], 16)
            sp.dma_start(w1_0[:], io["w1_0"]).then_inc(sems["w1_loaded"], 16)
            sp.wait_ge(sems["empty_made"], 2)
            for i in range(2):
                sp.dma_start(slots[i].rearrange("(j p) c -> p j c", p=P),
                             empty_row[:].rearrange("p (a c) -> p a c", a=1).broadcast_to([P, SLOT_TILES, ROW])
                             ).then_inc(sems["prefilled"], 16)
            sp.wait_ge(sems["x1_done"], ST * B + 1)
            sp.dma_start(w2_0[:], io["w2_0"]).then_inc(sems["w2_loaded"], 16)

            def load_slots(layer):
                sp.wait_ge(sem_of(f"scattered{layer}"), 16 * NT)

                def step(j):
                    if isinstance(j.lap, int) and j.n >= SLOT_TILES:
                        return
                    wait(sp, f"y_stored{layer}_{j.c}", 16 * j.lap)
                    sp.dma_start(xg[:, j.c, :], slots[layer][bass.ds(j.n * P, P), :]).then_inc(
                        sem_of(f"xg_loaded{layer}_{j.c}"), 16)
                expert_steps(sp, step)
                for c in range(RING):
                    sp.wait_ge(sem_of(f"y_stored{layer}_{c}"), 16 * ((SLOT_TILES - c + RING - 1) // RING))

            load_slots(0)
            sp.dma_start(x_res[:], x2_dram.rearrange("(t p) d -> p t d", p=P)).then_inc(sems["x2_loaded"], 16)
            load_slots(1)

        @block.gpsimd
        def _(pool):
            nc.gpsimd.memset(ident[:], 0.0).then_inc(sems["pool_self"], 1)
            pool.wait_ge(sems["pool_self"], 1)
            nc.gpsimd.affine_select(out=ident[:], in_=ident[:], compare_op=ALU.not_equal, fill=1.0, base=0,
                                    pattern=[[-1, P]], channel_multiplier=1).then_inc(sems["ident_made"], 1)
            nc.gpsimd.memset(empty_row[:], 0.0).then_inc(sems["empty_made"], 1)
            pool.wait_ge(sems["empty_made"], 1)
            nc.gpsimd.memset(empty_row[:, 2 * D:2 * D + 1].bitcast(I32), NO_TOKEN).then_inc(sems["empty_made"], 1)
            pool.wait_ge(sems["small_loaded"], 16 * 7)
            pool.wait_ge(sems["x_loaded"], 16)
            pool.wait_ge(sems["ctx_loaded"], 16)

            def stage_ctx(b, part):
                src = ctx_t[:, bass.ds(b, 1), :].rearrange("p a s -> p (a s)")
                if part == 0:
                    nc.gpsimd.tensor_copy(ct_hi[:], src).then_inc(sems["pool_self"], 1)
                else:
                    nc.gpsimd.tensor_tensor(ct_lo[:], src, f32(ct_hi[:]), ALU.subtract).then_inc(sems["ct_ready"], 1)

            def units(b, nxt):
                for i in range(H + 1):
                    if i >= 1:
                        u = i - 1
                        pool.wait_ge(sems["recip_done"], b * H + u + 1)
                        staging = u == H - 1 and nxt
                        for n, c in enumerate((0, T // 2) if staging else (0,)):
                            if n:
                                pool.wait_ge(sems["pool_self"], b + 3)
                            p = probs[:, u % PRING, 1, c:c + (T // 2 if staging else T)]
                            last = nc.gpsimd.tensor_tensor(p, p, rsums[:, u % PRING, 1:2].broadcast_to([P, p.shape[1]]), ALU.mult)
                        last.then_inc(sems["probs1_done"], 1)
                    if i == H - 1 and nxt:
                        stage_ctx(b + 1, 0)
                    if i == H and nxt:
                        stage_ctx(b + 1, 1)

            stage_ctx(0, 0)
            pool.wait_ge(sems["pool_self"], 2)
            stage_ctx(0, 1)
            nc.gpsimd.tensor_tensor(x_res[:], x_in[:], bo0_bc.rearrange("p (a d) -> p a d", a=1).broadcast_to([P, NT, D]),
                                    ALU.add).then_inc(sems["xb_made"], 1)
            nc.gpsimd.memset(upper[:], 1.0).then_inc(sems["consts_made"], 1)
            nc.gpsimd.memset(ones[:], 1.0).then_inc(sems["consts_made"], 1)
            nc.gpsimd.memset(before[:], 1.0).then_inc(sems["consts_made"], 1)
            nc.gpsimd.memset(block_mask[:], 1.0).then_inc(sems["consts_made"], 1)
            nc.gpsimd.iota(first_i[:], pattern=[[-1, E]], base=E, channel_multiplier=0).then_inc(sems["consts_made"], 1)
            nc.gpsimd.iota(tile_no_i[:], pattern=[[1, SLOT_TILES]], base=0, channel_multiplier=0).then_inc(sems["consts_made"], 1)
            nc.gpsimd.iota(token_no[:], pattern=[[P, NT]], base=0, channel_multiplier=1).then_inc(sems["consts_made"], 1)
            pool.wait_ge(sems["consts_made"], 7)
            nc.gpsimd.affine_select(out=upper[:], in_=upper[:], compare_op=ALU.is_gt, fill=0.0, base=0,
                                    pattern=[[1, P]], channel_multiplier=-1).then_inc(sems["consts_made"], 1)
            nc.gpsimd.affine_select(out=before[:], in_=before[:], compare_op=ALU.is_gt, fill=0.0, base=0,
                                    pattern=[[1, E], [-1, E]], channel_multiplier=0).then_inc(sems["consts_made"], 1)
            mask = block_mask[:].rearrange("p (h d) -> p h d", d=D1)
            nc.gpsimd.affine_select(out=mask, in_=mask, compare_op=ALU.is_ge, fill=0.0, base=0,
                                    pattern=[[-D1, H1], [0, D1]], channel_multiplier=1).then_inc(sems["consts_made"], 1)
            nc.gpsimd.tensor_copy(first[:], first_i[:]).then_inc(sems["consts_made"], 1)
            nc.gpsimd.tensor_copy(tile_no[:], tile_no_i[:]).then_inc(sems["consts_made"], 1)
            pool.wait_ge(sems["consts_made"], 12)
            nc.gpsimd.affine_select(out=mask, in_=mask, compare_op=ALU.is_ge, fill=0.0, base=D1 - 1,
                                    pattern=[[D1, H1], [0, D1]], channel_multiplier=-1).then_inc(sems["consts_made"], 1)
            with pool.Fori(0, B - 1) as b:
                units(b, True)
            units(B - 1, False)

            def route(layer):
                if layer == 0:
                    pool.wait_ge(sems["x1_done"], ST * B + 1)
                else:
                    pool.wait_ge(sems["x3_done"], G4)
                nc.gpsimd.tensor_copy(rows[:, :, 2 * D].bitcast(I32), token_no[:]).then_inc(sem_of(f"rows_id{layer}"), 1)
                pool.wait_ge(sem_of(f"rows_id{layer}"), 1)
                pool.wait_ge(sem_of(f"rows_x{layer}"), 1)
                pool.wait_ge(sem_of(f"gates_done{layer}"), 1)
                pool.wait_ge(sem_of(f"slot_done{layer}"), 1)
                pool.wait_ge(sems["prefilled"], 32)
                for t in range(NT):
                    nc.gpsimd.indirect_dma_start(slots[layer], bass.IndirectOffsetOnAxis(ap=slot[layer][:, t:t + 1], axis=0),
                                                 rows[:, t, :], None).then_inc(sem_of(f"scattered{layer}"), 16)

                for n in range(SLOT_TILES):
                    c = n % RING
                    pool.wait_ge(sem_of(f"yo_done{layer}"), n + 1)
                    nc.gpsimd.indirect_dma_start((x2_dram, io["out"])[layer],
                                                 bass.IndirectOffsetOnAxis(ap=xg[:, c, 2 * D:2 * D + 1].bitcast(I32), axis=0),
                                                 yo[:, c, :], None, bounds_check=B * S - 1,
                                                 oob_is_err=False).then_inc(sem_of(f"y_stored{layer}_{c}"), 16)

            route(0)
            pool.wait_ge(sems["ln_out1"], G4)
            nc.gpsimd.tensor_tensor(x_res[:], x_res[:], bo1_bc.rearrange("p (a d) -> p a d", a=1).broadcast_to([P, NT, D]),
                                    ALU.add).then_inc(sems["xb1_done"], 1)
            route(1)

        @block.scalar
        def _(act):
            act.dma_start(ctx_t[:], io["ctx"]).then_inc(sems["ctx_loaded"], 16)
            act.dma_start(bqk[:, 0, :], io["bq0"]).then_inc(sems["small_loaded"], 16)
            act.dma_start(bqk[:, 1, :], io["bk0"]).then_inc(sems["small_loaded"], 16)
            act.dma_start(bv_bc[:], io["bv0"].broadcast_to([P, HD])).then_inc(sems["small_loaded"], 16)
            act.dma_start(v_tmp[:, 0:2, :], io["mv0"].rearrange("p (a c) -> p a c", a=2)).then_inc(sems["small_loaded"], 16)

            act.wait_ge(sems["stats_done"], 1)
            nc.scalar.activation(nt_b[:], nt_a[:], ACT.Ln).then_inc(sems["split_hi"], 1)
            act.wait_ge(sems["split_hi"], 1)
            nc.scalar.activation(rstd[:], nt_b[:], ACT.Exp, scale=-0.5).then_inc(sems["split_hi"], 1)
            act.wait_ge(sems["w_loaded"], 16 * 4)
            act.wait_ge(sems["small_loaded"], 16 * 7)
            for w in range(3):
                nc.scalar.activation(w_hi[:, w, :], wraw[:, w, :], ACT.Copy,
                                     scale=0.125 if w == 0 else 1.0).then_inc(sems["split_hi"], 1)
            nc.scalar.activation(k_hi[:, :, S:T], mk_raw, ACT.Copy).then_inc(sems["split_hi"], 1)
            for half in range(2):
                nc.scalar.activation(v_hl[:, KT - 1, half * 8:half * 8 + 8, 0, :],
                                     v_tmp[:, half, :].rearrange("p (h d) -> p h d", d=DK), ACT.Copy).then_inc(sems["split_hi"], 1)
            act.wait_ge(sems["split_done"], 1)

            def xt(b):
                act.wait_ge(sems["xt_ps"], b + 1)
                nc.scalar.activation(xt_hi[:], m_ps[:, 0:S], ACT.Copy).then_inc(sems["xt_hi_done"], 1)

            def k_part(b, hp):
                act.wait_ge(sems["k_ps"], b * HP + hp + 1)
                nc.scalar.activation(k_hi[:, hp, 0:S], m_ps[:, 0:S], ACT.Identity,
                                     bias=bqk_s[:, 1, hp:hp + 1]).then_inc(sems["k_hi_done"], 1)

            def q_part(b, hp):
                act.wait_ge(sems["q_ps"], b * HP + hp + 1)
                nc.scalar.activation(q_hi[:, hp % 2, :], m_ps[:, 0:S], ACT.Identity,
                                     bias=bqk_s[:, 0, hp:hp + 1]).then_inc(sems["q_hi_done"], 1)

            def v_part(b):
                for j in range(4):
                    act.wait_ge(sems["v_tmp_done"], b * 4 + j + 1)
                    nc.scalar.activation(v_hl[:, j // 2, (j % 2) * 8:(j % 2) * 8 + 8, 0, :],
                                         v_tmp[:, j, :].rearrange("p (h d) -> p h d", d=DK), ACT.Copy).then_inc(sems["v_hi_done"], 1)

            def units(b, nxt):
                for i in range(H + 3):
                    hp = i // 2 + 1
                    if hp < HP:
                        (q_part if i % 2 else k_part)(b, hp)
                    if 2 <= i < H + 2:
                        u = i - 2
                        if u >= 2:
                            act.wait_ge(sems["o_ps_done"], b * H + u - 1)
                        act.wait_ge(sems["pta_ps"], b * H + u + 1)
                        nc.scalar.activation(pt_hi[:, u % 2, 0:512], pta[:], ACT.Copy).then_inc(sems["pta_hi"], 1)
                        act.wait_ge(sems["ptb_ps"], b * H + u + 1)
                        nc.scalar.activation(pt_hi[:, u % 2, 512:768], ptb[:, 0:256], ACT.Copy).then_inc(sems["ptb_hi"], 1)
                    if i < H:
                        if i >= PRING:
                            act.wait_ge(sems["ptb_ps"], b * H + i - PRING + 1)
                        act.wait_ge(sems["max_done"], b * H + i + 1)
                        for t in range(ST):
                            nc.scalar.activation(probs[:, i % PRING, t, :], s_ps[2 * (i % 2) + t][:, 0:T], ACT.Exp,
                                                 bias=nmax[:, i % PRING, t:t + 1],
                                                 accum_out=psums[:, i % PRING, t:t + 1]).then_inc(sems["exp_done"], 1)
                    if i == H and nxt:
                        xt(b + 1)
                    if i >= 3:
                        u = i - 3
                        act.wait_ge(sems["o_ps_done"], b * H + u + 1)
                        nc.scalar.activation(ot[:, u, :], o_ps[:, 0:S], ACT.Copy).then_inc(sems["ot_done"], 1)
                if nxt:
                    v_part(b + 1)
                    k_part(b + 1, 0)
                    q_part(b + 1, 0)

            xt(0)
            v_part(0)
            k_part(0, 0)
            q_part(0, 0)
            with act.Fori(0, B - 1) as b:
                units(b, True)
            units(B - 1, False)

            n_self = [0]

            def ln(k):
                act.wait_ge(sem_of(f"ln_var{k}"), 1)
                n_self[0] += 1
                nc.scalar.activation(nt_b[:], nt_a[:], ACT.Ln).then_inc(sems["act_self"], 1)
                act.wait_ge(sems["act_self"], n_self[0])
                nc.scalar.activation(rstd[:], nt_b[:], ACT.Exp, scale=-0.5).then_inc(sem_of(f"ln_rs{k}"), 1)

            def four_transposed(ps, done, used, g, before_it=0):
                act.wait_ge(sem_of(ps), g + 1)
                if g >= 2:
                    act.wait_ge(sem_of(used), before_it + g - 1)
                nc.scalar.activation(xt4[:, g % 2, :, :].rearrange("p a c -> p (a c)"), bank[g % 2], ACT.Copy).then_inc(sem_of(done), 1)

            def route(layer):
                nc.scalar.activation(rows[:, :, D:2 * D], x_res[:], ACT.Copy).then_inc(sem_of(f"rows_x{layer}"), 1)
                ln(2 * layer)
                for g in range(G4):
                    four_transposed(f"xt4_ps{layer}", f"xt4_done{layer}", f"logits_ps{layer}", g)
                act.wait_ge(sem_of(f"shifted{layer}"), 1)
                nc.scalar.activation(scr[:], scr[:], ACT.Exp).then_inc(sem_of(f"exps_done{layer}"), 1)

            def experts(layer):
                def xgt_of(j):
                    if isinstance(j.lap, int) and j.n >= SLOT_TILES:
                        return
                    act.wait_ge(sem_of(f"tx_ps{layer}"), j.n + 1)
                    wait(act, f"hb_ps{layer}", j.n - 1)
                    nc.scalar.activation(xgt[:, j.c % 2, :], bank[6][:, 0:P], ACT.Copy).then_inc(sem_of(f"xgt_done{layer}"), 1)

                def step(j):
                    last = isinstance(j.lap, int) and j.n >= SLOT_TILES
                    if not last and layer == 0:
                        act.wait_ge(sems["ha_ps0"], j.n + 1)
                        wait(act, "gm_done0", j.n - 1)
                        nc.scalar.activation(act_t[:, j.c % 2, :], bank[0], ACT.Silu).then_inc(sems["act_done0"], 1)
                    if not last and layer == 1:
                        act.wait_ge(sems["act_done1"], j.n + 1)
                        wait(act, "gt_ps1", j.n - 1)
                        nc.scalar.activation(gm[:, j.c % 2, :], act_t[:, j.c % 2, :], ACT.Gelu).then_inc(sems["gm_done1"], 1)
                    if not (isinstance(j.lap, int) and j.n == 0):
                        i = j.at(-1)
                        act.wait_ge(sem_of(f"gt_ps{layer}"), i.n + 1)
                        wait(act, f"y_ps{layer}", i.n - 1)
                        nc.scalar.activation(gt[:, i.c % 2, :], bank[2], ACT.Copy).then_inc(sem_of(f"gt_done{layer}"), 1)
                    xgt_of(j.at(1))
                xgt_of(Tile(0, 0))
                expert_steps(act, step)

            act.wait_ge(sems["x1_done"], ST * B + 1)
            route(0)
            act.dma_start(w1_1[:], io["w1_1"]).then_inc(sems["l1_loaded"], 16)
            act.dma_start(w2_1[:], io["w2_1"]).then_inc(sems["l1_loaded"], 16)
            act.dma_start(b1_bc[:].rearrange("p e f -> p (e f)"), io["b1_1"].broadcast_to([P, E * FF])).then_inc(sems["l1_loaded"], 16)
            act.dma_start(b2_bc[:].rearrange("p e f -> p (e f)"), io["b2_1"].broadcast_to([P, E * D])).then_inc(sems["l1_loaded"], 16)
            for n in range(G4):
                act.wait_ge(sems["mn_done"], n + 1)
                nc.scalar.activation(e1[:, n % 2], e1[:, n % 2], ACT.Exp).then_inc(sems["ex1_done"], 1)
                act.wait_ge(sems["v1_ps"], n + 1)
                nc.scalar.activation(v1t[:, 4 * n:4 * n + 4, :].rearrange("p a c -> p (a c)"), bank[6 + n % 2],
                                     ACT.Identity, bias=bv1[:]).then_inc(sems["v1_done"], 1)
            experts(0)
            ln(1)
            for g in range(G4 + 1):
                if g < G4:
                    four_transposed("xta_ps", "xta_done", "kq_ps", g, G4)
                if g >= 1:
                    n = G4 + g - 1
                    act.wait_ge(sems["mn_done"], n + 1)
                    nc.scalar.activation(e1[:, n % 2], e1[:, n % 2], ACT.Exp).then_inc(sems["ex1_done"], 1)
            for g in range(G4):
                four_transposed("ot1_ps", "ot1_done", "wo1_ps", g)
            act.wait_ge(sems["x3_done"], G4)
            route(1)
            experts(1)

        @block.vector
        def _(dve):
            n_self = [0]

            def link(ins):
                n_self[0] += 1
                ins.then_inc(sems["dve_self"], 1)
                dve.wait_ge(sems["dve_self"], n_self[0])

            dve.wait_ge(sems["x_loaded"], 16)
            for t in range(NT):
                last = nc.vector.bn_stats(stats[:, t, :], x_in[:, t, :])
            link(last)
            for t in range(NT):
                last = nc.vector.bn_aggr(meanvar[:, t, :], stats[:, t, :])
            link(last)
            nc.vector.tensor_scalar(nt_a[:], meanvar[:, :, 1], EPS, None, ALU.add).then_inc(sems["stats_done"], 1)
            dve.wait_ge(sems["split_hi"], 2)
            link(nc.vector.tensor_tensor(nt_b[:], rstd[:], rstd[:], ALU.mult))
            link(nc.vector.tensor_tensor(nt_b[:], nt_b[:], nt_a[:], ALU.mult))
            link(nc.vector.tensor_scalar(nt_b[:], nt_b[:], -0.5, 1.5, ALU.mult, ALU.add))
            link(nc.vector.tensor_tensor(rstd[:], rstd[:], nt_b[:], ALU.mult))

            def norm_tiles(b):
                for t in range(ST):
                    n = b * ST + t
                    last = nc.vector.tensor_scalar(xn[:, t, :], x_in[:, bass.ds(n, 1), :].rearrange("p a d -> p (a d)"),
                                                   meanvar[:, bass.ds(n, 1), 0], rstd[:, bass.ds(n, 1)],
                                                   ALU.subtract, ALU.mult)
                    last.then_inc(sems["xn_ready"], 1)

            norm_tiles(0)
            dve.wait_ge(sems["small_loaded"], 16 * 7)
            nc.vector.tensor_scalar(bqk_s[:, 0, :], bqk[:, 0, :], 0.125, None, ALU.mult)
            nc.vector.tensor_copy(bqk_s[:, 1, :], bqk[:, 1, :])
            for w in range(3):
                dve.wait_ge(sems["split_hi"], 3 + w)
                if w == 0:
                    nc.vector.scalar_tensor_tensor(out=w_lo[:, w, :], in0=wraw[:, w, :], scalar=0.125, in1=f32(w_hi[:, w, :]),
                                                   op0=ALU.mult, op1=ALU.subtract)
                else:
                    nc.vector.tensor_tensor(w_lo[:, w, :], wraw[:, w, :], f32(w_hi[:, w, :]), ALU.subtract)
            dve.wait_ge(sems["split_hi"], 6)
            nc.vector.tensor_tensor(k_lo[:, :, S:T], mk_raw, f32(k_hi[:, :, S:T]), ALU.subtract)
            dve.wait_ge(sems["split_hi"], 8)
            for half in range(2):
                last = nc.vector.tensor_tensor(v_hl[:, KT - 1, half * 8:half * 8 + 8, 1, :],
                                               v_tmp[:, half, :].rearrange("p (h d) -> p h d", d=DK),
                                               f32(v_hl[:, KT - 1, half * 8:half * 8 + 8, 0, :]), ALU.subtract)
            last.then_inc(sems["split_done"], 1)
            dve.wait_ge(sems["split_done"], 1)
            dve.wait_ge(sems["xb_made"], 1)
            nc.vector.memset(nt_b[:], 0.0).then_inc(sems["x1_done"], 1)

            def xt(b):
                dve.wait_ge(sems["xt_hi_done"], b + 1)
                nc.vector.tensor_tensor(xt_lo[:], m_ps[:, 0:S], f32(xt_hi[:]), ALU.subtract).then_inc(sems["xt_done"], 1)

            def k_part(b, hp):
                dve.wait_ge(sems["k_hi_done"], b * HP + hp + 1)
                nc.vector.scalar_tensor_tensor(out=k_lo[:, hp, 0:S], in0=m_ps[:, 0:S], scalar=bqk_s[:, 1, hp:hp + 1],
                                               in1=f32(k_hi[:, hp, 0:S]), op0=ALU.add,
                                               op1=ALU.subtract).then_inc(sems["k_done"], 1)

            def q_part(b, hp):
                dve.wait_ge(sems["q_hi_done"], b * HP + hp + 1)
                nc.vector.scalar_tensor_tensor(out=q_lo[:, hp % 2, :], in0=m_ps[:, 0:S], scalar=bqk_s[:, 0, hp:hp + 1],
                                               in1=f32(q_hi[:, hp % 2, :]), op0=ALU.add,
                                               op1=ALU.subtract).then_inc(sems["q_done"], 1)

            def v_part(b):
                def lo(j):
                    dve.wait_ge(sems["v_hi_done"], b * 4 + j + 1)
                    heads = slice((j % 2) * 8, (j % 2) * 8 + 8)
                    nc.vector.tensor_tensor(v_hl[:, j // 2, heads, 1, :], v_tmp[:, j, :].rearrange("p (h d) -> p h d", d=DK),
                                            f32(v_hl[:, j // 2, heads, 0, :]), ALU.subtract).then_inc(sems["v_done"], 1)
                for j in range(4):
                    dve.wait_ge(sems["v_ps"], b * 4 + j + 1)
                    nc.vector.tensor_tensor(v_tmp[:, j, :], s_ps[j], bv_bc[:, (j % 2) * 512:(j % 2) * 512 + 512],
                                            ALU.add).then_inc(sems["v_tmp_done"], 1)
                    if j >= 1:
                        lo(j - 1)
                lo(3)

            def add_residual(b, t):
                dve.wait_ge(sems["wo_ps"], b * ST + t + 1)
                xr = x_res[:, bass.ds(b * ST + t, 1), :].rearrange("p a d -> p (a d)")
                nc.vector.tensor_tensor(xr, (pta, ptb)[t][:, 0:D], xr, ALU.add).then_inc(sems["x1_done"], 1)

            def units(b, nxt):
                for i in range(H + 3):
                    if i < H:
                        dve.wait_ge(sems["scores_ps"], b * H + i + 1)
                        pair = 2 * (i % 2)
                        nc.vector.tensor_reduce(nmax[:, i % PRING, :], s_all[:, pair:pair + ST, 0:T],
                                                AX_X, ALU.max, negate=True).then_inc(sems["max_done"], 1)
                    hp = i // 2 + 1
                    if hp < HP:
                        (q_part if i % 2 else k_part)(b, hp)
                    if 1 <= i <= H:
                        u = i - 1
                        dve.wait_ge(sems["exp_done"], b * 2 * H + 2 * u + 2)
                        nc.vector.reciprocal(rsums[:, u % PRING, :], psums[:, u % PRING, :]).then_inc(sems["recip_done"], 1)
                        dve.wait_ge(sems["recip_done"], b * H + u + 1)
                        p = probs[:, u % PRING, 0, :]
                        nc.vector.tensor_scalar(p, p, rsums[:, u % PRING, 0:1], None, ALU.mult).then_inc(sems["probs0_done"], 1)
                    if 2 <= i < H + 2:
                        u = i - 2
                        dve.wait_ge(sems["pta_hi"], b * H + u + 1)
                        nc.vector.tensor_tensor(pt_lo[:, u % 2, 0:512], pta[:], f32(pt_hi[:, u % 2, 0:512]),
                                                ALU.subtract).then_inc(sems["pta_done"], 1)
                        dve.wait_ge(sems["ptb_hi"], b * H + u + 1)
                        nc.vector.tensor_tensor(pt_lo[:, u % 2, 512:768], ptb[:, 0:256], f32(pt_hi[:, u % 2, 512:768]),
                                                ALU.subtract).then_inc(sems["ptb_done"], 1)
                    if i == H and nxt:
                        xt(b + 1)
                    if i == 12 and nxt:
                        norm_tiles(b + 1)
                if nxt:
                    v_part(b + 1)
                    k_part(b + 1, 0)
                    add_residual(b, 0)
                    q_part(b + 1, 0)
                    add_residual(b, 1)
                else:
                    add_residual(b, 0)
                    add_residual(b, 1)

            xt(0)
            v_part(0)
            k_part(0, 0)
            q_part(0, 0)
            with dve.Fori(0, B - 1) as b:
                units(b, True)
            units(B - 1, False)

            def ln(k, dst):
                for t in range(NT):
                    last = nc.vector.bn_stats(stats[:, t, :], x_res[:, t, :])
                link(last)
                for t in range(NT):
                    last = nc.vector.bn_aggr(meanvar[:, t, :], stats[:, t, :])
                link(last)
                nc.vector.tensor_scalar(nt_a[:], meanvar[:, :, 1], EPS, None, ALU.add).then_inc(sem_of(f"ln_var{k}"), 1)
                dve.wait_ge(sem_of(f"ln_rs{k}"), 1)
                link(nc.vector.tensor_tensor(nt_b[:], rstd[:], rstd[:], ALU.mult))
                link(nc.vector.tensor_tensor(nt_b[:], nt_b[:], nt_a[:], ALU.mult))
                link(nc.vector.tensor_scalar(nt_b[:], nt_b[:], -0.5, 1.5, ALU.mult, ALU.add))
                link(nc.vector.tensor_tensor(rstd[:], rstd[:], nt_b[:], ALU.mult))
                for t in range(NT):
                    last = nc.vector.tensor_scalar(dst(t), x_res[:, t, :], meanvar[:, t, 0:1], rstd[:, t:t + 1],
                                                   ALU.subtract, ALU.mult)
                    if t % 4 == 3:
                        last.then_inc(sem_of(f"ln_out{k}"), 1)

            def inner(ap, n):
                return ap.rearrange("p (a b) -> p a b", b=1).broadcast_to([P, ap.shape[1], n])

            def outer(ap, n):
                return ap.rearrange("p (b a) -> p b a", b=1).broadcast_to([P, n, ap.shape[1]])

            def route(layer):
                ln(2 * layer, lambda t: rows[:, t, 0:D])
                link(nc.vector.memset(onehot[:, NT, :], 0.0))
                dve.wait_ge(sem_of(f"logits_ps{layer}"), G4)
                link(nc.vector.tensor_tensor(logits[:], bank[2][:, 0:NT * E].rearrange("p (t e) -> p t e", e=E),
                                             outer(rb_bc[:, layer, :], NT), ALU.add))
                link(nc.vector.tensor_reduce(col[0][:], logits[:], AX_X, ALU.max))
                nc.vector.tensor_tensor(scr[:], logits[:], inner(col[0][:], E), ALU.subtract).then_inc(sem_of(f"shifted{layer}"), 1)
                link(nc.vector.tensor_tensor(chosen[:], logits[:], inner(col[0][:], E), ALU.is_equal))
                link(nc.vector.tensor_tensor(chosen[:], chosen[:], outer(first[:], NT), ALU.mult))
                link(nc.vector.tensor_reduce(col[1][:], chosen[:], AX_X, ALU.max))
                link(nc.vector.tensor_tensor(chosen[:], chosen[:], inner(col[1][:], E), ALU.is_equal))
                nc.vector.tensor_copy(onehot[:, 0:NT, :], chosen[:]).then_inc(sem_of(f"onehot_done{layer}"), 1)
                dve.wait_ge(sem_of(f"exps_done{layer}"), 1)
                link(nc.vector.tensor_reduce(col[2][:], scr[:], AX_X, ALU.add))
                nc.vector.reciprocal(rows[:, :, ROW - 1], col[2][:]).then_inc(sem_of(f"gates_done{layer}"), 1)
                dve.wait_ge(sem_of(f"ranks_ps{layer}"), 1)
                link(nc.vector.tensor_scalar(counts_i[:], bank[3][:, NT * E:(NT + 1) * E], float(P - 1), None, ALU.add))
                link(nc.vector.tensor_scalar(counts_i[:], counts_i[:], 7, None, ALU.arith_shift_right))
                link(nc.vector.tensor_copy(tiles_f[:], counts_i[:]))
                link(nc.vector.tensor_tensor(sq[:], before[:], outer(tiles_f[:], E), ALU.mult))
                link(nc.vector.tensor_reduce(base[:], sq[:], AX_X, ALU.add))
                link(nc.vector.scalar_tensor_tensor(out=scr[:], in0=outer(base[:], NT), scalar=float(P),
                                                    in1=bank[3][:, 0:NT * E].rearrange("p (t e) -> p t e", e=E),
                                                    op0=ALU.mult, op1=ALU.add))
                link(nc.vector.tensor_tensor(scr[:], scr[:], chosen[:], ALU.mult))
                link(nc.vector.tensor_reduce(slot_f[:], scr[:], AX_X, ALU.add))
                nc.vector.tensor_copy(slot[layer][:], slot_f[:]).then_inc(sem_of(f"slot_done{layer}"), 1)
                link(nc.vector.tensor_tensor(counts[:], base[:], tiles_f[:], ALU.add))
                link(nc.vector.tensor_tensor(cmp_t[:], outer(counts[:], SLOT_TILES), inner(tile_no[:], E), ALU.is_le))
                link(nc.vector.tensor_reduce(texp_f[:], cmp_t[:], AX_X, ALU.add))
                nc.vector.tensor_scalar(texp[layer][:], texp_f[:], float(E - 1), None, ALU.min).then_inc(sem_of(f"texp_done{layer}"), 1)

            def experts(layer):
                dve.wait_ge(sem_of(f"texp_done{layer}"), 1)

                def expert_of(j):
                    return dve.value_load(texp[layer][0:1, bass.ds(j.n, 1)], min_val=0, max_val=E - 1)

                def step(j):
                    if not (isinstance(j.lap, int) and j.n >= SLOT_TILES):
                        r2 = j.c % 2
                        if layer == 0:
                            dve.wait_ge(sems["act_done0"], j.n + 1)
                            dve.wait_ge(sems["hb_ps0"], j.n + 1)
                            wait(dve, "gt_ps0", j.n - 1)
                            nc.vector.tensor_tensor(gm[:, r2, :], act_t[:, r2, :], bank[1], ALU.mult).then_inc(sems["gm_done0"], 1)
                        else:
                            e = expert_of(j)
                            dve.wait_ge(sems["hb_ps1"], j.n + 1)
                            wait(dve, "gm_done1", j.n - 1)
                            nc.vector.tensor_tensor(act_t[:, r2, :], bank[r2],
                                                    b1_bc[:, bass.ds(e, 1), :].rearrange("p a f -> p (a f)"),
                                                    ALU.add).then_inc(sems["act_done1"], 1)
                    if isinstance(j.lap, int) and j.n == 0:
                        return
                    i = j.at(-1)
                    if layer == 1:
                        e = expert_of(i)
                    dve.wait_ge(sem_of(f"y_ps{layer}"), i.n + 1)
                    wait(dve, f"y_stored{layer}_{i.c}", 16 * i.lap)
                    y = bank[3][:, 0:D]
                    if layer == 1:
                        nc.vector.tensor_tensor(yb[:, i.c % 2, :], y, b2_bc[:, bass.ds(e, 1), :].rearrange("p a f -> p (a f)"),
                                                ALU.add).then_inc(sems["yb_done1"], 1)
                        dve.wait_ge(sems["yb_done1"], i.n + 1)
                        y = yb[:, i.c % 2, :]
                    nc.vector.scalar_tensor_tensor(out=yo[:, i.c, :], in0=y, scalar=xg[:, i.c, ROW - 1:ROW],
                                                   in1=xg[:, i.c, D:2 * D], op0=ALU.mult,
                                                   op1=ALU.add).then_inc(sem_of(f"yo_done{layer}"), 1)
                expert_steps(dve, step)

            def elu1_a(n):
                dve.wait_ge(sems["kq_ps"], n + 1)
                wait(dve, "kq_done", n - 1)
                link(nc.vector.tensor_tensor(z1[:, n % 2], bank[4 + n % 2].rearrange("p (a c) -> p a c", a=4),
                                             outer(bk1_bc if n < G4 else bq1_bc, 4), ALU.add))
                nc.vector.tensor_scalar(e1[:, n % 2], z1[:, n % 2], 0.0, None, ALU.min).then_inc(sems["mn_done"], 1)

            def elu1_b(n):
                dve.wait_ge(sems["ex1_done"], n + 1)
                dst = (k1 if n < G4 else q1)[:, 4 * (n % G4):4 * (n % G4) + 4, :]
                nc.vector.scalar_tensor_tensor(out=dst, in0=z1[:, n % 2], scalar=0.0, in1=e1[:, n % 2],
                                               op0=ALU.max, op1=ALU.add).then_inc(sems["kq_done"], 1)

            dve.wait_ge(sems["r_loaded"], 16 * 12)
            dve.wait_ge(sems["consts_made"], 13)
            dve.wait_ge(sems["x1_done"], ST * B + 1)
            route(0)
            for n in range(G4 + 1):
                if n < G4:
                    elu1_a(n)
                if n >= 1:
                    elu1_b(n - 1)
            experts(0)
            dve.wait_ge(sems["x2_loaded"], 16)
            ln(1, lambda t: x_in[:, t, :])
            for n in range(G4, 2 * G4 + 1):
                if n < 2 * G4:
                    elu1_a(n)
                if n > G4:
                    elu1_b(n - 1)
            dve.wait_ge(sems["kq_done"], 2 * G4)
            link(nc.vector.tensor_tensor(rows[:, :, 0:D], k1[:], q1, ALU.mult))
            for g in range(2):
                dve.wait_ge(sems["s1_ps"], g + 1)
                nc.vector.tensor_tensor(s1[:, 4 * g:4 * g + 4, :], bank[2 + g].rearrange("p (a c) -> p a c", a=4),
                                        outer(block_mask[:], 4), ALU.mult).then_inc(sems["s1_done"], 1)
            link(nc.vector.tensor_reduce(den[:], rows[:, :, 0:D].rearrange("p t (h d) -> p t h d", d=D1), AX_X, ALU.add))
            link(nc.vector.tensor_scalar(den[:], den[:], 1e-6, None, ALU.add))
            link(nc.vector.reciprocal(den[:], den[:]))
            for g in range(G4 + 1):
                if g < G4:
                    dve.wait_ge(sems["o1_ps"], g + 1)
                    wait(dve, "ot1_ps", g - 1)
                    nc.vector.tensor_tensor(z1[:, g % 2].rearrange("p a (h d) -> p a h d", d=D1),
                                            bank[4 + g % 2].rearrange("p (a h d) -> p a h d", a=4, d=D1),
                                            den[:, 4 * g:4 * g + 4, :].rearrange("p a (h z) -> p a h z", z=1)
                                            .broadcast_to([P, 4, H1, D1]), ALU.mult).then_inc(sems["o1_done"], 1)
                if g >= 1:
                    dve.wait_ge(sems["xb1_done"], 1)
                    dve.wait_ge(sems["wo1_ps"], g)
                    xr = x_res[:, 4 * g - 4:4 * g, :]
                    nc.vector.tensor_tensor(xr, bank[6 + (g - 1) % 2].rearrange("p (a c) -> p a c", a=4), xr,
                                            ALU.add).then_inc(sems["x3_done"], 1)
            dve.wait_ge(sems["x3_done"], G4)
            route(1)
            experts(1)

        @block.tensor
        def _(pe):
            def xt(b):
                pe.wait_ge(sems["xn_ready"], b * ST + ST)
                if not (isinstance(b, int) and b == 0):
                    pe.wait_ge(sems["q_done"], b * HP)
                for t in range(ST):
                    last = nc.tensor.transpose(m_ps[:, t * P:(t + 1) * P], xn[:, t, :], ident[:])
                last.then_inc(sems["xt_ps"], 1)

            def three(out, a_hi, a_lo, b_hi, b_lo):
                nc.tensor.matmul(out, a_hi, b_hi, start=True, stop=False)
                nc.tensor.matmul(out, a_lo, b_hi, start=False, stop=False)
                return nc.tensor.matmul(out, a_hi, b_lo, start=False, stop=True)

            def v_part(b):
                pe.wait_ge(sems["ct_ready"], b + 1)
                for j in range(4):
                    tk = slice((j // 2) * P, (j // 2) * P + P)
                    c = slice((j % 2) * 512, (j % 2) * 512 + 512)
                    three(s_ps[j], ct_hi[:, tk], ct_lo[:, tk], w_hi[:, 2, c], w_lo[:, 2, c]).then_inc(sems["v_ps"], 1)

            def k_part(b, hp):
                if hp == 0:
                    pe.wait_ge(sems["xt_done"], b + 1)
                else:
                    pe.wait_ge(sems["q_done"], b * HP + hp)
                c = slice(hp * P, hp * P + P)
                three(m_ps[:, 0:S], w_hi[:, 1, c], w_lo[:, 1, c], ct_hi[:], ct_lo[:]).then_inc(sems["k_ps"], 1)

            def q_part(b, hp):
                pe.wait_ge(sems["k_done"], b * HP + hp + 1)
                c = slice(hp * P, hp * P + P)
                three(m_ps[:, 0:S], w_hi[:, 0, c], w_lo[:, 0, c], xt_hi[:], xt_lo[:]).then_inc(sems["q_ps"], 1)

            def scores(b, u):
                hp, rows = u // 2, slice(DK * (u % 2), DK * (u % 2) + DK)
                if u == 0:
                    pe.wait_ge(sems["v_tmp_done"], b * 4 + 4)
                if u % 2 == 0:
                    pe.wait_ge(sems["q_done"], b * HP + hp + 1)
                if u >= 2:
                    pe.wait_ge(sems["exp_done"], b * 2 * H + 2 * u - 2)
                for t in range(ST):
                    c = slice(t * P, t * P + P)
                    last = three(s_ps[2 * (u % 2) + t][:, 0:T], q_hi[rows, hp % 2, c], q_lo[rows, hp % 2, c],
                                 k_hi[rows, hp, :], k_lo[rows, hp, :])
                last.then_inc(sems["scores_ps"], 1)

            def transposes(b, u):
                pe.wait_ge(sems["probs0_done"], b * H + u + 1)
                pe.wait_ge(sems["probs1_done"], b * H + u + 1)
                if u == 0:
                    pe.wait_ge(sems["x1_done"], b * ST + 1)
                if u >= 1:
                    pe.wait_ge(sems["pta_done"], b * H + u)
                for k in range(2):
                    for t in range(ST):
                        last = nc.tensor.transpose(pta[:, (k * ST + t) * P:(k * ST + t + 1) * P],
                                                   probs[:, u % PRING, t, k * P:(k + 1) * P], ident[:])
                last.then_inc(sems["pta_ps"], 1)
                if u >= 1:
                    pe.wait_ge(sems["ptb_done"], b * H + u)
                for t in range(ST):
                    last = nc.tensor.transpose(ptb[:, t * P:(t + 1) * P], probs[:, u % PRING, t, 2 * P:3 * P], ident[:])
                last.then_inc(sems["ptb_ps"], 1)

            def weighted(b, u):
                if u == 0:
                    pe.wait_ge(sems["v_done"], b * 4 + 4)
                else:
                    pe.wait_ge(sems["ot_done"], b * H + u)
                pe.wait_ge(sems["ptb_done"], b * H + u + 1)
                for k in range(KT):
                    for part in (pt_hi, pt_lo):
                        last = nc.tensor.matmul(o_ps[:, 0:S], v_hl[:, k, u, :, :].rearrange("p a d -> p (a d)"),
                                                part[:, u % 2, k * S:(k + 1) * S],
                                                start=(k == 0 and part is pt_hi), stop=(k == KT - 1 and part is pt_lo))
                last.then_inc(sems["o_ps_done"], 1)

            def project_out(b, t):
                pe.wait_ge(sems["ot_done"], b * H + H)
                bank = (pta, ptb)[t]
                for h in range(H):
                    last = nc.tensor.matmul(bank[:, 0:D], ot[:, h, t * P:(t + 1) * P], wo0[:, h, :],
                                            start=(h == 0), stop=(h == H - 1))
                last.then_inc(sems["wo_ps"], 1)

            def units(b, nxt):
                for i in range(H + 3):
                    if i < H:
                        scores(b, i)
                    hp = i // 2 + 1
                    if hp < HP:
                        (q_part if i % 2 else k_part)(b, hp)
                    if 2 <= i < H + 2:
                        transposes(b, i - 2)
                    if i == H and nxt:
                        xt(b + 1)
                    if i >= 3:
                        weighted(b, i - 3)
                if nxt:
                    v_part(b + 1)
                    k_part(b + 1, 0)
                    project_out(b, 0)
                    q_part(b + 1, 0)
                    project_out(b, 1)
                else:
                    project_out(b, 0)
                    project_out(b, 1)

            pe.wait_ge(sems["ident_made"], 1)
            xt(0)
            pe.wait_ge(sems["split_done"], 1)
            v_part(0)
            k_part(0, 0)
            q_part(0, 0)
            with pe.Fori(0, B - 1) as b:
                units(b, True)
            units(B - 1, False)

            def grouped(ps, done, ready, src, use, free):
                for g in range(G4 + 1):
                    if g < G4:
                        pe.wait_ge(sem_of(ready), g + 1)
                        wait(pe, done, g - 1)
                        for i in range(4):
                            last = nc.tensor.transpose(bank[g % 2][:, i * P:(i + 1) * P], src(g, i), ident[:])
                        last.then_inc(sem_of(ps), 1)
                    if g >= 1:
                        pe.wait_ge(sem_of(done), g)
                        free(g - 1)
                        use(g - 1)

            def route(layer):
                def logits_of(g):
                    for i in range(4):
                        t = 4 * g + i
                        last = nc.tensor.matmul(bank[2][:, t * E:(t + 1) * E], xt4[:, g % 2, i, :], router[:, layer, :],
                                                start=True, stop=True)
                    last.then_inc(sem_of(f"logits_ps{layer}"), 1)
                grouped(f"xt4_ps{layer}", f"xt4_done{layer}", f"ln_out{2 * layer}", lambda g, i: rows[:, 4 * g + i, 0:D],
                        logits_of, lambda g: None)

            def ranks(layer):
                pe.wait_ge(sem_of(f"onehot_done{layer}"), 1)
                nc.tensor.matmul(bank[3][:, 0:(NT + 1) * E], upper[:], onehot[:].rearrange("p t e -> p (t e)"), start=True, stop=False)
                for t in range(NT):
                    last = nc.tensor.matmul(bank[3][:, (t + 1) * E:(NT + 1) * E].rearrange("p (t e) -> p t e", e=E), ones[:],
                                            onehot[:, t:t + 1, :].broadcast_to([P, NT - t, E]), start=False, stop=(t == NT - 1))
                last.then_inc(sem_of(f"ranks_ps{layer}"), 1)

            def experts(layer):
                w1, w2 = ((w1_0, w2_0), (w1_1, w2_1))[layer]
                pe.wait_ge(sem_of(f"texp_done{layer}"), 1)

                def expert_of(j):
                    return pe.value_load(texp[layer][0:1, bass.ds(j.n, 1)], min_val=0, max_val=E - 1)

                def transpose_in(j):
                    if isinstance(j.lap, int) and j.n >= SLOT_TILES:
                        return
                    pe.wait_ge(sem_of(f"xg_loaded{layer}_{j.c}"), 16 * j.lap + 16)
                    wait(pe, f"xgt_done{layer}", j.n)
                    nc.tensor.transpose(bank[6][:, 0:P], xg[:, j.c, 0:D], ident[:]).then_inc(sem_of(f"tx_ps{layer}"), 1)

                def up(e, j, half, to):
                    cols = w1[:, bass.ds(e, 1), half * FF:(half + 1) * FF].rearrange("p a f -> p (a f)")
                    return nc.tensor.matmul(to, xgt[:, j.c % 2, :], cols, start=True, stop=True)

                def step(j):
                    up_too = not (isinstance(j.lap, int) and j.n >= SLOT_TILES)
                    down_too = not (isinstance(j.lap, int) and j.n == 0)
                    i = j.at(-1) if down_too else None
                    if up_too:
                        e = expert_of(j)
                        pe.wait_ge(sem_of(f"xgt_done{layer}"), j.n + 1)
                        if layer == 0:
                            wait(pe, "act_done0", j.n)
                            up(e, j, 0, bank[0]).then_inc(sems["ha_ps0"], 1)
                        else:
                            wait(pe, "act_done1", j.n - 1)
                            up(e, j, 0, bank[j.c % 2]).then_inc(sems["hb_ps1"], 1)
                    if down_too:
                        pe.wait_ge(sem_of(f"gm_done{layer}"), i.n + 1)
                        wait(pe, f"gt_done{layer}", i.n)
                        for k in range(FK):
                            last = nc.tensor.transpose(bank[2][:, k * P:(k + 1) * P], gm[:, i.c % 2, k * P:(k + 1) * P], ident[:])
                        last.then_inc(sem_of(f"gt_ps{layer}"), 1)
                    if up_too and layer == 0:
                        wait(pe, "gm_done0", j.n)
                        up(e, j, 1, bank[1]).then_inc(sems["hb_ps0"], 1)
                    if up_too:
                        transpose_in(j.at(1))
                    if down_too:
                        ei = expert_of(i)
                        pe.wait_ge(sem_of(f"gt_done{layer}"), i.n + 1)
                        wait(pe, "yo_done0" if layer == 0 else "yb_done1", i.n)
                        for k in range(FK):
                            last = nc.tensor.matmul(bank[3][:, 0:D], gt[:, i.c % 2, k * P:(k + 1) * P],
                                                    w2[:, bass.ds(ei, 1), k, :].rearrange("p a d -> p (a d)"),
                                                    start=(k == 0), stop=(k == FK - 1))
                        last.then_inc(sem_of(f"y_ps{layer}"), 1)
                transpose_in(Tile(0, 0))
                expert_steps(pe, step)

            def project4(lhs, which, to, name):
                for i in range(4):
                    last = nc.tensor.matmul(to[:, i * D:(i + 1) * D], lhs(i), w_attn1[:, which, :], start=True, stop=True)
                last.then_inc(sem_of(name), 1)

            pe.wait_ge(sems["r_loaded"], 16 * 12)
            route(0)
            ctx_tiles = ctx_t[:].rearrange("p b (t c) -> p (b t) c", c=P)
            pe.wait_ge(sems["consts_made"], 13)
            for g in range(G4):
                wait(pe, "mn_done", g - 1)
                project4(lambda i: ctx_tiles[:, 4 * g + i, :], 1, bank[4 + g % 2], "kq_ps")
                wait(pe, "v1_done", g - 1)
                nc.tensor.matmul(bank[6 + g % 2], w_attn1[:, 2, :], ctx_tiles[:, 4 * g:4 * g + 4, :].rearrange("p a c -> p (a c)"),
                                 start=True, stop=True).then_inc(sems["v1_ps"], 1)
                if g == 1:
                    ranks(0)
            pe.wait_ge(sems["v1_done"], G4)
            pe.wait_ge(sems["w1_loaded"], 16)
            pe.wait_ge(sems["w2_loaded"], 16)
            experts(0)

            def project_q(g):
                for i in range(4):
                    last = nc.tensor.matmul(bank[4 + g % 2][:, i * D:(i + 1) * D], xt4[:, g % 2, i, :], w_attn1[:, 0, :],
                                            start=True, stop=True)
                last.then_inc(sems["kq_ps"], 1)
            grouped("xta_ps", "xta_done", "ln_out1", lambda g, i: x_in[:, 4 * g + i, :],
                    project_q, lambda g: wait(pe, "mn_done", G4 + g - 1))
            pe.wait_ge(sems["kq_done"], 2 * G4)
            for b in range(B):
                for t in range(ST):
                    last = nc.tensor.matmul(bank[2 + b // 4][:, (b % 4) * D:(b % 4 + 1) * D], k1[:, b * ST + t, :],
                                            q1[:, b * ST + t, :], start=(t == 0), stop=(t == ST - 1))
                if b % 4 == 3:
                    last.then_inc(sems["s1_ps"], 1)
            for g in range(G4 + 2):
                if g < G4:
                    if g % 2 == 0:
                        pe.wait_ge(sems["s1_done"], g // 2 + 1)
                    wait(pe, "o1_done", g - 1)
                    for i in range(4):
                        t = 4 * g + i
                        last = nc.tensor.matmul(bank[4 + g % 2][:, i * D:(i + 1) * D], v1t[:, t, :], s1[:, t // ST, :],
                                                start=True, stop=True)
                    last.then_inc(sems["o1_ps"], 1)
                if 1 <= g <= G4:
                    pe.wait_ge(sems["o1_done"], g)
                    wait(pe, "ot1_done", g - 2)
                    for i in range(4):
                        last = nc.tensor.transpose(bank[(g - 1) % 2][:, i * P:(i + 1) * P], z1[:, (g - 1) % 2, i, :], ident[:])
                    last.then_inc(sems["ot1_ps"], 1)
                if g >= 2:
                    n = g - 2
                    pe.wait_ge(sems["ot1_done"], n + 1)
                    wait(pe, "x3_done", n - 1)
                    project4(lambda i: xt4[:, n % 2, i, :], 3, bank[6 + n % 2], "wo1_ps")
            pe.wait_ge(sems["x3_done"], G4)
            route(1)
            ranks(1)
            pe.wait_ge(sems["l1_loaded"], 64)
            experts(1)


_P0, _P1 = "L0_xattn_", "L1_xattn_"


def _layout(i):
    import numpy as np
    return {
        "x": i["x"].reshape(B * S, D), "ctx": i["ctx_1024"].transpose(2, 0, 1),
        "wq0": i[_P0 + "wq_w"], "wk0": i[_P0 + "wk_w"], "wv0": i[_P0 + "wv_w"],
        "bq0": i[_P0 + "wq_b"].reshape(HP, P).T, "bk0": i[_P0 + "wk_b"].reshape(HP, P).T, "bv0": i[_P0 + "wv_b"][None],
        "mk0": i[_P0 + "mk"][0].T.reshape(HP, P, MEM).transpose(1, 0, 2), "mv0": i[_P0 + "mv"][0],
        "wo0": i[_P0 + "wo_w"].reshape(H, DK, D).transpose(1, 0, 2), "bo0": i[_P0 + "wo_b"][None],
        "wr0": i["L0_ffn_router_w"], "br0": i["L0_ffn_router_b"][None],
        "w1_0": i["L0_ffn_w1"].transpose(1, 0, 2), "w2_0": i["L0_ffn_w2"].reshape(E, FK, P, D).transpose(2, 0, 1, 3),
        "wq1": i[_P1 + "Wq"], "wk1": i[_P1 + "Wk"], "wv1": i[_P1 + "Wv"], "wo1": i[_P1 + "Wo"],
        "bq1": i[_P1 + "bq"][None], "bk1": i[_P1 + "bk"][None], "bv1": i[_P1 + "bv"][:, None], "bo1": i[_P1 + "bo"][None],
        "wr1": i["L1_ffn_Wr"], "br1": i["L1_ffn_br"][None],
        "w1_1": i["L1_ffn_W1"].transpose(1, 0, 2), "b1_1": i["L1_ffn_b1"].reshape(1, E * FF),
        "w2_1": i["L1_ffn_W2"].reshape(E, FK, P, D).transpose(2, 0, 1, 3), "b2_1": i["L1_ffn_b2"].reshape(1, E * D),
    }


def kernel(**inputs):
    import numpy as np
    import concourse.bacc as bacc
    from concourse.bass_utils import run_bass_kernel_spmd

    nc = bacc.Bacc("TRN2", target_bir_lowering=False, num_devices=1)
    arrays, io = {}, {}
    for name, a in _layout({k: np.asarray(v) for k, v in inputs.items()}).items():
        arrays["in_" + name] = np.ascontiguousarray(a)
        io[name] = nc.dram_tensor("in_" + name, a.shape, mybir.dt.from_np(a.dtype), kind="ExternalInput").ap()
    io["out"] = nc.dram_tensor("out", (B * S, D), F32, kind="ExternalOutput").ap()
    build(nc, io)
    r = run_bass_kernel_spmd(nc, [arrays], core_ids=[0])
    return r.results[0]["out"].reshape(B, S, D)
```

```python
from contextlib import ExitStack

import concourse.bass as bass
from concourse import mybir

F32 = mybir.dt.float32
F32R = mybir.dt.float32r
BF16 = mybir.dt.bfloat16
I32 = mybir.dt.int32
U32 = mybir.dt.uint32
ACT = mybir.ActivationFunctionType
ALU = mybir.AluOpType
AX_X = mybir.AxisListType.X

P = 128
D = 128
B, S = 8, 256
NT = B * S // P
ST = S // P
H, DK = 16, 64
HP = H // 2
HD = H * DK
MEM = 128
T = S + MEM
KT = T // P
E = 8
FF = 512
FK = FF // P
SLOT_TILES = (B * S + E * (P - 1)) // P
H1, D1 = 16, 8
EPS = 1e-5
ROW = 2 * D + 2
RING = 6
NO_TOKEN = 1 << 20
G4 = NT // 4
PRING = 4
WG = 4
WP = H // WG * ST
VALUES_STEP = (15, 0, 3, 5)
ROT = 7
SIDE = {0: ("values", 0, 1, 0), 1: ("out", 2, 0, -1), 2: ("out", 2, 1, -1), 3: ("values", 1, 0, 0), 4: ("out", 3, 0, -1), 5: ("values", 1, 1, 0),
        6: ("out", 3, 1, -1), 7: ("out", 0, 0, 0), 8: ("out", 0, 1, 0), 11: ("out", 1, 0, 0), 12: ("out", 1, 1, 0),
        13: ("tokens", 0, 0, 1), 15: ("values", 0, 0, 1)}


def f32(ap):
    return ap.bitcast(F32)


def build(nc, io):
    ctx = ExitStack()
    with ctx:
        def sb(name, shape, dt=F32):
            return ctx.enter_context(nc.sbuf_tensor(name, shape, dt))

        def sem(name):
            return ctx.enter_context(nc.semaphore(name))

        ident = sb("ident", [P, P])
        x_in = sb("x_in", [P, NT, D])
        x_res = sb("x_res", [P, NT, D])
        w1_0 = sb("w1_0", [P, E, 2 * FF])
        upper = sb("upper", [P, P], BF16)
        ones = sb("ones", [P, P], BF16)
        before = sb("before", [P, E, E])
        first = sb("first", [P, E])
        tile_no = sb("tile_no", [P, SLOT_TILES])
        block_mask = sb("block_mask", [P, D])
        first_i = sb("first_i", [P, E], I32)
        tile_no_i = sb("tile_no_i", [P, SLOT_TILES], I32)
        token_no = sb("token_no", [P, NT], I32)
        empty_row = sb("empty_row", [P, ROW])
        bias_row = sb("bias_row", [P, 2 + 3 + 2, D])
        bo0_bc = bias_row[:, 0, :]
        bq1_bc, bk1_bc, bo1_bc = (bias_row[:, i, :] for i in (1, 2, 3))
        router = sb("router", [P, 2, E])
        rb_bc = sb("rb_bc", [P, 2, E])
        bv1 = sb("bv1", [P, 1])
        w_attn1 = sb("w_attn1", [P, 4, D])
        stats = sb("stats", [P, NT, 6])
        meanvar = sb("meanvar", [P, NT, 2])
        rstd = sb("rstd", [P, NT])
        nt_a = sb("nt_a", [P, NT])
        nt_b = sb("nt_b", [P, NT])
        ctx_t = sb("ctx_t", [P, B, S])
        phase = ExitStack()

        def tmp(name, shape, dt=F32):
            return phase.enter_context(nc.sbuf_tensor(name, shape, dt))

        w_hi = tmp("w_hi", [P, 3, HD], F32R)
        w_lo = tmp("w_lo", [P, 3, HD], F32R)
        bqk = tmp("bqk", [P, 2, HP])
        bqk_s = tmp("bqk_s", [P, 2, HP])
        bv_bc = tmp("bv_bc", [P, HD])
        wo0 = tmp("wo0", [P, H, D])
        xn = tmp("xn", [P, ST, D])
        xt_hi = tmp("xt_hi", [P, S], F32R)
        xt_lo = tmp("xt_lo", [P, S], F32R)
        ct_hi = tmp("ct_hi", [P, S], F32R)
        ct_lo = tmp("ct_lo", [P, S], F32R)
        k_hi = tmp("k_hi", [P, HP, T], F32R)
        k_lo = tmp("k_lo", [P, HP, T], F32R)
        q_hi = tmp("q_hi", [P, 2, S], F32R)
        q_lo = tmp("q_lo", [P, 2, S], F32R)
        v_tmp = tmp("v_tmp", [P, 2, 512])
        v_hl = tmp("v_hl", [P, KT, H, 2, DK], F32R)
        probs = tmp("probs", [P, PRING, ST, T])
        nmax = tmp("nmax", [P, PRING, ST])
        psums = tmp("psums", [P, PRING, ST])
        rsums = tmp("rsums", [P, PRING, ST])
        pt_hi = tmp("pt_hi", [P, 2, KT * S], F32R)
        pt_lo = tmp("pt_lo", [P, 2, KT * S], F32R)
        ot = tmp("ot", [P, H, S])
        wraw = ot[:, 0:12, :].rearrange("p (w a) c -> p w (a c)", w=3)
        mk_raw = ot[:, 12:16, :].rearrange("p a (b c) -> p (a b) c", c=MEM)

        phase.close()
        phase = ctx
        w2_0 = tmp("w2_0", [P, E, FK, D])
        w1_1 = tmp("w1_1", [P, E, FF + FK])
        w2_1 = tmp("w2_1", [P, E, FK + 1, D])
        rows = tmp("rows", [P, NT, ROW])
        onehot = tmp("onehot", [P, NT + 1, E], BF16)
        logits = tmp("logits", [P, NT, E])
        chosen = tmp("chosen", [P, NT, E])
        scr = tmp("scr", [P, NT, E])
        col = [tmp(f"col{i}", [P, NT]) for i in range(3)]
        counts = tmp("counts", [P, E])
        counts_i = tmp("counts_i", [P, E], I32)
        tiles_f = tmp("tiles_f", [P, E])
        base = tmp("base", [P, E])
        sq = tmp("sq", [P, E, E])
        cmp_t = tmp("cmp_t", [P, SLOT_TILES, E])
        texp_f = tmp("texp_f", [P, SLOT_TILES])
        texp = [tmp(f"texp{i}", [P, SLOT_TILES], I32) for i in range(2)]
        slot_f = tmp("slot_f", [P, NT])
        slot = [tmp(f"slot{i}", [P, NT], I32) for i in range(2)]
        xt4 = tmp("xt4", [P, 2, 4, P])
        xg = tmp("xg", [P, RING, ROW])
        xgt = tmp("xgt", [P, 2, P])
        z_t = tmp("z_t", [P, 2, FK, P])
        h_t = tmp("h_t", [P, 2, FK, P])
        w_up = tmp("w_up", [P, 2, 2 * FF])
        w_dn = tmp("w_dn", [P, 2, FK + 1, D])
        yb = tmp("yb", [P, 2, D])
        yo = tmp("yo", [P, RING, D])
        k1 = tmp("k1", [P, NT, D])
        q1 = rows[:, :, D:2 * D]
        v1t = tmp("v1t", [P, NT, P])
        z1 = tmp("z1", [P, 2, 4, D])
        e1 = tmp("e1", [P, 2, 4, D])
        s1 = tmp("s1", [P, B, D])
        den = tmp("den", [P, NT, H1])

        s_all = ctx.enter_context(nc.psum_tensor("s_all", [P, 4, 512], F32))
        s_ps = [s_all[:, i, :] for i in range(4)]
        pta = ctx.enter_context(nc.psum_tensor("pta", [P, 512], F32))
        ptb = ctx.enter_context(nc.psum_tensor("ptb", [P, 512], F32))
        o_ps = ctx.enter_context(nc.psum_tensor("o_ps", [P, 512], F32))
        m_ps = ctx.enter_context(nc.psum_tensor("m_ps", [P, 512], F32))

        bank = [s_all[:, i, :] for i in range(4)] + [pta[:], ptb[:], o_ps[:], m_ps[:]]

        slots = [nc.dram_tensor(f"slots{i}", [SLOT_TILES * P, ROW], F32, kind="Internal").ap() for i in range(2)]
        x2_dram = nc.dram_tensor("x2_dram", [B * S, D], F32, kind="Internal").ap()

        sems = {}

        names = ("x_loaded ctx_loaded w_loaded small_loaded ident_made xb_made prepared "
                 "stats_done ln_done dve_self pool_self split_hi split_done "
                 "xn_ready ct_hi_done ct_ready xt_ps xt_hi_done xt_done v_ps v_tmp_done v_hi_done v_done "
                 "k_ps k_hi_done k_done q_ps q_hi_done q_done "
                 "scores_ps max_done exp_done recip_done probs_done pta_ps ptb_ps pta_hi ptb_hi pta_done ptb_done "
                 "o_ps_done ot_done wo_ps x1_done stored").split()
        for n in names:
            sems[n] = sem(n)

        for i in range(3):
            for n in "ln_var ln_rs ln_out".split():
                sems[f"{n}{i}"] = sem(f"{n}{i}")
        for i in range(2):
            for n in ("xt4_ps xt4_done logits_ps onehot_done shifted exps_done ranks_ps gates_done rows_x rows_id texp_done "
                      "slot_done scattered staged_up staged_dn tx_ps xgt_done a_ps h_done y_ps yo_done").split():
                sems[f"{n}{i}"] = sem(f"{n}{i}")
            for c in range(RING):
                for n in "xg_loaded y_stored".split():
                    sems[f"{n}{i}_{c}"] = sem(f"{n}{i}_{c}")
        for n in ("r_loaded w1_loaded w2_loaded l1_loaded empty_made prefilled consts_made act_self x2_loaded xb1_done "
                  "kq_ps mn_done ex1_done kq_done v1_ps v1_done s1_ps s1_done o1_ps o1_done ot1_ps ot1_done wo1_ps x3_done "
                  "xta_ps xta_done gate_ps silu_done biased yb_done").split():
            sems[n] = sem(n)
        sem_of = sems.__getitem__

        class Tile:

            def __init__(self, lap, c):
                self.lap, self.c = (lap + c // RING, c % RING)
                self.n = self.lap * RING + self.c

            def at(self, k):
                return Tile(self.lap, self.c + k)

        def wait(eng, name, value):
            if not isinstance(value, int) or value > 0:
                eng.wait_ge(sem_of(name), value)

        def expert_steps(eng, step):
            laps = SLOT_TILES // RING
            for c in range(RING):
                step(Tile(0, c))
            with eng.Fori(1, laps) as lap:
                for c in range(RING):
                    step(Tile(lap, c))
            for n in range(laps * RING, SLOT_TILES + 1):
                step(Tile(n // RING, n % RING))

        def side(b, i, first, last):
            kind, n, t, db = SIDE.get(i, SIDE.get(i - H, (None, 0, 0, 0)) if last and i >= H else (None, 0, 0, 0))
            if i >= H:
                return (kind, b, n, t) if kind == "out" and db == -1 else None
            if kind is None or (db == -1 and first) or (db == 1 and last):
                return None
            return kind, b + db, n, t

        def unit_at(b, i, first):
            return (b, i) if i >= 0 else None if first else (b - 1, i + H)

        def attention_steps(eng, step):
            for i in range(ROT):
                step(0, i, True, False)
            with eng.Fori(1, B) as b:
                for i in range(ROT, H):
                    step(b - 1, i, False, False)
                for i in range(ROT):
                    step(b, i, False, False)
            for i in range(ROT, H + 3):
                step(B - 1, i, False, True)
            step(B - 1, H + 4, False, True)
            step(B - 1, H + 6, False, True)

        def side_bank(i):
            return s_ps[2 * ((i - 1) % 2)] if i < H + 3 else s_ps[1 + i // 2 % 2 * 2]

        block = ctx.enter_context(nc.Block())

        @block.sync
        def _(sp):
            sp.dma_start(x_in[:], io["x"].rearrange("(t p) d -> p t d", p=P)).then_inc(sems["x_loaded"], 16)
            sp.dma_start(bo0_bc, io["bo0"].broadcast_to([P, D])).then_inc(sems["small_loaded"], 16)
            sp.dma_start(wraw[:, 0, :], io["wq0"]).then_inc(sems["w_loaded"], 16)
            sp.dma_start(wraw[:, 1, :], io["wk0"]).then_inc(sems["w_loaded"], 16)
            sp.dma_start(wraw[:, 2, :], io["wv0"]).then_inc(sems["w_loaded"], 16)
            sp.dma_start(mk_raw, io["mk0"]).then_inc(sems["w_loaded"], 16)
            sp.dma_start(wo0[0:DK], io["wo0"]).then_inc(sems["small_loaded"], 16)
            sp.dma_start(wo0[DK:P], io["wo0"]).then_inc(sems["small_loaded"], 16)
            for i, n in enumerate(("wr0", "wr1")):
                sp.dma_start(router[:, i, :], io[n]).then_inc(sems["r_loaded"], 16)
            for i, n in enumerate(("br0", "br1")):
                sp.dma_start(rb_bc[:, i, :], io[n].broadcast_to([P, E])).then_inc(sems["r_loaded"], 16)
            for i, n in enumerate(("bq1", "bk1", "bo1")):
                sp.dma_start(bias_row[:, 1 + i, :], io[n].broadcast_to([P, D])).then_inc(sems["r_loaded"], 16)
            for i, n in enumerate(("wq1", "wk1", "wv1", "wo1")):
                sp.dma_start(w_attn1[:, i, :], io[n]).then_inc(sems["r_loaded"], 16)
            sp.dma_start(bv1[:], io["bv1"]).then_inc(sems["r_loaded"], 16)
            sp.dma_start(w1_0[:], io["w1_0"]).then_inc(sems["w1_loaded"], 16)
            sp.wait_ge(sems["empty_made"], 2)
            for i in range(2):
                sp.dma_start(slots[i].rearrange("(j p) c -> p j c", p=P),
                             empty_row[:].rearrange("p (a c) -> p a c", a=1).broadcast_to([P, SLOT_TILES, ROW])
                             ).then_inc(sems["prefilled"], 16)
            sp.wait_ge(sems["x1_done"], WP * B)
            sp.dma_start(w2_0[:], io["w2_0"]).then_inc(sems["w2_loaded"], 16)

            def load_slots(layer):
                sp.wait_ge(sem_of(f"scattered{layer}"), 16 * NT)

                def step(j):
                    if isinstance(j.lap, int) and j.n >= SLOT_TILES:
                        return
                    wait(sp, f"y_stored{layer}_{j.c}", 16 * j.lap)
                    sp.dma_start(xg[:, j.c, :], slots[layer][bass.ds(j.n * P, P), :]).then_inc(
                        sem_of(f"xg_loaded{layer}_{j.c}"), 16)
                expert_steps(sp, step)
                for c in range(RING):
                    sp.wait_ge(sem_of(f"y_stored{layer}_{c}"), 16 * ((SLOT_TILES - c + RING - 1) // RING))

            load_slots(0)
            sp.dma_start(x_res[:], x2_dram.rearrange("(t p) d -> p t d", p=P)).then_inc(sems["x2_loaded"], 16)
            load_slots(1)

        @block.gpsimd
        def _(pool):
            nc.gpsimd.memset(ident[:], 0.0).then_inc(sems["pool_self"], 1)
            pool.wait_ge(sems["pool_self"], 1)
            nc.gpsimd.affine_select(out=ident[:], in_=ident[:], compare_op=ALU.not_equal, fill=1.0, base=0,
                                    pattern=[[-1, P]], channel_multiplier=1).then_inc(sems["ident_made"], 1)
            nc.gpsimd.memset(empty_row[:], 0.0).then_inc(sems["empty_made"], 1)
            pool.wait_ge(sems["empty_made"], 1)
            nc.gpsimd.memset(empty_row[:, 2 * D:2 * D + 1].bitcast(I32), NO_TOKEN).then_inc(sems["empty_made"], 1)
            pool.wait_ge(sems["small_loaded"], 16 * 7)
            pool.wait_ge(sems["x_loaded"], 16)
            pool.wait_ge(sems["ctx_loaded"], 16)

            def ctx_rest(b):
                nc.gpsimd.tensor_tensor(ct_lo[:], ctx_t[:, bass.ds(b, 1), :].rearrange("p a s -> p (a s)"), f32(ct_hi[:]),
                                        ALU.subtract).then_inc(sems["ct_ready"], 1)

            def step(b, i, first, last):
                if i == 14 and not last:
                    pool.wait_ge(sems["ct_hi_done"], b + 2)
                    ctx_rest(b + 1)
                if unit_at(b, i - 1, first) and i - 1 < H:
                    ub, u = unit_at(b, i - 1, first)
                    pool.wait_ge(sems["recip_done"], ub * H + u + 1)
                    for t in range(ST):
                        p = probs[:, u % PRING, t, :]
                        nc.gpsimd.tensor_tensor(p, p, rsums[:, u % PRING, t:t + 1].broadcast_to([P, T]),
                                                ALU.mult).then_inc(sems["probs_done"], 1)

            pool.wait_ge(sems["ct_hi_done"], 1)
            ctx_rest(0)
            nc.gpsimd.tensor_tensor(x_res[:], x_in[:], bo0_bc.rearrange("p (a d) -> p a d", a=1).broadcast_to([P, NT, D]),
                                    ALU.add).then_inc(sems["xb_made"], 1)
            nc.gpsimd.memset(upper[:], 1.0).then_inc(sems["consts_made"], 1)
            nc.gpsimd.memset(ones[:], 1.0).then_inc(sems["consts_made"], 1)
            nc.gpsimd.memset(before[:], 1.0).then_inc(sems["consts_made"], 1)
            nc.gpsimd.memset(block_mask[:], 1.0).then_inc(sems["consts_made"], 1)
            nc.gpsimd.iota(first_i[:], pattern=[[-1, E]], base=E, channel_multiplier=0).then_inc(sems["consts_made"], 1)
            nc.gpsimd.iota(tile_no_i[:], pattern=[[1, SLOT_TILES]], base=0, channel_multiplier=0).then_inc(sems["consts_made"], 1)
            nc.gpsimd.iota(token_no[:], pattern=[[P, NT]], base=0, channel_multiplier=1).then_inc(sems["consts_made"], 1)
            pool.wait_ge(sems["consts_made"], 7)
            nc.gpsimd.affine_select(out=upper[:], in_=upper[:], compare_op=ALU.is_gt, fill=0.0, base=0,
                                    pattern=[[1, P]], channel_multiplier=-1).then_inc(sems["consts_made"], 1)
            nc.gpsimd.affine_select(out=before[:], in_=before[:], compare_op=ALU.is_gt, fill=0.0, base=0,
                                    pattern=[[1, E], [-1, E]], channel_multiplier=0).then_inc(sems["consts_made"], 1)
            mask = block_mask[:].rearrange("p (h d) -> p h d", d=D1)
            nc.gpsimd.affine_select(out=mask, in_=mask, compare_op=ALU.is_ge, fill=0.0, base=0,
                                    pattern=[[-D1, H1], [0, D1]], channel_multiplier=1).then_inc(sems["consts_made"], 1)
            nc.gpsimd.tensor_copy(first[:], first_i[:]).then_inc(sems["consts_made"], 1)
            nc.gpsimd.tensor_copy(tile_no[:], tile_no_i[:]).then_inc(sems["consts_made"], 1)
            pool.wait_ge(sems["consts_made"], 12)
            nc.gpsimd.affine_select(out=mask, in_=mask, compare_op=ALU.is_ge, fill=0.0, base=D1 - 1,
                                    pattern=[[D1, H1], [0, D1]], channel_multiplier=-1).then_inc(sems["consts_made"], 1)
            attention_steps(pool, step)

            def route(layer):
                if layer == 0:
                    pool.wait_ge(sems["x1_done"], WP * B)
                else:
                    pool.wait_ge(sems["x3_done"], G4)
                nc.gpsimd.tensor_copy(rows[:, :, 2 * D].bitcast(I32), token_no[:]).then_inc(sem_of(f"rows_id{layer}"), 1)
                pool.wait_ge(sem_of(f"rows_id{layer}"), 1)
                pool.wait_ge(sem_of(f"rows_x{layer}"), 1)
                pool.wait_ge(sem_of(f"gates_done{layer}"), 1)
                pool.wait_ge(sem_of(f"slot_done{layer}"), 1)
                pool.wait_ge(sems["prefilled"], 32)
                for t in range(NT):
                    nc.gpsimd.indirect_dma_start(slots[layer], bass.IndirectOffsetOnAxis(ap=slot[layer][:, t:t + 1], axis=0),
                                                 rows[:, t, :], None).then_inc(sem_of(f"scattered{layer}"), 16)

                for n in range(SLOT_TILES):
                    c = n % RING
                    pool.wait_ge(sem_of(f"yo_done{layer}"), n + 1)
                    nc.gpsimd.indirect_dma_start((x2_dram, io["out"])[layer],
                                                 bass.IndirectOffsetOnAxis(ap=xg[:, c, 2 * D:2 * D + 1].bitcast(I32), axis=0),
                                                 yo[:, c, :], None, bounds_check=B * S - 1,
                                                 oob_is_err=False).then_inc(sem_of(f"y_stored{layer}_{c}"), 16)

            route(0)
            pool.wait_ge(sems["ln_out1"], G4)
            nc.gpsimd.tensor_tensor(x_res[:], x_res[:], bo1_bc.rearrange("p (a d) -> p a d", a=1).broadcast_to([P, NT, D]),
                                    ALU.add).then_inc(sems["xb1_done"], 1)
            route(1)

        @block.scalar
        def _(act):
            act.dma_start(ctx_t[:], io["ctx"]).then_inc(sems["ctx_loaded"], 16)
            act.dma_start(bqk[:, 0, :], io["bq0"]).then_inc(sems["small_loaded"], 16)
            act.dma_start(bqk[:, 1, :], io["bk0"]).then_inc(sems["small_loaded"], 16)
            act.dma_start(bv_bc[:], io["bv0"].broadcast_to([P, HD])).then_inc(sems["small_loaded"], 16)
            act.dma_start(v_tmp[:, 0:2, :], io["mv0"].rearrange("p (a c) -> p a c", a=2)).then_inc(sems["small_loaded"], 16)

            act.wait_ge(sems["stats_done"], 1)
            nc.scalar.activation(nt_b[:], nt_a[:], ACT.Ln).then_inc(sems["split_hi"], 1)
            act.wait_ge(sems["split_hi"], 1)
            nc.scalar.activation(rstd[:], nt_b[:], ACT.Exp, scale=-0.5).then_inc(sems["split_hi"], 1)
            act.wait_ge(sems["w_loaded"], 16 * 4)
            act.wait_ge(sems["small_loaded"], 16 * 7)
            for w in range(3):
                nc.scalar.activation(w_hi[:, w, :], wraw[:, w, :], ACT.Copy,
                                     scale=0.125 if w == 0 else 1.0).then_inc(sems["split_hi"], 1)
            nc.scalar.activation(k_hi[:, :, S:T], mk_raw, ACT.Copy).then_inc(sems["split_hi"], 1)
            for half in range(2):
                nc.scalar.activation(v_hl[:, KT - 1, half * 8:half * 8 + 8, 0, :],
                                     v_tmp[:, half, :].rearrange("p (h d) -> p h d", d=DK), ACT.Copy).then_inc(sems["split_hi"], 1)
            act.wait_ge(sems["split_done"], 1)

            def xt(b):
                act.wait_ge(sems["xt_ps"], b + 1)
                nc.scalar.activation(xt_hi[:], side_bank(13)[:, 0:S], ACT.Copy).then_inc(sems["xt_hi_done"], 1)

            def k_part(b, hp):
                act.wait_ge(sems["k_ps"], b * HP + hp + 1)
                nc.scalar.activation(k_hi[:, hp, 0:S], m_ps[:, 0:S], ACT.Identity,
                                     bias=bqk_s[:, 1, hp:hp + 1]).then_inc(sems["k_hi_done"], 1)

            def q_part(b, hp):
                act.wait_ge(sems["q_ps"], b * HP + hp + 1)
                nc.scalar.activation(q_hi[:, hp % 2, :], m_ps[:, 0:S], ACT.Identity,
                                     bias=bqk_s[:, 0, hp:hp + 1]).then_inc(sems["q_hi_done"], 1)

            def values(b, half, t):
                j = 2 * half + t
                act.wait_ge(sems["v_tmp_done"], b * 4 + j + 1)
                nc.scalar.activation(v_hl[:, t, half * 8:half * 8 + 8, 0, :],
                                     v_tmp[:, t, :].rearrange("p (h d) -> p h d", d=DK), ACT.Copy).then_inc(sems["v_hi_done"], 1)

            def step(b, i, first, last):
                if i < H - 2:
                    (q_part if i % 2 else k_part)(b, i // 2 + 1)
                elif i < H and not last:
                    (k_part if i % 2 else q_part)(b + 1, 0)
                if i == 13 and not last:
                    xt(b + 1)
                if unit_at(b, i - 2, first) and i - 2 < H:
                    ub, u = unit_at(b, i - 2, first)
                    wait(act, "o_ps_done", ub * H + u - 1)
                    act.wait_ge(sems["pta_ps"], ub * H + u + 1)
                    nc.scalar.activation(pt_hi[:, u % 2, 0:512], pta[:], ACT.Copy).then_inc(sems["pta_hi"], 1)
                    act.wait_ge(sems["ptb_ps"], ub * H + u + 1)
                    nc.scalar.activation(pt_hi[:, u % 2, 512:768], ptb[:, 0:256], ACT.Copy).then_inc(sems["ptb_hi"], 1)
                if i < H:
                    wait(act, "ptb_ps", b * H + i - PRING + 1)
                    act.wait_ge(sems["max_done"], b * H + i + 1)
                    for t in range(ST):
                        nc.scalar.activation(probs[:, i % PRING, t, :], s_ps[2 * (i % 2) + t][:, 0:T], ACT.Exp,
                                             bias=nmax[:, i % PRING, t:t + 1],
                                             accum_out=psums[:, i % PRING, t:t + 1]).then_inc(sems["exp_done"], 1)
                if unit_at(b, i - 3, first) and i - 3 < H:
                    ub, u = unit_at(b, i - 3, first)
                    act.wait_ge(sems["o_ps_done"], ub * H + u + 1)
                    nc.scalar.activation(ot[:, u, :], o_ps[:, 0:S], ACT.Copy).then_inc(sems["ot_done"], 1)
                task = side(b, i, first, last)
                if task and task[0] == "values":
                    values(*task[1:])
            xt(0)
            q_part(0, 0)
            k_part(0, 0)
            values(0, 0, 0)
            attention_steps(act, step)

            n_self = [0]

            def ln(k):
                act.wait_ge(sem_of(f"ln_var{k}"), 1)
                n_self[0] += 1
                nc.scalar.activation(nt_b[:], nt_a[:], ACT.Ln).then_inc(sems["act_self"], 1)
                act.wait_ge(sems["act_self"], n_self[0])
                nc.scalar.activation(rstd[:], nt_b[:], ACT.Exp, scale=-0.5).then_inc(sem_of(f"ln_rs{k}"), 1)

            def four_transposed(ps, done, used, g, before_it=0):
                act.wait_ge(sem_of(ps), g + 1)
                if g >= 2:
                    act.wait_ge(sem_of(used), before_it + g - 1)
                nc.scalar.activation(xt4[:, g % 2, :, :].rearrange("p a c -> p (a c)"), bank[g % 2], ACT.Copy).then_inc(sem_of(done), 1)

            def route(layer):
                nc.scalar.activation(rows[:, :, D:2 * D], x_res[:], ACT.Copy).then_inc(sem_of(f"rows_x{layer}"), 1)
                ln(2 * layer)
                for g in range(G4):
                    four_transposed(f"xt4_ps{layer}", f"xt4_done{layer}", f"logits_ps{layer}", g)
                act.wait_ge(sem_of(f"shifted{layer}"), 1)
                nc.scalar.activation(scr[:], scr[:], ACT.Exp).then_inc(sem_of(f"exps_done{layer}"), 1)

            def experts(layer):
                act.wait_ge(sem_of(f"texp_done{layer}"), 1)
                act.wait_ge(sems[("w2_loaded", "l1_loaded")[layer]], (16, 64)[layer])
                w2 = (w2_0, w2_1)[layer]

                def stage(j):
                    wait(act, ("y_ps0", "yb_done")[layer], j.n - 1)
                    e = act.value_load(texp[layer][0:1, bass.ds(j.n, 1)], min_val=0, max_val=E - 1)
                    nc.scalar.activation(w_dn[:, j.c % 2, 0:w2.shape[2], :], w2[:, bass.ds(e, 1), :, :].rearrange("p a k d -> p (a k) d"),
                                         ACT.Copy).then_inc(sem_of(f"staged_dn{layer}"), 1)

                def xgt_of(j):
                    if isinstance(j.lap, int) and j.n >= SLOT_TILES:
                        return
                    act.wait_ge(sem_of(f"tx_ps{layer}"), j.n + 1)
                    wait(act, "gate_ps" if layer == 0 else "a_ps1", j.n - 1)
                    nc.scalar.activation(xgt[:, j.c % 2, :], bank[6 + j.c % 2][:, 0:P], ACT.Copy).then_inc(sem_of(f"xgt_done{layer}"), 1)

                def step(j):
                    if isinstance(j.lap, int) and j.n >= SLOT_TILES:
                        return
                    r2 = j.c % 2
                    if layer == 0:
                        act.wait_ge(sems["a_ps0"], j.n + 1)
                        wait(act, "h_done0", j.n - 1)
                        nc.scalar.activation(z_t[:, r2].rearrange("p k c -> p (k c)"), bank[r2], ACT.Silu).then_inc(sems["silu_done"], 1)
                        xgt_of(j.at(1))
                        stage(j)
                    else:
                        stage(j)
                        xgt_of(j.at(1))
                        act.wait_ge(sems["biased"], j.n + 1)
                        wait(act, "y_ps1", j.n - 1)
                        nc.scalar.activation(h_t[:, r2].rearrange("p k c -> p (k c)"), z_t[:, r2].rearrange("p k c -> p (k c)"),
                                             ACT.Gelu).then_inc(sems["h_done1"], 1)
                xgt_of(Tile(0, 0))
                expert_steps(act, step)

            act.wait_ge(sems["x1_done"], WP * B)
            route(0)
            act.dma_start(w1_1[:, :, 0:FF], io["w1_1"]).then_inc(sems["l1_loaded"], 16)
            act.dma_start(w2_1[:, :, 0:FK, :], io["w2_1"]).then_inc(sems["l1_loaded"], 16)
            act.dma_start(w1_1[:, :, FF:FF + FK], io["b1_1"]).then_inc(sems["l1_loaded"], 16)
            act.dma_start(w2_1[:, :, FK, :], io["b2_1"].broadcast_to([P, E, D])).then_inc(sems["l1_loaded"], 16)
            for n in range(G4):
                act.wait_ge(sems["mn_done"], n + 1)
                nc.scalar.activation(e1[:, n % 2], e1[:, n % 2], ACT.Exp).then_inc(sems["ex1_done"], 1)
                act.wait_ge(sems["v1_ps"], n + 1)
                nc.scalar.activation(v1t[:, 4 * n:4 * n + 4, :].rearrange("p a c -> p (a c)"), bank[6 + n % 2],
                                     ACT.Identity, bias=bv1[:]).then_inc(sems["v1_done"], 1)
            experts(0)
            ln(1)
            for g in range(G4 + 1):
                if g < G4:
                    four_transposed("xta_ps", "xta_done", "kq_ps", g, G4)
                if g >= 1:
                    n = G4 + g - 1
                    act.wait_ge(sems["mn_done"], n + 1)
                    nc.scalar.activation(e1[:, n % 2], e1[:, n % 2], ACT.Exp).then_inc(sems["ex1_done"], 1)
            for g in range(G4):
                four_transposed("ot1_ps", "ot1_done", "wo1_ps", g)
            act.wait_ge(sems["x3_done"], G4)
            route(1)
            experts(1)

        @block.vector
        def _(dve):
            n_self = [0]

            def link(ins):
                n_self[0] += 1
                ins.then_inc(sems["dve_self"], 1)
                dve.wait_ge(sems["dve_self"], n_self[0])

            dve.wait_ge(sems["x_loaded"], 16)
            for t in range(NT):
                last = nc.vector.bn_stats(stats[:, t, :], x_in[:, t, :])
            link(last)
            for t in range(NT):
                last = nc.vector.bn_aggr(meanvar[:, t, :], stats[:, t, :])
            link(last)
            nc.vector.tensor_scalar(nt_a[:], meanvar[:, :, 1], EPS, None, ALU.add).then_inc(sems["stats_done"], 1)
            dve.wait_ge(sems["split_hi"], 2)
            link(nc.vector.tensor_tensor(nt_b[:], rstd[:], rstd[:], ALU.mult))
            link(nc.vector.tensor_tensor(nt_b[:], nt_b[:], nt_a[:], ALU.mult))
            link(nc.vector.tensor_scalar(nt_b[:], nt_b[:], -0.5, 1.5, ALU.mult, ALU.add))
            link(nc.vector.tensor_tensor(rstd[:], rstd[:], nt_b[:], ALU.mult))

            def norm_tiles(b):
                for t in range(ST):
                    n = b * ST + t
                    last = nc.vector.tensor_scalar(xn[:, t, :], x_in[:, bass.ds(n, 1), :].rearrange("p a d -> p (a d)"),
                                                   meanvar[:, bass.ds(n, 1), 0], rstd[:, bass.ds(n, 1)],
                                                   ALU.subtract, ALU.mult)
                    last.then_inc(sems["xn_ready"], 1)

            norm_tiles(0)

            def ctx_hi(b):
                nc.vector.tensor_copy(ct_hi[:], ctx_t[:, bass.ds(b, 1), :].rearrange("p a s -> p (a s)")
                                      ).then_inc(sems["ct_hi_done"], 1)
            dve.wait_ge(sems["ctx_loaded"], 16)
            ctx_hi(0)
            dve.wait_ge(sems["small_loaded"], 16 * 7)
            nc.vector.tensor_scalar(bqk_s[:, 0, :], bqk[:, 0, :], 0.125, None, ALU.mult)
            nc.vector.tensor_copy(bqk_s[:, 1, :], bqk[:, 1, :])
            for w in range(3):
                dve.wait_ge(sems["split_hi"], 3 + w)
                if w == 0:
                    nc.vector.scalar_tensor_tensor(out=w_lo[:, w, :], in0=wraw[:, w, :], scalar=0.125, in1=f32(w_hi[:, w, :]),
                                                   op0=ALU.mult, op1=ALU.subtract)
                else:
                    nc.vector.tensor_tensor(w_lo[:, w, :], wraw[:, w, :], f32(w_hi[:, w, :]), ALU.subtract)
            dve.wait_ge(sems["split_hi"], 6)
            nc.vector.tensor_tensor(k_lo[:, :, S:T], mk_raw, f32(k_hi[:, :, S:T]), ALU.subtract)
            dve.wait_ge(sems["split_hi"], 8)
            for half in range(2):
                last = nc.vector.tensor_tensor(v_hl[:, KT - 1, half * 8:half * 8 + 8, 1, :],
                                               v_tmp[:, half, :].rearrange("p (h d) -> p h d", d=DK),
                                               f32(v_hl[:, KT - 1, half * 8:half * 8 + 8, 0, :]), ALU.subtract)
            last.then_inc(sems["split_done"], 1)
            dve.wait_ge(sems["split_done"], 1)
            dve.wait_ge(sems["xb_made"], 1)

            def xt(b):
                dve.wait_ge(sems["xt_hi_done"], b + 1)
                nc.vector.tensor_tensor(xt_lo[:], side_bank(13)[:, 0:S], f32(xt_hi[:]), ALU.subtract).then_inc(sems["xt_done"], 1)

            def k_part(b, hp):
                dve.wait_ge(sems["k_hi_done"], b * HP + hp + 1)
                nc.vector.scalar_tensor_tensor(out=k_lo[:, hp, 0:S], in0=m_ps[:, 0:S], scalar=bqk_s[:, 1, hp:hp + 1],
                                               in1=f32(k_hi[:, hp, 0:S]), op0=ALU.add,
                                               op1=ALU.subtract).then_inc(sems["k_done"], 1)

            def q_part(b, hp):
                dve.wait_ge(sems["q_hi_done"], b * HP + hp + 1)
                nc.vector.scalar_tensor_tensor(out=q_lo[:, hp % 2, :], in0=m_ps[:, 0:S], scalar=bqk_s[:, 0, hp:hp + 1],
                                               in1=f32(q_hi[:, hp % 2, :]), op0=ALU.add,
                                               op1=ALU.subtract).then_inc(sems["q_done"], 1)

            def values(b, half, t):
                j = 2 * half + t
                wait(dve, "v_done", b * 4 + j - 1)
                dve.wait_ge(sems["v_ps"], b * 4 + j + 1)
                nc.vector.tensor_tensor(v_tmp[:, t, :], side_bank(VALUES_STEP[j]), bv_bc[:, half * 512:half * 512 + 512],
                                        ALU.add).then_inc(sems["v_tmp_done"], 1)

            def values_lo(b, half, t):
                j = 2 * half + t
                dve.wait_ge(sems["v_hi_done"], b * 4 + j + 1)
                heads = slice(half * 8, half * 8 + 8)
                nc.vector.tensor_tensor(v_hl[:, t, heads, 1, :], v_tmp[:, t, :].rearrange("p (h d) -> p h d", d=DK),
                                        f32(v_hl[:, t, heads, 0, :]), ALU.subtract).then_inc(sems["v_done"], 1)

            def add_out(b, g, t, bank):
                n = b * WP + g * ST + t
                dve.wait_ge(sems["wo_ps"], n + 1)
                if g > 0:
                    dve.wait_ge(sems["x1_done"], n - 1)
                xr = x_res[:, bass.ds(b * ST + t, 1), :].rearrange("p a d -> p (a d)")
                nc.vector.tensor_tensor(xr, bank[:, 0:D], xr, ALU.add).then_inc(sems["x1_done"], 1)

            def step(b, i, first, last):
                if i < H:
                    dve.wait_ge(sems["scores_ps"], b * H + i + 1)
                    pair = 2 * (i % 2)
                    nc.vector.tensor_reduce(nmax[:, i % PRING, :], s_all[:, pair:pair + ST, 0:T],
                                            AX_X, ALU.max, negate=True).then_inc(sems["max_done"], 1)
                if i < H - 2:
                    (q_part if i % 2 else k_part)(b, i // 2 + 1)
                elif i < H and not last:
                    (k_part if i % 2 else q_part)(b + 1, 0)
                if unit_at(b, i - 1, first) and i - 1 < H:
                    ub, u = unit_at(b, i - 1, first)
                    dve.wait_ge(sems["exp_done"], ub * 2 * H + 2 * u + 2)
                    nc.vector.reciprocal(rsums[:, u % PRING, :], psums[:, u % PRING, :]).then_inc(sems["recip_done"], 1)
                task = side(b, i, first, last)
                if task and task[0] == "values":
                    values(*task[1:])
                if task and task[0] == "tokens":
                    xt(task[1])
                if task and task[0] == "out":
                    add_out(*task[1:], side_bank(i))
                if unit_at(b, i - 2, first) and i - 2 < H:
                    ub, u = unit_at(b, i - 2, first)
                    dve.wait_ge(sems["pta_hi"], ub * H + u + 1)
                    nc.vector.tensor_tensor(pt_lo[:, u % 2, 0:512], pta[:], f32(pt_hi[:, u % 2, 0:512]),
                                            ALU.subtract).then_inc(sems["pta_done"], 1)
                    dve.wait_ge(sems["ptb_hi"], ub * H + u + 1)
                    nc.vector.tensor_tensor(pt_lo[:, u % 2, 512:768], ptb[:, 0:256], f32(pt_hi[:, u % 2, 512:768]),
                                            ALU.subtract).then_inc(sems["ptb_done"], 1)
                before = side(b, i - 1, first, last) if i > 0 else ("values", b, 0, 0)
                if before and before[0] == "values":
                    values_lo(*before[1:])
                if i == 13 and not last:
                    dve.wait_ge(sems["k_ps"], b * HP + HP)
                    ctx_hi(b + 1)
                if i == 11 and not last:
                    norm_tiles(b + 1)

            xt(0)
            q_part(0, 0)
            k_part(0, 0)
            values(0, 0, 0)
            attention_steps(dve, step)

            def ln(k, dst):
                for t in range(NT):
                    last = nc.vector.bn_stats(stats[:, t, :], x_res[:, t, :])
                link(last)
                for t in range(NT):
                    last = nc.vector.bn_aggr(meanvar[:, t, :], stats[:, t, :])
                link(last)
                nc.vector.tensor_scalar(nt_a[:], meanvar[:, :, 1], EPS, None, ALU.add).then_inc(sem_of(f"ln_var{k}"), 1)
                dve.wait_ge(sem_of(f"ln_rs{k}"), 1)
                link(nc.vector.tensor_tensor(nt_b[:], rstd[:], rstd[:], ALU.mult))
                link(nc.vector.tensor_tensor(nt_b[:], nt_b[:], nt_a[:], ALU.mult))
                link(nc.vector.tensor_scalar(nt_b[:], nt_b[:], -0.5, 1.5, ALU.mult, ALU.add))
                link(nc.vector.tensor_tensor(rstd[:], rstd[:], nt_b[:], ALU.mult))
                for t in range(NT):
                    last = nc.vector.tensor_scalar(dst(t), x_res[:, t, :], meanvar[:, t, 0:1], rstd[:, t:t + 1],
                                                   ALU.subtract, ALU.mult)
                    if t % 4 == 3:
                        last.then_inc(sem_of(f"ln_out{k}"), 1)

            def inner(ap, n):
                return ap.rearrange("p (a b) -> p a b", b=1).broadcast_to([P, ap.shape[1], n])

            def outer(ap, n):
                return ap.rearrange("p (b a) -> p b a", b=1).broadcast_to([P, n, ap.shape[1]])

            def route(layer):
                ln(2 * layer, lambda t: rows[:, t, 0:D])
                link(nc.vector.memset(onehot[:, NT, :], 0.0))
                dve.wait_ge(sem_of(f"logits_ps{layer}"), G4)
                link(nc.vector.tensor_tensor(logits[:], bank[2][:, 0:NT * E].rearrange("p (t e) -> p t e", e=E),
                                             outer(rb_bc[:, layer, :], NT), ALU.add))
                link(nc.vector.tensor_reduce(col[0][:], logits[:], AX_X, ALU.max))
                nc.vector.tensor_tensor(scr[:], logits[:], inner(col[0][:], E), ALU.subtract).then_inc(sem_of(f"shifted{layer}"), 1)
                link(nc.vector.tensor_tensor(chosen[:], logits[:], inner(col[0][:], E), ALU.is_equal))
                link(nc.vector.tensor_tensor(chosen[:], chosen[:], outer(first[:], NT), ALU.mult))
                link(nc.vector.tensor_reduce(col[1][:], chosen[:], AX_X, ALU.max))
                link(nc.vector.tensor_tensor(chosen[:], chosen[:], inner(col[1][:], E), ALU.is_equal))
                nc.vector.tensor_copy(onehot[:, 0:NT, :], chosen[:]).then_inc(sem_of(f"onehot_done{layer}"), 1)
                dve.wait_ge(sem_of(f"exps_done{layer}"), 1)
                link(nc.vector.tensor_reduce(col[2][:], scr[:], AX_X, ALU.add))
                nc.vector.reciprocal(rows[:, :, ROW - 1], col[2][:]).then_inc(sem_of(f"gates_done{layer}"), 1)
                dve.wait_ge(sem_of(f"ranks_ps{layer}"), 1)
                link(nc.vector.tensor_scalar(counts_i[:], bank[3][:, NT * E:(NT + 1) * E], float(P - 1), None, ALU.add))
                link(nc.vector.tensor_scalar(counts_i[:], counts_i[:], 7, None, ALU.arith_shift_right))
                link(nc.vector.tensor_copy(tiles_f[:], counts_i[:]))
                link(nc.vector.tensor_tensor(sq[:], before[:], outer(tiles_f[:], E), ALU.mult))
                link(nc.vector.tensor_reduce(base[:], sq[:], AX_X, ALU.add))
                link(nc.vector.scalar_tensor_tensor(out=scr[:], in0=outer(base[:], NT), scalar=float(P),
                                                    in1=bank[3][:, 0:NT * E].rearrange("p (t e) -> p t e", e=E),
                                                    op0=ALU.mult, op1=ALU.add))
                link(nc.vector.tensor_tensor(scr[:], scr[:], chosen[:], ALU.mult))
                link(nc.vector.tensor_reduce(slot_f[:], scr[:], AX_X, ALU.add))
                nc.vector.tensor_copy(slot[layer][:], slot_f[:]).then_inc(sem_of(f"slot_done{layer}"), 1)
                link(nc.vector.tensor_tensor(counts[:], base[:], tiles_f[:], ALU.add))
                link(nc.vector.tensor_tensor(cmp_t[:], outer(counts[:], SLOT_TILES), inner(tile_no[:], E), ALU.is_le))
                link(nc.vector.tensor_reduce(texp_f[:], cmp_t[:], AX_X, ALU.add))
                nc.vector.tensor_scalar(texp[layer][:], texp_f[:], float(E - 1), None, ALU.min).then_inc(sem_of(f"texp_done{layer}"), 1)

            def experts(layer):
                dve.wait_ge(sem_of(f"texp_done{layer}"), 1)

                def expert_of(j):
                    return dve.value_load(texp[layer][0:1, bass.ds(j.n, 1)], min_val=0, max_val=E - 1)

                w1 = (w1_0, w1_1)[layer]

                def stage(j):
                    if isinstance(j.lap, int) and j.n >= SLOT_TILES:
                        return
                    wait(dve, "gate_ps" if layer == 0 else "biased", j.n - 1)
                    nc.vector.tensor_copy(w_up[:, j.c % 2, 0:w1.shape[2]], w1[:, bass.ds(expert_of(j), 1), :].rearrange("p a f -> p (a f)")
                                          ).then_inc(sem_of(f"staged_up{layer}"), 1)

                def step(j):
                    stage(j.at(1))
                    if not (isinstance(j.lap, int) and j.n >= SLOT_TILES):
                        r2 = j.c % 2
                        if layer == 0:
                            dve.wait_ge(sems["silu_done"], j.n + 1)
                            dve.wait_ge(sems["gate_ps"], j.n + 1)
                            wait(dve, "y_ps0", j.n - 1)
                            nc.vector.tensor_tensor(h_t[:, r2].rearrange("p k c -> p (k c)"),
                                                    z_t[:, r2].rearrange("p k c -> p (k c)"), bank[4 + r2],
                                                    ALU.mult).then_inc(sems["h_done0"], 1)
                        else:
                            dve.wait_ge(sems["a_ps1"], j.n + 1)
                            dve.wait_ge(sems["staged_up1"], j.n + 1)
                            wait(dve, "h_done1", j.n - 1)
                            nc.vector.tensor_tensor(z_t[:, r2], bank[r2].rearrange("p (k c) -> p k c", k=FK), inner(w_up[:, r2, FF:FF + FK], P),
                                                    ALU.add).then_inc(sems["biased"], 1)
                    if isinstance(j.lap, int) and j.n == 0:
                        return
                    i = j.at(-1)
                    dve.wait_ge(sem_of(f"y_ps{layer}"), i.n + 1)
                    wait(dve, f"y_stored{layer}_{i.c}", 16 * i.lap)
                    y = bank[2 + i.c % 2][:, 0:D]
                    if layer == 1:
                        nc.vector.tensor_tensor(yb[:, i.c % 2, :], y, w_dn[:, i.c % 2, FK, :],
                                                ALU.add).then_inc(sems["yb_done"], 1)
                        dve.wait_ge(sems["yb_done"], i.n + 1)
                        y = yb[:, i.c % 2, :]
                    nc.vector.scalar_tensor_tensor(out=yo[:, i.c, :], in0=y, scalar=xg[:, i.c, ROW - 1:ROW],
                                                   in1=xg[:, i.c, D:2 * D], op0=ALU.mult,
                                                   op1=ALU.add).then_inc(sem_of(f"yo_done{layer}"), 1)
                dve.wait_ge(sems["w1_loaded" if layer == 0 else "l1_loaded"], 16 if layer == 0 else 64)
                stage(Tile(0, 0))
                expert_steps(dve, step)

            def elu1_a(n):
                dve.wait_ge(sems["kq_ps"], n + 1)
                wait(dve, "kq_done", n - 1)
                link(nc.vector.tensor_tensor(z1[:, n % 2], bank[4 + n % 2].rearrange("p (a c) -> p a c", a=4),
                                             outer(bk1_bc if n < G4 else bq1_bc, 4), ALU.add))
                nc.vector.tensor_scalar(e1[:, n % 2], z1[:, n % 2], 0.0, None, ALU.min).then_inc(sems["mn_done"], 1)

            def elu1_b(n):
                dve.wait_ge(sems["ex1_done"], n + 1)
                dst = (k1 if n < G4 else q1)[:, 4 * (n % G4):4 * (n % G4) + 4, :]
                nc.vector.scalar_tensor_tensor(out=dst, in0=z1[:, n % 2], scalar=0.0, in1=e1[:, n % 2],
                                               op0=ALU.max, op1=ALU.add).then_inc(sems["kq_done"], 1)

            dve.wait_ge(sems["r_loaded"], 16 * 12)
            dve.wait_ge(sems["consts_made"], 13)
            dve.wait_ge(sems["x1_done"], WP * B)
            route(0)
            for n in range(G4 + 1):
                if n < G4:
                    elu1_a(n)
                if n >= 1:
                    elu1_b(n - 1)
            experts(0)
            dve.wait_ge(sems["x2_loaded"], 16)
            ln(1, lambda t: x_in[:, t, :])
            for n in range(G4, 2 * G4 + 1):
                if n < 2 * G4:
                    elu1_a(n)
                if n > G4:
                    elu1_b(n - 1)
            dve.wait_ge(sems["kq_done"], 2 * G4)
            link(nc.vector.tensor_tensor(rows[:, :, 0:D], k1[:], q1, ALU.mult))
            for g in range(2):
                dve.wait_ge(sems["s1_ps"], g + 1)
                nc.vector.tensor_tensor(s1[:, 4 * g:4 * g + 4, :], bank[2 + g].rearrange("p (a c) -> p a c", a=4),
                                        outer(block_mask[:], 4), ALU.mult).then_inc(sems["s1_done"], 1)
            link(nc.vector.tensor_reduce(den[:], rows[:, :, 0:D].rearrange("p t (h d) -> p t h d", d=D1), AX_X, ALU.add))
            link(nc.vector.tensor_scalar(den[:], den[:], 1e-6, None, ALU.add))
            link(nc.vector.reciprocal(den[:], den[:]))
            for g in range(G4 + 1):
                if g < G4:
                    dve.wait_ge(sems["o1_ps"], g + 1)
                    wait(dve, "ot1_ps", g - 1)
                    nc.vector.tensor_tensor(z1[:, g % 2].rearrange("p a (h d) -> p a h d", d=D1),
                                            bank[4 + g % 2].rearrange("p (a h d) -> p a h d", a=4, d=D1),
                                            den[:, 4 * g:4 * g + 4, :].rearrange("p a (h z) -> p a h z", z=1)
                                            .broadcast_to([P, 4, H1, D1]), ALU.mult).then_inc(sems["o1_done"], 1)
                if g >= 1:
                    dve.wait_ge(sems["xb1_done"], 1)
                    dve.wait_ge(sems["wo1_ps"], g)
                    xr = x_res[:, 4 * g - 4:4 * g, :]
                    nc.vector.tensor_tensor(xr, bank[6 + (g - 1) % 2].rearrange("p (a c) -> p a c", a=4), xr,
                                            ALU.add).then_inc(sems["x3_done"], 1)
            dve.wait_ge(sems["x3_done"], G4)
            route(1)
            experts(1)

        @block.tensor
        def _(pe):
            def xt(b):
                pe.wait_ge(sems["xn_ready"], b * ST + ST)
                for t in range(ST):
                    last = nc.tensor.transpose(side_bank(13)[:, t * P:(t + 1) * P], xn[:, t, :], ident[:])
                last.then_inc(sems["xt_ps"], 1)

            def three(out, a_hi, a_lo, b_hi, b_lo):
                nc.tensor.matmul(out, a_hi, b_hi, start=True, stop=False)
                nc.tensor.matmul(out, a_lo, b_hi, start=False, stop=False)
                return nc.tensor.matmul(out, a_hi, b_lo, start=False, stop=True)

            def values(b, half, t):
                j = 2 * half + t
                tk = slice(t * P, t * P + P)
                c = slice(half * 512, half * 512 + 512)
                three(side_bank(VALUES_STEP[j]), ct_hi[:, tk], ct_lo[:, tk], w_hi[:, 2, c], w_lo[:, 2, c]).then_inc(sems["v_ps"], 1)

            def k_part(b, hp):
                if hp == 0:
                    pe.wait_ge(sems["ct_ready"], b + 1)
                    pe.wait_ge(sems["q_done"], b * HP + 1)
                elif hp == 1:
                    pe.wait_ge(sems["k_done"], b * HP + 1)
                else:
                    pe.wait_ge(sems["q_done"], b * HP + hp)
                c = slice(hp * P, hp * P + P)
                three(m_ps[:, 0:S], w_hi[:, 1, c], w_lo[:, 1, c], ct_hi[:], ct_lo[:]).then_inc(sems["k_ps"], 1)

            def q_part(b, hp):
                if hp == 0:
                    pe.wait_ge(sems["xt_done"], b + 1)
                    wait(pe, "q_done", b * HP)
                else:
                    pe.wait_ge(sems["k_done"], b * HP + hp + 1)
                c = slice(hp * P, hp * P + P)
                three(m_ps[:, 0:S], w_hi[:, 0, c], w_lo[:, 0, c], xt_hi[:], xt_lo[:]).then_inc(sems["q_ps"], 1)

            def scores(b, u, first, end):
                hp, rows = u // 2, slice(DK * (u % 2), DK * (u % 2) + DK)
                task = side(b, u - 1, first, end) if u > 0 else ("values", b, 0, 0)
                if task:
                    kind, tb, n, t = task
                    if kind == "values":
                        pe.wait_ge(sems["v_tmp_done"], tb * 4 + 2 * n + t + 1)
                    elif kind == "tokens":
                        pe.wait_ge(sems["xt_done"], tb + 1)
                    else:
                        pe.wait_ge(sems["x1_done"], tb * WP + n * ST + t + 1)
                if u % 2 == 0:
                    pe.wait_ge(sems["k_done" if u == 0 else "q_done"], b * HP + hp + 1)
                wait(pe, "exp_done", b * 2 * H + 2 * u - 2)
                for t in range(ST):
                    c = slice(t * P, t * P + P)
                    last = three(s_ps[2 * (u % 2) + t][:, 0:T], q_hi[rows, hp % 2, c], q_lo[rows, hp % 2, c],
                                 k_hi[rows, hp, :], k_lo[rows, hp, :])
                last.then_inc(sems["scores_ps"], 1)

            def transposes(b, u):
                pe.wait_ge(sems["probs_done"], b * ST * H + ST * u + ST)
                wait(pe, "pta_done", b * H + u)
                for k in range(2):
                    for t in range(ST):
                        last = nc.tensor.transpose(pta[:, (k * ST + t) * P:(k * ST + t + 1) * P],
                                                   probs[:, u % PRING, t, k * P:(k + 1) * P], ident[:])
                last.then_inc(sems["pta_ps"], 1)
                wait(pe, "ptb_done", b * H + u)
                for t in range(ST):
                    last = nc.tensor.transpose(ptb[:, t * P:(t + 1) * P], probs[:, u % PRING, t, 2 * P:3 * P], ident[:])
                last.then_inc(sems["ptb_ps"], 1)

            def weighted(b, u):
                if u % 8 == 0:
                    pe.wait_ge(sems["v_done"], b * 4 + u // 8 * ST + ST)
                wait(pe, "ot_done", b * H + u)
                pe.wait_ge(sems["ptb_done"], b * H + u + 1)
                for k in range(KT):
                    for part in (pt_hi, pt_lo):
                        last = nc.tensor.matmul(o_ps[:, 0:S], v_hl[:, k, u, :, :].rearrange("p a d -> p (a d)"),
                                                part[:, u % 2, k * S:(k + 1) * S],
                                                start=(k == 0 and part is pt_hi), stop=(k == KT - 1 and part is pt_lo))
                last.then_inc(sems["o_ps_done"], 1)

            def project_out(b, g, t, bank):
                pe.wait_ge(sems["ot_done"], b * H + g * WG + WG)
                for h in range(g * WG, g * WG + WG):
                    last = nc.tensor.matmul(bank[:, 0:D], ot[:, h, t * P:(t + 1) * P], wo0[:, h, :],
                                            start=(h == g * WG), stop=(h == g * WG + WG - 1))
                last.then_inc(sems["wo_ps"], 1)

            def step(b, i, first, last):
                if i < H:
                    scores(b, i, first, last)
                if i < H - 2:
                    (q_part if i % 2 else k_part)(b, i // 2 + 1)
                elif i < H and not last:
                    (k_part if i % 2 else q_part)(b + 1, 0)
                task = side(b, i, first, last)
                if task:
                    wait(pe, "exp_done", b * 2 * H + 2 * min(i, H) - (1 if i < H + 1 else 0))
                    if task[0] == "values":
                        values(*task[1:])
                    elif task[0] == "tokens":
                        xt(task[1])
                    else:
                        project_out(*task[1:], side_bank(i))
                if unit_at(b, i - 2, first) and i - 2 < H:
                    transposes(*unit_at(b, i - 2, first))
                if unit_at(b, i - 3, first) and i - 3 < H:
                    weighted(*unit_at(b, i - 3, first))
            pe.wait_ge(sems["ident_made"], 1)
            xt(0)
            pe.wait_ge(sems["split_done"], 1)
            q_part(0, 0)
            k_part(0, 0)
            values(0, 0, 0)
            attention_steps(pe, step)

            def grouped(ps, done, ready, src, use, free):
                for g in range(G4 + 1):
                    if g < G4:
                        pe.wait_ge(sem_of(ready), g + 1)
                        wait(pe, done, g - 1)
                        for i in range(4):
                            last = nc.tensor.transpose(bank[g % 2][:, i * P:(i + 1) * P], src(g, i), ident[:])
                        last.then_inc(sem_of(ps), 1)
                    if g >= 1:
                        pe.wait_ge(sem_of(done), g)
                        free(g - 1)
                        use(g - 1)

            def route(layer):
                def logits_of(g):
                    for i in range(4):
                        t = 4 * g + i
                        last = nc.tensor.matmul(bank[2][:, t * E:(t + 1) * E], xt4[:, g % 2, i, :], router[:, layer, :],
                                                start=True, stop=True)
                    last.then_inc(sem_of(f"logits_ps{layer}"), 1)
                grouped(f"xt4_ps{layer}", f"xt4_done{layer}", f"ln_out{2 * layer}", lambda g, i: rows[:, 4 * g + i, 0:D],
                        logits_of, lambda g: None)

            def ranks(layer):
                pe.wait_ge(sem_of(f"onehot_done{layer}"), 1)
                nc.tensor.matmul(bank[3][:, 0:(NT + 1) * E], upper[:], onehot[:].rearrange("p t e -> p (t e)"), start=True, stop=False)
                for t in range(NT):
                    last = nc.tensor.matmul(bank[3][:, (t + 1) * E:(NT + 1) * E].rearrange("p (t e) -> p t e", e=E), ones[:],
                                            onehot[:, t:t + 1, :].broadcast_to([P, NT - t, E]), start=False, stop=(t == NT - 1))
                last.then_inc(sem_of(f"ranks_ps{layer}"), 1)

            def experts(layer):
                def transpose_in(j):
                    if isinstance(j.lap, int) and j.n >= SLOT_TILES:
                        return
                    pe.wait_ge(sem_of(f"xg_loaded{layer}_{j.c}"), 16 * j.lap + 16)
                    wait(pe, f"xgt_done{layer}", j.n - 1)
                    nc.tensor.transpose(bank[6 + j.c % 2][:, 0:P], xg[:, j.c, 0:D], ident[:]).then_inc(sem_of(f"tx_ps{layer}"), 1)

                def up(j, half, to):
                    for k in range(FK):
                        last = nc.tensor.matmul(to[:, k * P:(k + 1) * P], w_up[:, j.c % 2, (half * FK + k) * P:(half * FK + k + 1) * P], xgt[:, j.c % 2, :], start=True, stop=True)
                    return last

                def step(j):
                    up_too = not (isinstance(j.lap, int) and j.n >= SLOT_TILES)
                    down_too = not (isinstance(j.lap, int) and j.n == 0)
                    if up_too:
                        pe.wait_ge(sem_of(f"staged_up{layer}"), j.n + 1)
                        pe.wait_ge(sem_of(f"xgt_done{layer}"), j.n + 1)
                        wait(pe, ("silu_done", "biased")[layer], j.n - 1)
                        up(j, 0, bank[j.c % 2]).then_inc(sem_of(f"a_ps{layer}"), 1)
                        if layer == 0:
                            wait(pe, "h_done0", j.n - 1)
                            up(j, 1, bank[4 + j.c % 2]).then_inc(sems["gate_ps"], 1)
                        transpose_in(j.at(1))
                    if down_too:
                        i = j.at(-1)
                        pe.wait_ge(sem_of(f"staged_dn{layer}"), i.n + 1)
                        pe.wait_ge(sem_of(f"h_done{layer}"), i.n + 1)
                        wait(pe, "yo_done0" if layer == 0 else "yb_done", i.n - 1)
                        for k in range(FK):
                            last = nc.tensor.matmul(bank[2 + i.c % 2][:, 0:D], h_t[:, i.c % 2, k, :],
                                                    w_dn[:, i.c % 2, k, :],
                                                    start=(k == 0), stop=(k == FK - 1))
                        last.then_inc(sem_of(f"y_ps{layer}"), 1)
                transpose_in(Tile(0, 0))
                expert_steps(pe, step)

            def project4(lhs, which, to, name):
                for i in range(4):
                    last = nc.tensor.matmul(to[:, i * D:(i + 1) * D], lhs(i), w_attn1[:, which, :], start=True, stop=True)
                last.then_inc(sem_of(name), 1)

            pe.wait_ge(sems["r_loaded"], 16 * 12)
            route(0)
            ctx_tiles = ctx_t[:].rearrange("p b (t c) -> p (b t) c", c=P)
            pe.wait_ge(sems["consts_made"], 13)
            for g in range(G4):
                wait(pe, "mn_done", g - 1)
                project4(lambda i: ctx_tiles[:, 4 * g + i, :], 1, bank[4 + g % 2], "kq_ps")
                wait(pe, "v1_done", g - 1)
                nc.tensor.matmul(bank[6 + g % 2], w_attn1[:, 2, :], ctx_tiles[:, 4 * g:4 * g + 4, :].rearrange("p a c -> p (a c)"),
                                 start=True, stop=True).then_inc(sems["v1_ps"], 1)
                if g == 1:
                    ranks(0)
            pe.wait_ge(sems["v1_done"], G4)
            pe.wait_ge(sems["w1_loaded"], 16)
            pe.wait_ge(sems["w2_loaded"], 16)
            experts(0)

            def project_q(g):
                for i in range(4):
                    last = nc.tensor.matmul(bank[4 + g % 2][:, i * D:(i + 1) * D], xt4[:, g % 2, i, :], w_attn1[:, 0, :],
                                            start=True, stop=True)
                last.then_inc(sems["kq_ps"], 1)
            grouped("xta_ps", "xta_done", "ln_out1", lambda g, i: x_in[:, 4 * g + i, :],
                    project_q, lambda g: wait(pe, "mn_done", G4 + g - 1))
            pe.wait_ge(sems["kq_done"], 2 * G4)
            for b in range(B):
                for t in range(ST):
                    last = nc.tensor.matmul(bank[2 + b // 4][:, (b % 4) * D:(b % 4 + 1) * D], k1[:, b * ST + t, :],
                                            q1[:, b * ST + t, :], start=(t == 0), stop=(t == ST - 1))
                if b % 4 == 3:
                    last.then_inc(sems["s1_ps"], 1)
            for g in range(G4 + 2):
                if g < G4:
                    if g % 2 == 0:
                        pe.wait_ge(sems["s1_done"], g // 2 + 1)
                    wait(pe, "o1_done", g - 1)
                    for i in range(4):
                        t = 4 * g + i
                        last = nc.tensor.matmul(bank[4 + g % 2][:, i * D:(i + 1) * D], v1t[:, t, :], s1[:, t // ST, :],
                                                start=True, stop=True)
                    last.then_inc(sems["o1_ps"], 1)
                if 1 <= g <= G4:
                    pe.wait_ge(sems["o1_done"], g)
                    wait(pe, "ot1_done", g - 2)
                    for i in range(4):
                        last = nc.tensor.transpose(bank[(g - 1) % 2][:, i * P:(i + 1) * P], z1[:, (g - 1) % 2, i, :], ident[:])
                    last.then_inc(sems["ot1_ps"], 1)
                if g >= 2:
                    n = g - 2
                    pe.wait_ge(sems["ot1_done"], n + 1)
                    wait(pe, "x3_done", n - 1)
                    project4(lambda i: xt4[:, n % 2, i, :], 3, bank[6 + n % 2], "wo1_ps")
            pe.wait_ge(sems["x3_done"], G4)
            route(1)
            ranks(1)
            pe.wait_ge(sems["l1_loaded"], 64)
            experts(1)


_P0, _P1 = "L0_xattn_", "L1_xattn_"


def _layout(i):
    import numpy as np
    return {
        "x": i["x"].reshape(B * S, D), "ctx": i["ctx_1024"].transpose(2, 0, 1),
        "wq0": i[_P0 + "wq_w"], "wk0": i[_P0 + "wk_w"], "wv0": i[_P0 + "wv_w"],
        "bq0": i[_P0 + "wq_b"].reshape(HP, P).T, "bk0": i[_P0 + "wk_b"].reshape(HP, P).T, "bv0": i[_P0 + "wv_b"][None],
        "mk0": i[_P0 + "mk"][0].T.reshape(HP, P, MEM).transpose(1, 0, 2), "mv0": i[_P0 + "mv"][0],
        "wo0": i[_P0 + "wo_w"].reshape(H, DK, D).transpose(1, 0, 2), "bo0": i[_P0 + "wo_b"][None],
        "wr0": i["L0_ffn_router_w"], "br0": i["L0_ffn_router_b"][None],
        "w1_0": i["L0_ffn_w1"].transpose(1, 0, 2), "w2_0": i["L0_ffn_w2"].reshape(E, FK, P, D).transpose(2, 0, 1, 3),
        "wq1": i[_P1 + "Wq"], "wk1": i[_P1 + "Wk"], "wv1": i[_P1 + "Wv"], "wo1": i[_P1 + "Wo"],
        "bq1": i[_P1 + "bq"][None], "bk1": i[_P1 + "bk"][None], "bv1": i[_P1 + "bv"][:, None], "bo1": i[_P1 + "bo"][None],
        "wr1": i["L1_ffn_Wr"], "br1": i["L1_ffn_br"][None],
        "w1_1": i["L1_ffn_W1"].transpose(1, 0, 2), "b1_1": i["L1_ffn_b1"].reshape(E, FK, P).transpose(2, 0, 1),
        "w2_1": i["L1_ffn_W2"].reshape(E, FK, P, D).transpose(2, 0, 1, 3), "b2_1": i["L1_ffn_b2"][None],
    }


def kernel(**inputs):
    import numpy as np
    import concourse.bacc as bacc
    from concourse.bass_utils import run_bass_kernel_spmd

    nc = bacc.Bacc("TRN2", target_bir_lowering=False, num_devices=1)
    arrays, io = {}, {}
    for name, a in _layout({k: np.asarray(v) for k, v in inputs.items()}).items():
        arrays["in_" + name] = np.ascontiguousarray(a)
        io[name] = nc.dram_tensor("in_" + name, a.shape, mybir.dt.from_np(a.dtype), kind="ExternalInput").ap()
    io["out"] = nc.dram_tensor("out", (B * S, D), F32, kind="ExternalOutput").ap()
    build(nc, io)
    r = run_bass_kernel_spmd(nc, [arrays], core_ids=[0])
    return r.results[0]["out"].reshape(B, S, D)
```

```python
from contextlib import ExitStack

import concourse.bass as bass
from concourse import mybir

F32 = mybir.dt.float32
F32R = mybir.dt.float32r
BF16 = mybir.dt.bfloat16
I32 = mybir.dt.int32
U32 = mybir.dt.uint32
ACT = mybir.ActivationFunctionType
ALU = mybir.AluOpType
AX_X = mybir.AxisListType.X

P = 128
D = 128
B, S = 8, 256
NT = B * S // P
ST = S // P
H, DK = 16, 64
HP = H // 2
HD = H * DK
MEM = 128
T = S + MEM
KT = T // P
E = 8
FF = 512
FK = FF // P
SLOT_TILES = (B * S + E * (P - 1)) // P
H1, D1 = 16, 8
EPS = 1e-5
ROW = 2 * D + 2
RING = 8
NO_TOKEN = 1 << 20
G4 = NT // 4
PRING = 4
WG = 4
WP = H // WG * ST
VALUES_STEP = (15, 0, 3, 5)
ROT = 11
SIDE = {0: ("values", 0, 1, 0), 1: ("out", 2, 0, -1), 2: ("out", 2, 1, -1), 3: ("values", 1, 0, 0), 4: ("out", 3, 0, -1), 5: ("values", 1, 1, 0),
        6: ("out", 3, 1, -1), 7: ("out", 0, 0, 0), 8: ("out", 0, 1, 0), 11: ("out", 1, 0, 0), 12: ("out", 1, 1, 0),
        13: ("tokens", 0, 0, 1), 15: ("values", 0, 0, 1)}


def f32(ap):
    return ap.bitcast(F32)


def build(nc, io):
    ctx = ExitStack()
    with ctx:
        def sb(name, shape, dt=F32):
            return ctx.enter_context(nc.sbuf_tensor(name, shape, dt))

        def sem(name):
            return ctx.enter_context(nc.semaphore(name))

        ident = sb("ident", [P, P])
        x_in = sb("x_in", [P, NT, D])
        x_mv = sb("x_mv", [P, NT, D + 2])
        x_res = x_mv[:, :, 0:D]
        meanvar = x_mv[:, :, D:D + 2]
        w1_0 = sb("w1_0", [P, E, 2 * FF])
        upper = sb("upper", [P, P], BF16)
        ones = sb("ones", [P, P], BF16)
        before = sb("before", [P, E, E])
        first = sb("first", [P, E])
        tile_no = sb("tile_no", [P, SLOT_TILES])
        block_mask = sb("block_mask", [P, D])
        first_i = sb("first_i", [P, E], I32)
        tile_no_i = sb("tile_no_i", [P, SLOT_TILES], I32)
        token_no = sb("token_no", [P, NT], I32)
        empty_row = sb("empty_row", [P, ROW])
        bias_row = sb("bias_row", [P, 2 + 3 + 2, D])
        bo0_bc = bias_row[:, 0, :]
        bq1_bc, bk1_bc, bo1_bc = (bias_row[:, i, :] for i in (1, 2, 3))
        router = sb("router", [P, 2, E])
        rb_bc = sb("rb_bc", [P, 2, E])
        bv1 = sb("bv1", [P, 1])
        w_attn1 = sb("w_attn1", [P, 4, D])
        stats = sb("stats", [P, NT, 6])
        rstd = sb("rstd", [P, NT])
        unread = sb("unread", [P, 1])
        nt_a = sb("nt_a", [P, NT])
        nt_b = sb("nt_b", [P, NT])
        ctx_t = sb("ctx_t", [P, B, S])
        phase = ExitStack()

        def tmp(name, shape, dt=F32):
            return phase.enter_context(nc.sbuf_tensor(name, shape, dt))

        w_hi = tmp("w_hi", [P, 3, HD], F32R)
        w_lo = tmp("w_lo", [P, 3, HD], F32R)
        bqk = tmp("bqk", [P, 2, HP])
        bqk_s = tmp("bqk_s", [P, 2, HP])
        bv_bc = tmp("bv_bc", [P, HD])
        wo0 = tmp("wo0", [P, H, D])
        xn = tmp("xn", [P, ST, D])
        xt_hi = tmp("xt_hi", [P, S], F32R)
        xt_lo = tmp("xt_lo", [P, S], F32R)
        ct_hi = tmp("ct_hi", [P, S], F32R)
        ct_lo = tmp("ct_lo", [P, S], F32R)
        k_hi = tmp("k_hi", [P, HP, T], F32R)
        k_lo = tmp("k_lo", [P, HP, T], F32R)
        q_hi = tmp("q_hi", [P, 2, S], F32R)
        q_lo = tmp("q_lo", [P, 2, S], F32R)
        v_tmp = tmp("v_tmp", [P, 2, 512])
        v_hl = tmp("v_hl", [P, KT, H, 2, DK], F32R)
        probs = tmp("probs", [P, PRING, ST, T])
        nmax = tmp("nmax", [P, PRING, ST])
        psums = tmp("psums", [P, PRING, ST])
        rsums = tmp("rsums", [P, PRING, ST])
        pt_hi = tmp("pt_hi", [P, 2, KT * S], F32R)
        pt_lo = tmp("pt_lo", [P, 2, KT * S], F32R)
        ot = tmp("ot", [P, H, S])
        wraw = ot[:, 0:12, :].rearrange("p (w a) c -> p w (a c)", w=3)
        mk_raw = ot[:, 12:16, :].rearrange("p a (b c) -> p (a b) c", c=MEM)

        phase.close()
        phase = ctx
        w2_0 = tmp("w2_0", [P, E, FK, D])
        w1_1 = tmp("w1_1", [P, E, FF + FK])
        w2_1 = tmp("w2_1", [P, E, FK + 1, D])
        rows = tmp("rows", [P, NT, ROW])
        onehot = tmp("onehot", [P, NT + 1, E], BF16)
        logits = tmp("logits", [P, NT, E])
        chosen = tmp("chosen", [P, NT, E])
        scr = tmp("scr", [P, NT, E])
        col = [tmp(f"col{i}", [P, NT]) for i in range(3)]
        counts = tmp("counts", [P, E])
        counts_i = tmp("counts_i", [P, E], I32)
        tiles_f = tmp("tiles_f", [P, E])
        base = tmp("base", [P, E])
        sq = tmp("sq", [P, E, E])
        cmp_t = tmp("cmp_t", [P, SLOT_TILES, E])
        texp_f = tmp("texp_f", [P, SLOT_TILES])
        texp = [tmp(f"texp{i}", [P, SLOT_TILES], I32) for i in range(2)]
        slot_f = tmp("slot_f", [P, NT])
        slot = [tmp(f"slot{i}", [P, NT], I32) for i in range(2)]
        xt4 = tmp("xt4", [P, 2, 4, P])
        xg = tmp("xg", [P, RING, ROW])
        xgt = tmp("xgt", [P, 2, P])
        z_t = tmp("z_t", [P, 2, FK, P])
        h_t = tmp("h_t", [P, 2, FK, P])
        w_up = tmp("w_up", [P, 2, 2 * FF])
        w_dn = tmp("w_dn", [P, 2, FK + 1, D])
        yo = tmp("yo", [P, RING, D + 2])
        yo_stats = tmp("yo_stats", [P, 2, 6])
        k1 = tmp("k1", [P, NT, D])
        q1 = rows[:, :, D:2 * D]
        v1t = tmp("v1t", [P, NT, P])
        z1 = tmp("z1", [P, 2, 4, D])
        e1 = tmp("e1", [P, 2, 4, D])
        s1 = tmp("s1", [P, B, D])
        den = tmp("den", [P, NT, H1])

        s_all = ctx.enter_context(nc.psum_tensor("s_all", [P, 4, 512], F32))
        s_ps = [s_all[:, i, :] for i in range(4)]
        pta = ctx.enter_context(nc.psum_tensor("pta", [P, 512], F32))
        ptb = ctx.enter_context(nc.psum_tensor("ptb", [P, 512], F32))
        o_ps = ctx.enter_context(nc.psum_tensor("o_ps", [P, 512], F32))
        m_ps = ctx.enter_context(nc.psum_tensor("m_ps", [P, 512], F32))

        bank = [s_all[:, i, :] for i in range(4)] + [pta[:], ptb[:], o_ps[:], m_ps[:]]

        slots = [nc.dram_tensor(f"slots{i}", [SLOT_TILES * P, ROW], F32, kind="Internal").ap() for i in range(2)]
        x2_dram = nc.dram_tensor("x2_dram", [B * S, D + 2], F32, kind="Internal").ap()

        sems = {}

        names = ("x_loaded ctx_loaded wq_loaded wk_loaded wv_loaded mk_loaded mv_loaded bqk_loaded bvo_loaded wo_loaded "
                 "wq_hi wk_hi wv_hi mk_hi mv_hi wq_lo wk_lo wv_lo mk_lo mv_lo bqk_done ln_self ident_made xb_made "
                 "stats_done dve_self x1_stats "
                 "xn_ready ct_hi_done ct_ready xt_ps xt_hi_done xt_done v_ps v_tmp_done v_hi_done v_done "
                 "k_ps k_hi_done k_done q_ps q_hi_done q_done "
                 "scores_ps max_done exp_done recip_done probs_done pta_ps ptb_ps pta_hi ptb_hi pta_done ptb_done "
                 "o_ps_done ot_done wo_ps x1_done").split()
        for n in names:
            sems[n] = sem(n)

        for i in range(3):
            for n in "ln_var ln_rs ln_out".split():
                sems[f"{n}{i}"] = sem(f"{n}{i}")
        for i in range(2):
            for n in ("xt4_ps xt4_done logits_ps scattered staged_up staged_dn tx_ps xgt_done a_ps h_done y_ps yo_done").split():
                sems[f"{n}{i}"] = sem(f"{n}{i}")
        for c in range(RING):
            for n in "xg_loaded y_stored".split():
                sems[f"{n}_{c}"] = sem(f"{n}_{c}")
        for n in ("onehot_done shifted exps_done ranks_ps gates_done rows_x rows_id texp_done slot_done "
                  "r_loaded w1_loaded w2_loaded l1_loaded empty_made prefilled consts_made act_self x2_loaded xb1_done "
                  "qk_done kq_ps z1_done ex1_done kq_done v1_ps v1_done s1_ps s1_done o1_ps o1_done ot1_ps ot1_done wo1_ps x3_done "
                  "xta_ps xta_done gate_ps silu_done biased b2_mixed pool_mul yo_summed yo_counted").split():
            sems[n] = sem(n)
        sem_of = sems.__getitem__

        class Tile:

            def __init__(self, lap, c):
                self.lap, self.c = (lap + c // RING, c % RING)
                self.n = self.lap * RING + self.c

            def at(self, k):
                return Tile(self.lap, self.c + k)

        def wait(eng, name, value):
            if not isinstance(value, int) or value > 0:
                eng.wait_ge(sem_of(name), value)

        def moved(layer, c, laps):
            return 16 * (layer * ((SLOT_TILES - c + RING - 1) // RING) + laps)

        def expert_steps(eng, step):
            laps = SLOT_TILES // RING
            for c in range(RING):
                step(Tile(0, c))
            with eng.Fori(1, laps) as lap:
                for c in range(RING):
                    step(Tile(lap, c))
            for n in range(laps * RING, SLOT_TILES + 1):
                step(Tile(n // RING, n % RING))

        def side(b, i, first, last):
            kind, n, t, db = SIDE.get(i, SIDE.get(i - H, (None, 0, 0, 0)) if last and i >= H else (None, 0, 0, 0))
            if i >= H:
                return (kind, b, n, t) if kind == "out" and db == -1 else None
            if kind is None or (db == -1 and first) or (db == 1 and last):
                return None
            return kind, b + db, n, t

        def unit_at(b, i, first):
            return (b, i) if i >= 0 else None if first else (b - 1, i + H)

        def attention_steps(eng, step):
            for i in range(ROT):
                step(0, i, True, False)
            with eng.Fori(1, B) as b:
                for i in range(ROT, H):
                    step(b - 1, i, False, False)
                for i in range(ROT):
                    step(b, i, False, False)
            for i in range(ROT, H + 3):
                step(B - 1, i, False, True)
            step(B - 1, H + 4, False, True)
            step(B - 1, H + 6, False, True)

        def side_bank(i):
            return s_ps[2 * ((i - 1) % 2)] if i < H + 3 else s_ps[1 + i // 2 % 2 * 2]

        block = ctx.enter_context(nc.Block())

        @block.sync
        def _(sp):
            sp.dma_start(x_in[:], io["x"].rearrange("(t p) d -> p t d", p=P)).then_inc(sems["x_loaded"], 16)
            sp.dma_start(wraw[:, 0, :], io["wq0"]).then_inc(sems["wq_loaded"], 16)
            sp.dma_start(wraw[:, 1, :], io["wk0"]).then_inc(sems["wk_loaded"], 16)
            sp.dma_start(wraw[:, 2, :], io["wv0"]).then_inc(sems["wv_loaded"], 16)
            sp.dma_start(bv_bc[:], io["bv0"].broadcast_to([P, HD])).then_inc(sems["bvo_loaded"], 16)
            sp.dma_start(bo0_bc, io["bo0"].broadcast_to([P, D])).then_inc(sems["bvo_loaded"], 16)
            sp.dma_start(wo0[0:DK], io["wo0"]).then_inc(sems["wo_loaded"], 16)
            sp.dma_start(wo0[DK:P], io["wo0"]).then_inc(sems["wo_loaded"], 16)
            for i, n in enumerate(("wr0", "wr1")):
                sp.dma_start(router[:, i, :], io[n]).then_inc(sems["r_loaded"], 16)
            for i, n in enumerate(("br0", "br1")):
                sp.dma_start(rb_bc[:, i, :], io[n].broadcast_to([P, E])).then_inc(sems["r_loaded"], 16)
            for i, n in enumerate(("bq1", "bk1", "bo1")):
                sp.dma_start(bias_row[:, 1 + i, :], io[n].broadcast_to([P, D])).then_inc(sems["r_loaded"], 16)
            for i, n in enumerate(("wq1", "wk1", "wv1", "wo1")):
                sp.dma_start(w_attn1[:, i, :], io[n]).then_inc(sems["r_loaded"], 16)
            sp.dma_start(bv1[:], io["bv1"]).then_inc(sems["r_loaded"], 16)
            sp.dma_start(w1_0[:], io["w1_0"]).then_inc(sems["w1_loaded"], 16)
            sp.wait_ge(sems["empty_made"], 2)
            for i in range(2):
                sp.dma_start(slots[i].rearrange("(j p) c -> p j c", p=P),
                             empty_row[:].rearrange("p (a c) -> p a c", a=1).broadcast_to([P, SLOT_TILES, ROW])
                             ).then_inc(sems["prefilled"], 16)
            sp.wait_ge(sems["x1_done"], WP * B)
            sp.dma_start(w2_0[:], io["w2_0"]).then_inc(sems["w2_loaded"], 16)

            def load_slots(layer):
                sp.wait_ge(sem_of(f"scattered{layer}"), 16 * NT)

                def step(j):
                    if isinstance(j.lap, int) and j.n >= SLOT_TILES:
                        return
                    wait(sp, f"y_stored_{j.c}", moved(layer, j.c, j.lap))
                    sp.dma_start(xg[:, j.c, :], slots[layer][bass.ds(j.n * P, P), :]).then_inc(
                        sem_of(f"xg_loaded_{j.c}"), 16)
                expert_steps(sp, step)
                for c in range(RING):
                    sp.wait_ge(sem_of(f"y_stored_{c}"), moved(layer + 1, c, 0))

            load_slots(0)
            sp.dma_start(x_mv[:], x2_dram.rearrange("(t p) d -> p t d", p=P)).then_inc(sems["x2_loaded"], 16)
            load_slots(1)

        @block.gpsimd
        def _(pool):
            nc.gpsimd.memset(ident[:], 0.0).then_inc(sems["ident_made"], 1)
            pool.wait_ge(sems["ident_made"], 1)
            nc.gpsimd.affine_select(out=ident[:], in_=ident[:], compare_op=ALU.not_equal, fill=1.0, base=0,
                                    pattern=[[-1, P]], channel_multiplier=1).then_inc(sems["ident_made"], 1)
            nc.gpsimd.memset(empty_row[:], 0.0).then_inc(sems["empty_made"], 1)
            pool.wait_ge(sems["empty_made"], 1)
            nc.gpsimd.memset(empty_row[:, 2 * D:2 * D + 1].bitcast(I32), NO_TOKEN).then_inc(sems["empty_made"], 1)
            def ctx_rest(b):
                nc.gpsimd.tensor_tensor(ct_lo[:], ctx_t[:, bass.ds(b, 1), :].rearrange("p a s -> p (a s)"), f32(ct_hi[:]),
                                        ALU.subtract).then_inc(sems["ct_ready"], 1)

            def step(b, i, first, last):
                if i == 14 and not last:
                    pool.wait_ge(sems["ct_hi_done"], b + 2)
                    ctx_rest(b + 1)
                if unit_at(b, i - 1, first) and i - 1 < H:
                    ub, u = unit_at(b, i - 1, first)
                    pool.wait_ge(sems["recip_done"], ub * H + u + 1)
                    for t in range(ST):
                        p = probs[:, u % PRING, t, :]
                        nc.gpsimd.tensor_tensor(p, p, rsums[:, u % PRING, t:t + 1].broadcast_to([P, T]),
                                                ALU.mult).then_inc(sems["probs_done"], 1)

            pool.wait_ge(sems["wk_hi"], 1)
            nc.gpsimd.tensor_tensor(w_lo[:, 1, :], wraw[:, 1, :], f32(w_hi[:, 1, :]), ALU.subtract).then_inc(sems["wk_lo"], 1)
            pool.wait_ge(sems["ct_hi_done"], 1)
            ctx_rest(0)
            pool.wait_ge(sems["x_loaded"], 16)
            pool.wait_ge(sems["bvo_loaded"], 32)
            nc.gpsimd.tensor_tensor(x_res[:], x_in[:], bo0_bc.rearrange("p (a d) -> p a d", a=1).broadcast_to([P, NT, D]),
                                    ALU.add).then_inc(sems["xb_made"], 1)
            nc.gpsimd.memset(upper[:], 1.0).then_inc(sems["consts_made"], 1)
            nc.gpsimd.memset(ones[:], 1.0).then_inc(sems["consts_made"], 1)
            nc.gpsimd.memset(before[:], 1.0).then_inc(sems["consts_made"], 1)
            nc.gpsimd.memset(block_mask[:], 1.0).then_inc(sems["consts_made"], 1)
            nc.gpsimd.iota(first_i[:], pattern=[[-1, E]], base=E, channel_multiplier=0).then_inc(sems["consts_made"], 1)
            nc.gpsimd.iota(tile_no_i[:], pattern=[[1, SLOT_TILES]], base=0, channel_multiplier=0).then_inc(sems["consts_made"], 1)
            nc.gpsimd.iota(token_no[:], pattern=[[P, NT]], base=0, channel_multiplier=1).then_inc(sems["consts_made"], 1)
            pool.wait_ge(sems["consts_made"], 7)
            nc.gpsimd.affine_select(out=upper[:], in_=upper[:], compare_op=ALU.is_gt, fill=0.0, base=0,
                                    pattern=[[1, P]], channel_multiplier=-1).then_inc(sems["consts_made"], 1)
            nc.gpsimd.affine_select(out=before[:], in_=before[:], compare_op=ALU.is_gt, fill=0.0, base=0,
                                    pattern=[[1, E], [-1, E]], channel_multiplier=0).then_inc(sems["consts_made"], 1)
            mask = block_mask[:].rearrange("p (h d) -> p h d", d=D1)
            nc.gpsimd.affine_select(out=mask, in_=mask, compare_op=ALU.is_ge, fill=0.0, base=0,
                                    pattern=[[-D1, H1], [0, D1]], channel_multiplier=1).then_inc(sems["consts_made"], 1)
            nc.gpsimd.tensor_copy(first[:], first_i[:]).then_inc(sems["consts_made"], 1)
            nc.gpsimd.tensor_copy(tile_no[:], tile_no_i[:]).then_inc(sems["consts_made"], 1)
            pool.wait_ge(sems["consts_made"], 12)
            nc.gpsimd.affine_select(out=mask, in_=mask, compare_op=ALU.is_ge, fill=0.0, base=D1 - 1,
                                    pattern=[[D1, H1], [0, D1]], channel_multiplier=-1).then_inc(sems["consts_made"], 1)
            attention_steps(pool, step)

            def route(layer):
                if layer == 0:
                    pool.wait_ge(sems["x1_done"], WP * B)
                else:
                    pool.wait_ge(sems["x3_done"], G4)
                nc.gpsimd.tensor_copy(rows[:, :, 2 * D].bitcast(I32), token_no[:]).then_inc(sems["rows_id"], 1)
                pool.wait_ge(sems["rows_id"], layer + 1)
                pool.wait_ge(sems["rows_x"], layer + 1)
                pool.wait_ge(sems["gates_done"], layer + 1)
                pool.wait_ge(sems["slot_done"], layer + 1)
                pool.wait_ge(sems["prefilled"], 32)
                for t in range(NT):
                    nc.gpsimd.indirect_dma_start(slots[layer], bass.IndirectOffsetOnAxis(ap=slot[layer][:, t:t + 1], axis=0),
                                                 rows[:, t, :], None).then_inc(sem_of(f"scattered{layer}"), 16)

                def bias_in(n):
                    if n >= SLOT_TILES:
                        return
                    c = n % RING
                    pool.wait_ge(sem_of(f"xg_loaded_{c}"), moved(layer, c, n // RING + 1))
                    pool.wait_ge(sem_of(f"staged_dn{layer}"), n + 1)
                    nc.gpsimd.tensor_tensor(yo[:, c, 0:D], w_dn[:, n % 2, FK, :], xg[:, c, ROW - 1:ROW].broadcast_to([P, D]),
                                            ALU.mult).then_inc(sems["pool_mul"], 1)
                    pool.wait_ge(sems["pool_mul"], n + 1)
                    nc.gpsimd.tensor_tensor(yo[:, c, 0:D], yo[:, c, 0:D], xg[:, c, D:2 * D], ALU.add).then_inc(sems["b2_mixed"], 1)
                if layer == 1:
                    bias_in(0)
                    bias_in(1)
                for n in range(SLOT_TILES):
                    c = n % RING
                    if layer == 1 and n > 0:
                        bias_in(n + 1)
                    pool.wait_ge(sem_of(f"yo_done{layer}"), n + 1)
                    nc.gpsimd.indirect_dma_start((x2_dram, io["out"])[layer],
                                                 bass.IndirectOffsetOnAxis(ap=xg[:, c, 2 * D:2 * D + 1].bitcast(I32), axis=0),
                                                 yo[:, c, 0:(D + 2, D)[layer]], None, bounds_check=B * S - 1,
                                                 oob_is_err=False).then_inc(sem_of(f"y_stored_{c}"), 16)

            route(0)
            for g in range(G4):
                pool.wait_ge(sems["kq_done"], G4 + g + 1)
                r = slice(4 * g, 4 * g + 4)
                nc.gpsimd.tensor_tensor(rows[:, r, 0:D], k1[:, r, :], q1[:, r, :], ALU.mult).then_inc(sems["qk_done"], 1)
            nc.gpsimd.tensor_tensor(x_res[:], x_res[:], bo1_bc.rearrange("p (a d) -> p a d", a=1).broadcast_to([P, NT, D]),
                                    ALU.add).then_inc(sems["xb1_done"], 1)
            route(1)

        @block.scalar
        def _(act):
            act.dma_start(bqk[:, 0, :], io["bq0"]).then_inc(sems["bqk_loaded"], 16)
            act.dma_start(bqk[:, 1, :], io["bk0"]).then_inc(sems["bqk_loaded"], 16)
            act.dma_start(ctx_t[:], io["ctx"]).then_inc(sems["ctx_loaded"], 16)
            act.dma_start(mk_raw, io["mk0"]).then_inc(sems["mk_loaded"], 16)
            act.dma_start(v_tmp[:, 0:2, :], io["mv0"].rearrange("p (a c) -> p a c", a=2)).then_inc(sems["mv_loaded"], 16)

            act.wait_ge(sems["wq_loaded"], 16)
            nc.scalar.activation(w_hi[:, 0, :], wraw[:, 0, :], ACT.Copy, scale=0.125).then_inc(sems["wq_hi"], 1)
            act.wait_ge(sems["wk_loaded"], 16)
            nc.scalar.activation(w_hi[:, 1, :], wraw[:, 1, :], ACT.Copy).then_inc(sems["wk_hi"], 1)
            act.wait_ge(sems["stats_done"], 1)
            nc.scalar.activation(nt_b[:], nt_a[:], ACT.Ln).then_inc(sems["ln_self"], 1)
            act.wait_ge(sems["ln_self"], 1)
            nc.scalar.activation(rstd[:], nt_b[:], ACT.Exp, scale=-0.5).then_inc(sems["ln_self"], 1)
            act.wait_ge(sems["mk_loaded"], 16)
            nc.scalar.activation(k_hi[:, :, S:T], mk_raw, ACT.Copy).then_inc(sems["mk_hi"], 1)
            def xt(b):
                act.wait_ge(sems["xt_ps"], b + 1)
                nc.scalar.activation(xt_hi[:], side_bank(13)[:, 0:S], ACT.Copy).then_inc(sems["xt_hi_done"], 1)

            def k_part(b, hp):
                act.wait_ge(sems["k_ps"], b * HP + hp + 1)
                nc.scalar.activation(k_hi[:, hp, 0:S], m_ps[:, 0:S], ACT.Identity,
                                     bias=bqk_s[:, 1, hp:hp + 1]).then_inc(sems["k_hi_done"], 1)

            def q_part(b, hp):
                act.wait_ge(sems["q_ps"], b * HP + hp + 1)
                nc.scalar.activation(q_hi[:, hp % 2, :], m_ps[:, 0:S], ACT.Identity,
                                     bias=bqk_s[:, 0, hp:hp + 1]).then_inc(sems["q_hi_done"], 1)

            def values(b, half, t):
                j = 2 * half + t
                act.wait_ge(sems["v_tmp_done"], b * 4 + j + 1)
                nc.scalar.activation(v_hl[:, t, half * 8:half * 8 + 8, 0, :],
                                     v_tmp[:, t, :].rearrange("p (h d) -> p h d", d=DK), ACT.Copy).then_inc(sems["v_hi_done"], 1)

            def step(b, i, first, last):
                if i < H - 2:
                    (q_part if i % 2 else k_part)(b, i // 2 + 1)
                elif i < H and not last:
                    (k_part if i % 2 else q_part)(b + 1, 0)
                if i == 13 and not last:
                    xt(b + 1)
                if unit_at(b, i - 2, first) and i - 2 < H:
                    ub, u = unit_at(b, i - 2, first)
                    wait(act, "o_ps_done", ub * H + u - 1)
                    act.wait_ge(sems["pta_ps"], ub * H + u + 1)
                    nc.scalar.activation(pt_hi[:, u % 2, 0:512], pta[:], ACT.Copy).then_inc(sems["pta_hi"], 1)
                    act.wait_ge(sems["ptb_ps"], ub * H + u + 1)
                    nc.scalar.activation(pt_hi[:, u % 2, 512:768], ptb[:, 0:256], ACT.Copy).then_inc(sems["ptb_hi"], 1)
                if unit_at(b, i - 3, first) and i - 3 < H:
                    ub, u = unit_at(b, i - 3, first)
                    act.wait_ge(sems["o_ps_done"], ub * H + u + 1)
                    nc.scalar.activation(ot[:, u, :], o_ps[:, 0:S], ACT.Copy).then_inc(sems["ot_done"], 1)
                if i < H:
                    wait(act, "ptb_ps", b * H + i - PRING + 1)
                    act.wait_ge(sems["max_done"], b * H + i + 1)
                    for t in range(ST):
                        nc.scalar.activation(probs[:, i % PRING, t, :], s_ps[2 * (i % 2) + t][:, 0:T], ACT.Exp,
                                             bias=nmax[:, i % PRING, t:t + 1],
                                             accum_out=psums[:, i % PRING, t:t + 1]).then_inc(sems["exp_done"], 1)
                task = side(b, i, first, last)
                if task and task[0] == "values":
                    values(*task[1:])
            xt(0)
            act.wait_ge(sems["wv_loaded"], 16)
            nc.scalar.activation(w_hi[:, 2, :], wraw[:, 2, :], ACT.Copy).then_inc(sems["wv_hi"], 1)
            act.wait_ge(sems["bqk_done"], 2)
            q_part(0, 0)
            k_part(0, 0)
            act.wait_ge(sems["mv_loaded"], 16)
            for half in range(2):
                nc.scalar.activation(v_hl[:, KT - 1, half * 8:half * 8 + 8, 0, :],
                                     v_tmp[:, half, :].rearrange("p (h d) -> p h d", d=DK), ACT.Copy).then_inc(sems["mv_hi"], 1)
            values(0, 0, 0)
            attention_steps(act, step)

            n_self = [0]

            def load_table(function):
                nc.scalar.activation(unread[:], ident[:, 0:1], function).then_inc(sems["act_self"], 1)
                n_self[0] += 1
                act.wait_ge(sems["act_self"], n_self[0])

            def ln(k):
                act.wait_ge(sem_of(f"ln_var{k}"), 1)
                nc.scalar.activation(nt_b[:], nt_a[:], ACT.Sqrt).then_inc(sem_of(f"ln_rs{k}"), 1)
                load_table(ACT.Exp)

            def four_transposed(ps, done, used, g, before_it=0):
                act.wait_ge(sem_of(ps), g + 1)
                if g >= 2:
                    act.wait_ge(sem_of(used), before_it + g - 1)
                nc.scalar.activation(xt4[:, g % 2, :, :].rearrange("p a c -> p (a c)"), bank[g % 2], ACT.Copy).then_inc(sem_of(done), 1)

            def route(layer):
                ln(2 * layer)
                if layer == 0:
                    v1_of(0)
                    v1_of(1)
                for g in range(G4):
                    four_transposed(f"xt4_ps{layer}", f"xt4_done{layer}", f"logits_ps{layer}", g)
                nc.scalar.activation(rows[:, :, D:2 * D], x_res[:], ACT.Copy).then_inc(sems["rows_x"], 1)
                act.wait_ge(sems["shifted"], layer + 1)
                nc.scalar.activation(scr[:], scr[:], ACT.Exp).then_inc(sems["exps_done"], 1)

            def experts(layer):
                act.wait_ge(sems["texp_done"], layer + 1)
                act.wait_ge(sems[("w2_loaded", "l1_loaded")[layer]], (16, 64)[layer])
                w2 = (w2_0, w2_1)[layer]

                def stage(j):
                    wait(act, f"y_ps{layer}", j.n - 1)
                    if layer == 1:
                        wait(act, "b2_mixed", j.n - 1)
                    e = act.value_load(texp[layer][0:1, bass.ds(j.n, 1)], min_val=0, max_val=E - 1)
                    nc.scalar.activation(w_dn[:, j.c % 2, 0:w2.shape[2], :], w2[:, bass.ds(e, 1), :, :].rearrange("p a k d -> p (a k) d"),
                                         ACT.Copy).then_inc(sem_of(f"staged_dn{layer}"), 1)

                def xgt_of(j):
                    if isinstance(j.lap, int) and j.n >= SLOT_TILES:
                        return
                    act.wait_ge(sem_of(f"tx_ps{layer}"), j.n + 1)
                    wait(act, "gate_ps" if layer == 0 else "a_ps1", j.n - 1)
                    nc.scalar.activation(xgt[:, j.c % 2, :], bank[6 + j.c % 2][:, 0:P], ACT.Copy).then_inc(sem_of(f"xgt_done{layer}"), 1)

                def step(j):
                    if isinstance(j.lap, int) and j.n >= SLOT_TILES:
                        return
                    r2 = j.c % 2
                    if layer == 0:
                        act.wait_ge(sems["a_ps0"], j.n + 1)
                        wait(act, "h_done0", j.n - 1)
                        nc.scalar.activation(z_t[:, r2].rearrange("p k c -> p (k c)"), bank[r2], ACT.Silu).then_inc(sems["silu_done"], 1)
                        xgt_of(j.at(1))
                        stage(j)
                    else:
                        stage(j)
                        xgt_of(j.at(1))
                        act.wait_ge(sems["biased"], j.n + 1)
                        wait(act, "y_ps1", j.n - 1)
                        nc.scalar.activation(h_t[:, r2].rearrange("p k c -> p (k c)"), z_t[:, r2].rearrange("p k c -> p (k c)"),
                                             ACT.Gelu).then_inc(sems["h_done1"], 1)
                xgt_of(Tile(0, 0))
                expert_steps(act, step)

            def v1_of(n):
                act.wait_ge(sems["v1_ps"], n + 1)
                nc.scalar.activation(v1t[:, 4 * n:4 * n + 4, :].rearrange("p a c -> p (a c)"), bank[6 + n % 2],
                                     ACT.Identity, bias=bv1[:]).then_inc(sems["v1_done"], 1)

            def elu1(n):
                act.wait_ge(sems["z1_done"], n + 1)
                nc.scalar.activation(e1[:, n % 2], z1[:, n % 2], ACT.Exp).then_inc(sems["ex1_done"], 1)
                nc.scalar.activation(z1[:, n % 2], z1[:, n % 2], ACT.Relu).then_inc(sems["ex1_done"], 1)
            load_table(ACT.Sqrt)
            act.wait_ge(sems["x1_done"], WP * B)
            route(0)
            act.dma_start(w1_1[:, :, 0:FF], io["w1_1"]).then_inc(sems["l1_loaded"], 16)
            act.dma_start(w2_1[:, :, 0:FK, :], io["w2_1"]).then_inc(sems["l1_loaded"], 16)
            act.dma_start(w1_1[:, :, FF:FF + FK], io["b1_1"]).then_inc(sems["l1_loaded"], 16)
            act.dma_start(w2_1[:, :, FK, :], io["b2_1"].broadcast_to([P, E, D])).then_inc(sems["l1_loaded"], 16)
            elu1(0)
            elu1(1)
            v1_of(2)
            v1_of(3)
            elu1(2)
            elu1(3)
            load_table(ACT.Silu)
            experts(0)
            ln(1)
            for g in range(G4 + 1):
                if g < G4:
                    four_transposed("xta_ps", "xta_done", "kq_ps", g, G4)
                if g >= 1:
                    elu1(G4 + g - 1)
            for g in range(G4):
                four_transposed("ot1_ps", "ot1_done", "wo1_ps", g)
            load_table(ACT.Sqrt)
            act.wait_ge(sems["x3_done"], G4)
            route(1)
            load_table(ACT.Gelu)
            experts(1)

        @block.vector
        def _(dve):
            n_self = [0]

            def link(ins):
                n_self[0] += 1
                ins.then_inc(sems["dve_self"], 1)
                dve.wait_ge(sems["dve_self"], n_self[0])

            dve.wait_ge(sems["x_loaded"], 16)
            for t in range(NT):
                last = nc.vector.bn_stats(stats[:, t, :], x_in[:, t, :])
            link(last)
            for t in range(NT):
                last = nc.vector.bn_aggr(meanvar[:, t, :], stats[:, t, :])
            link(last)
            nc.vector.tensor_scalar(nt_a[:], meanvar[:, :, 1], EPS, None, ALU.add).then_inc(sems["stats_done"], 1)
            dve.wait_ge(sems["bqk_loaded"], 32)
            nc.vector.tensor_scalar(bqk_s[:, 0, :], bqk[:, 0, :], 0.125, None, ALU.mult).then_inc(sems["bqk_done"], 1)
            nc.vector.tensor_copy(bqk_s[:, 1, :], bqk[:, 1, :]).then_inc(sems["bqk_done"], 1)
            dve.wait_ge(sems["wq_hi"], 1)
            nc.vector.scalar_tensor_tensor(out=w_lo[:, 0, :], in0=wraw[:, 0, :], scalar=0.125, in1=f32(w_hi[:, 0, :]),
                                           op0=ALU.mult, op1=ALU.subtract).then_inc(sems["wq_lo"], 1)
            dve.wait_ge(sems["ln_self"], 2)
            link(nc.vector.tensor_tensor(nt_b[:], rstd[:], rstd[:], ALU.mult))
            link(nc.vector.tensor_tensor(nt_b[:], nt_b[:], nt_a[:], ALU.mult))
            link(nc.vector.tensor_scalar(nt_b[:], nt_b[:], -0.5, 1.5, ALU.mult, ALU.add))
            link(nc.vector.tensor_tensor(rstd[:], rstd[:], nt_b[:], ALU.mult))

            def norm_tiles(b):
                for t in range(ST):
                    n = b * ST + t
                    last = nc.vector.tensor_scalar(xn[:, t, :], x_in[:, bass.ds(n, 1), :].rearrange("p a d -> p (a d)"),
                                                   meanvar[:, bass.ds(n, 1), 0], rstd[:, bass.ds(n, 1)],
                                                   ALU.subtract, ALU.mult)
                    last.then_inc(sems["xn_ready"], 1)

            norm_tiles(0)

            def ctx_hi(b):
                nc.vector.tensor_copy(ct_hi[:], ctx_t[:, bass.ds(b, 1), :].rearrange("p a s -> p (a s)")
                                      ).then_inc(sems["ct_hi_done"], 1)
            dve.wait_ge(sems["ctx_loaded"], 16)
            ctx_hi(0)
            def xt(b):
                dve.wait_ge(sems["xt_hi_done"], b + 1)
                nc.vector.tensor_tensor(xt_lo[:], side_bank(13)[:, 0:S], f32(xt_hi[:]), ALU.subtract).then_inc(sems["xt_done"], 1)

            def k_part(b, hp):
                dve.wait_ge(sems["k_hi_done"], b * HP + hp + 1)
                nc.vector.scalar_tensor_tensor(out=k_lo[:, hp, 0:S], in0=m_ps[:, 0:S], scalar=bqk_s[:, 1, hp:hp + 1],
                                               in1=f32(k_hi[:, hp, 0:S]), op0=ALU.add,
                                               op1=ALU.subtract).then_inc(sems["k_done"], 1)

            def q_part(b, hp):
                dve.wait_ge(sems["q_hi_done"], b * HP + hp + 1)
                nc.vector.scalar_tensor_tensor(out=q_lo[:, hp % 2, :], in0=m_ps[:, 0:S], scalar=bqk_s[:, 0, hp:hp + 1],
                                               in1=f32(q_hi[:, hp % 2, :]), op0=ALU.add,
                                               op1=ALU.subtract).then_inc(sems["q_done"], 1)

            def values(b, half, t):
                j = 2 * half + t
                wait(dve, "v_done", b * 4 + j - 1)
                dve.wait_ge(sems["v_ps"], b * 4 + j + 1)
                nc.vector.tensor_tensor(v_tmp[:, t, :], side_bank(VALUES_STEP[j]), bv_bc[:, half * 512:half * 512 + 512],
                                        ALU.add).then_inc(sems["v_tmp_done"], 1)

            def values_lo(b, half, t):
                j = 2 * half + t
                dve.wait_ge(sems["v_hi_done"], b * 4 + j + 1)
                heads = slice(half * 8, half * 8 + 8)
                nc.vector.tensor_tensor(v_hl[:, t, heads, 1, :], v_tmp[:, t, :].rearrange("p (h d) -> p h d", d=DK),
                                        f32(v_hl[:, t, heads, 0, :]), ALU.subtract).then_inc(sems["v_done"], 1)

            def add_out(b, g, t, bank):
                n = b * WP + g * ST + t
                dve.wait_ge(sems["wo_ps"], n + 1)
                if g > 0:
                    dve.wait_ge(sems["x1_done"], n - 1)
                xr = x_res[:, bass.ds(b * ST + t, 1), :].rearrange("p a d -> p (a d)")
                nc.vector.tensor_tensor(xr, bank[:, 0:D], xr, ALU.add).then_inc(sems["x1_done"], 1)

            def residual_stats(b):
                for t in range(ST):
                    n = b * ST + t
                    nc.vector.bn_stats(stats[:, n, :] if isinstance(n, int) else stats[:, bass.ds(n, 1), :].rearrange("p a c -> p (a c)"),
                                       x_res[:, bass.ds(n, 1), :].rearrange("p a d -> p (a d)")).then_inc(sems["x1_stats"], 1)

            def step(b, i, first, last):
                if i < H:
                    dve.wait_ge(sems["scores_ps"], b * H + i + 1)
                    pair = 2 * (i % 2)
                    nc.vector.tensor_reduce(nmax[:, i % PRING, :], s_all[:, pair:pair + ST, 0:T],
                                            AX_X, ALU.max, negate=True).then_inc(sems["max_done"], 1)
                if i == 10 and not first:
                    dve.wait_ge(sems["x1_done"], (b - 1) * WP + WP)
                if unit_at(b, i - 1, first) and i - 1 < H:
                    ub, u = unit_at(b, i - 1, first)
                    dve.wait_ge(sems["exp_done"], ub * 2 * H + 2 * u + 2)
                    nc.vector.reciprocal(rsums[:, u % PRING, :], psums[:, u % PRING, :]).then_inc(sems["recip_done"], 1)
                if i < H - 2:
                    (q_part if i % 2 else k_part)(b, i // 2 + 1)
                elif i < H and not last:
                    (k_part if i % 2 else q_part)(b + 1, 0)
                task = side(b, i, first, last)
                if task and task[0] == "values":
                    values(*task[1:])
                if task and task[0] == "tokens":
                    xt(task[1])
                if task and task[0] == "out":
                    add_out(*task[1:], side_bank(i))
                if unit_at(b, i - 2, first) and i - 2 < H:
                    ub, u = unit_at(b, i - 2, first)
                    dve.wait_ge(sems["pta_hi"], ub * H + u + 1)
                    nc.vector.tensor_tensor(pt_lo[:, u % 2, 0:512], pta[:], f32(pt_hi[:, u % 2, 0:512]),
                                            ALU.subtract).then_inc(sems["pta_done"], 1)
                    dve.wait_ge(sems["ptb_hi"], ub * H + u + 1)
                    nc.vector.tensor_tensor(pt_lo[:, u % 2, 512:768], ptb[:, 0:256], f32(pt_hi[:, u % 2, 512:768]),
                                            ALU.subtract).then_inc(sems["ptb_done"], 1)
                before = side(b, i - 1, first, last) if i > 0 else ("values", b, 0, 0)
                if before and before[0] == "values":
                    values_lo(*before[1:])
                if i == 13 and not last:
                    dve.wait_ge(sems["k_ps"], b * HP + HP)
                    ctx_hi(b + 1)
                if i == 10 and not first:
                    residual_stats(b - 1)
                if i == 11 and not last:
                    norm_tiles(b + 1)

            xt(0)
            dve.wait_ge(sems["mk_hi"], 1)
            nc.vector.tensor_tensor(k_lo[:, :, S:T], mk_raw, f32(k_hi[:, :, S:T]), ALU.subtract).then_inc(sems["mk_lo"], 1)
            dve.wait_ge(sems["bqk_done"], 2)
            q_part(0, 0)
            dve.wait_ge(sems["wv_hi"], 1)
            nc.vector.tensor_tensor(w_lo[:, 2, :], wraw[:, 2, :], f32(w_hi[:, 2, :]), ALU.subtract).then_inc(sems["wv_lo"], 1)
            k_part(0, 0)
            dve.wait_ge(sems["bvo_loaded"], 32)
            for half in range(2):
                dve.wait_ge(sems["mv_hi"], half + 1)
                nc.vector.tensor_tensor(v_hl[:, KT - 1, half * 8:half * 8 + 8, 1, :],
                                        v_tmp[:, half, :].rearrange("p (h d) -> p h d", d=DK),
                                        f32(v_hl[:, KT - 1, half * 8:half * 8 + 8, 0, :]), ALU.subtract).then_inc(sems["mv_lo"], 1)
            dve.wait_ge(sems["mv_lo"], 2)
            values(0, 0, 0)
            dve.wait_ge(sems["xb_made"], 1)
            attention_steps(dve, step)

            def bn_group(g):
                for t in range(4 * g, 4 * g + 4):
                    last = nc.vector.bn_stats(stats[:, t, :], x_res[:, t, :])
                last.then_inc(sems["x1_stats"], 1)

            def aggregate(tiles, stats_count):
                dve.wait_ge(sems["x1_stats"], stats_count)
                for t in tiles:
                    last = nc.vector.bn_aggr(meanvar[:, t, :], stats[:, t, :])
                return last

            def ln(k, dst, stats_count, rest):
                if rest:
                    link(aggregate(rest, stats_count))
                nc.vector.tensor_scalar(nt_a[:], meanvar[:, :, 1], EPS, None, ALU.add).then_inc(sem_of(f"ln_var{k}"), 1)
                dve.wait_ge(sem_of(f"ln_rs{k}"), 1)
                link(nc.vector.reciprocal(rstd[:], nt_b[:]))
                link(nc.vector.tensor_tensor(nt_b[:], rstd[:], rstd[:], ALU.mult))
                link(nc.vector.tensor_tensor(nt_b[:], nt_b[:], nt_a[:], ALU.mult))
                link(nc.vector.tensor_scalar(nt_b[:], nt_b[:], -0.5, 1.5, ALU.mult, ALU.add))
                link(nc.vector.tensor_tensor(rstd[:], rstd[:], nt_b[:], ALU.mult))
                for t in range(NT):
                    last = nc.vector.tensor_scalar(dst(t), x_res[:, t, :], meanvar[:, t, 0:1], rstd[:, t:t + 1],
                                                   ALU.subtract, ALU.mult)
                    if t % 4 == 3:
                        last.then_inc(sem_of(f"ln_out{k}"), 1)

            def inner(ap, n):
                return ap.rearrange("p (a b) -> p a b", b=1).broadcast_to([P, ap.shape[1], n])

            def outer(ap, n):
                return ap.rearrange("p (b a) -> p b a", b=1).broadcast_to([P, n, ap.shape[1]])

            def route(layer):
                ln(2 * layer, lambda t: rows[:, t, 0:D], NT + G4 * layer, range((NT - ST, NT - 4)[layer], NT))
                link(nc.vector.memset(onehot[:, NT, :], 0.0))
                dve.wait_ge(sem_of(f"logits_ps{layer}"), G4)
                link(nc.vector.tensor_tensor(logits[:], bank[2][:, 0:NT * E].rearrange("p (t e) -> p t e", e=E),
                                             outer(rb_bc[:, layer, :], NT), ALU.add))
                link(nc.vector.tensor_reduce(col[0][:], logits[:], AX_X, ALU.max))
                nc.vector.tensor_tensor(scr[:], logits[:], inner(col[0][:], E), ALU.subtract).then_inc(sems["shifted"], 1)
                link(nc.vector.tensor_tensor(chosen[:], logits[:], inner(col[0][:], E), ALU.is_equal))
                link(nc.vector.tensor_tensor(chosen[:], chosen[:], outer(first[:], NT), ALU.mult))
                link(nc.vector.tensor_reduce(col[1][:], chosen[:], AX_X, ALU.max))
                nc.vector.tensor_tensor(onehot[:, 0:NT, :], chosen[:], inner(col[1][:], E),
                                        ALU.is_equal).then_inc(sems["onehot_done"], 1)
                dve.wait_ge(sems["exps_done"], layer + 1)
                link(nc.vector.tensor_reduce(col[2][:], scr[:], AX_X, ALU.add))
                nc.vector.reciprocal(rows[:, :, ROW - 1], col[2][:]).then_inc(sems["gates_done"], 1)
                dve.wait_ge(sems["ranks_ps"], layer + 1)
                link(nc.vector.tensor_scalar(counts_i[:], bank[3][:, NT * E:(NT + 1) * E], float(P - 1), None, ALU.add))
                link(nc.vector.tensor_scalar(counts_i[:], counts_i[:], 7, None, ALU.arith_shift_right))
                link(nc.vector.tensor_copy(tiles_f[:], counts_i[:]))
                link(nc.vector.tensor_tensor(sq[:], before[:], outer(tiles_f[:], E), ALU.mult))
                link(nc.vector.tensor_reduce(base[:], sq[:], AX_X, ALU.add))
                link(nc.vector.scalar_tensor_tensor(out=scr[:], in0=outer(base[:], NT), scalar=float(P),
                                                    in1=bank[3][:, 0:NT * E].rearrange("p (t e) -> p t e", e=E),
                                                    op0=ALU.mult, op1=ALU.add))
                link(nc.vector.tensor_tensor(scr[:], scr[:], onehot[:, 0:NT, :], ALU.mult))
                link(nc.vector.tensor_reduce(slot_f[:], scr[:], AX_X, ALU.add))
                nc.vector.tensor_copy(slot[layer][:], slot_f[:]).then_inc(sems["slot_done"], 1)
                link(nc.vector.tensor_tensor(counts[:], base[:], tiles_f[:], ALU.add))
                link(nc.vector.tensor_tensor(cmp_t[:], outer(counts[:], SLOT_TILES), inner(tile_no[:], E), ALU.is_le))
                link(nc.vector.tensor_reduce(texp_f[:], cmp_t[:], AX_X, ALU.add))
                nc.vector.tensor_scalar(texp[layer][:], texp_f[:], float(E - 1), None, ALU.min).then_inc(sems["texp_done"], 1)

            def experts(layer):
                dve.wait_ge(sems["texp_done"], layer + 1)

                def expert_of(j):
                    return dve.value_load(texp[layer][0:1, bass.ds(j.n, 1)], min_val=0, max_val=E - 1)

                w1 = (w1_0, w1_1)[layer]

                def stage(j):
                    if isinstance(j.lap, int) and j.n >= SLOT_TILES:
                        return
                    wait(dve, "gate_ps" if layer == 0 else "biased", j.n - 1)
                    nc.vector.tensor_copy(w_up[:, j.c % 2, 0:w1.shape[2]], w1[:, bass.ds(expert_of(j), 1), :].rearrange("p a f -> p (a f)")
                                          ).then_inc(sem_of(f"staged_up{layer}"), 1)

                def step(j):
                    stage(j.at(1))
                    if not (isinstance(j.lap, int) and j.n >= SLOT_TILES):
                        r2 = j.c % 2
                        if layer == 0:
                            dve.wait_ge(sems["silu_done"], j.n + 1)
                            dve.wait_ge(sems["gate_ps"], j.n + 1)
                            wait(dve, "y_ps0", j.n - 1)
                            nc.vector.tensor_tensor(h_t[:, r2].rearrange("p k c -> p (k c)"),
                                                    z_t[:, r2].rearrange("p k c -> p (k c)"), bank[4 + r2],
                                                    ALU.mult).then_inc(sems["h_done0"], 1)
                        else:
                            dve.wait_ge(sems["a_ps1"], j.n + 1)
                            dve.wait_ge(sems["staged_up1"], j.n + 1)
                            wait(dve, "h_done1", j.n - 1)
                            nc.vector.tensor_tensor(z_t[:, r2], bank[r2].rearrange("p (k c) -> p k c", k=FK), inner(w_up[:, r2, FF:FF + FK], P),
                                                    ALU.add).then_inc(sems["biased"], 1)
                    if isinstance(j.lap, int) and j.n == 0:
                        return
                    i = j.at(-1)
                    dve.wait_ge(sem_of(f"y_ps{layer}"), i.n + 1)
                    wait(dve, f"y_stored_{i.c}", moved(layer, i.c, i.lap))
                    if layer == 1:
                        dve.wait_ge(sems["b2_mixed"], i.n + 1)
                    nc.vector.scalar_tensor_tensor(out=yo[:, i.c, 0:D], in0=bank[2 + i.c % 2][:, 0:D], scalar=xg[:, i.c, ROW - 1:ROW],
                                                   in1=xg[:, i.c, D:2 * D] if layer == 0 else yo[:, i.c, 0:D], op0=ALU.mult,
                                                   op1=ALU.add).then_inc(sems["yo_summed" if layer == 0 else "yo_done1"], 1)
                    if layer == 0:
                        dve.wait_ge(sems["yo_summed"], i.n + 1)
                        nc.vector.bn_stats(yo_stats[:, i.c % 2, :], yo[:, i.c, 0:D]).then_inc(sems["yo_counted"], 1)
                        dve.wait_ge(sems["yo_counted"], i.n + 1)
                        nc.vector.bn_aggr(yo[:, i.c, D:D + 2], yo_stats[:, i.c % 2, :]).then_inc(sems["yo_done0"], 1)
                dve.wait_ge(sems["w1_loaded" if layer == 0 else "l1_loaded"], 16 if layer == 0 else 64)
                stage(Tile(0, 0))
                expert_steps(dve, step)

            def elu1_a(n):
                dve.wait_ge(sems["kq_ps"], n + 1)
                wait(dve, "kq_done", n - 1)
                nc.vector.tensor_tensor(z1[:, n % 2], bank[4 + n % 2].rearrange("p (a c) -> p a c", a=4),
                                        outer(bk1_bc if n < G4 else bq1_bc, 4), ALU.add).then_inc(sems["z1_done"], 1)

            def elu1_b(n):
                dve.wait_ge(sems["ex1_done"], 2 * n + 2)
                dst = (k1 if n < G4 else q1)[:, 4 * (n % G4):4 * (n % G4) + 4, :]
                nc.vector.scalar_tensor_tensor(out=dst, in0=e1[:, n % 2], scalar=1.0, in1=z1[:, n % 2],
                                               op0=ALU.min, op1=ALU.add).then_inc(sems["kq_done"], 1)

            dve.wait_ge(sems["r_loaded"], 16 * 12)
            dve.wait_ge(sems["consts_made"], 13)
            aggregate(range(NT - ST), NT - ST)
            dve.wait_ge(sems["x1_done"], WP * B)
            residual_stats(B - 1)
            route(0)
            for n in range(G4 + 1):
                if n < G4:
                    elu1_a(n)
                if n >= 1:
                    elu1_b(n - 1)
            experts(0)
            dve.wait_ge(sems["x2_loaded"], 16)
            ln(1, lambda t: x_in[:, t, :], 0, None)
            for n in range(G4, 2 * G4 + 1):
                if n < 2 * G4:
                    elu1_a(n)
                if n > G4:
                    elu1_b(n - 1)
            for g in range(G4):
                r = slice(4 * g, 4 * g + 4)
                dve.wait_ge(sems["qk_done"], g + 1)
                last = nc.vector.tensor_reduce(den[:, r, :], rows[:, r, 0:D].rearrange("p t (h d) -> p t h d", d=D1), AX_X, ALU.add)
            link(last)
            link(nc.vector.tensor_scalar(den[:], den[:], 1e-6, None, ALU.add))
            for g in range(2):
                dve.wait_ge(sems["s1_ps"], g + 1)
                nc.vector.tensor_tensor(s1[:, 4 * g:4 * g + 4, :], bank[2 + g].rearrange("p (a c) -> p a c", a=4),
                                        outer(block_mask[:], 4), ALU.mult).then_inc(sems["s1_done"], 1)
            link(nc.vector.reciprocal(den[:], den[:]))
            for g in range(G4 + 3):
                if g < G4:
                    r = slice(4 * g, 4 * g + 4)
                    dve.wait_ge(sems["o1_ps"], g + 1)
                    wait(dve, "ot1_ps", g - 1)
                    nc.vector.tensor_tensor(z1[:, g % 2].rearrange("p a (h d) -> p a h d", d=D1),
                                            bank[4 + g].rearrange("p (a h d) -> p a h d", a=4, d=D1),
                                            den[:, r, :].rearrange("p a (h z) -> p a h z", z=1)
                                            .broadcast_to([P, 4, H1, D1]), ALU.mult).then_inc(sems["o1_done"], 1)
                if g >= 4:
                    aggregate(range(4 * g - 16, 4 * g - 12), NT + g - 3)
                if g >= 3:
                    dve.wait_ge(sems["x3_done"], g - 2)
                    bn_group(g - 3)
                if 2 <= g < G4 + 2:
                    n = g - 2
                    dve.wait_ge(sems["xb1_done"], 1)
                    dve.wait_ge(sems["wo1_ps"], n + 1)
                    xr = x_res[:, 4 * n:4 * n + 4, :]
                    nc.vector.tensor_tensor(xr, bank[2 + n % 2].rearrange("p (a c) -> p a c", a=4), xr,
                                            ALU.add).then_inc(sems["x3_done"], 1)
            route(1)
            experts(1)

        @block.tensor
        def _(pe):
            def xt(b):
                pe.wait_ge(sems["xn_ready"], b * ST + ST)
                for t in range(ST):
                    last = nc.tensor.transpose(side_bank(13)[:, t * P:(t + 1) * P], xn[:, t, :], ident[:])
                last.then_inc(sems["xt_ps"], 1)

            def three(out, a_hi, a_lo, b_hi, b_lo):
                nc.tensor.matmul(out, a_hi, b_hi, start=True, stop=False)
                nc.tensor.matmul(out, a_lo, b_hi, start=False, stop=False)
                return nc.tensor.matmul(out, a_hi, b_lo, start=False, stop=True)

            def values(b, half, t):
                j = 2 * half + t
                tk = slice(t * P, t * P + P)
                c = slice(half * 512, half * 512 + 512)
                three(side_bank(VALUES_STEP[j]), ct_hi[:, tk], ct_lo[:, tk], w_hi[:, 2, c], w_lo[:, 2, c]).then_inc(sems["v_ps"], 1)

            def k_part(b, hp):
                if hp == 0:
                    pe.wait_ge(sems["ct_ready"], b + 1)
                    pe.wait_ge(sems["q_done"], b * HP + 1)
                elif hp == 1:
                    pe.wait_ge(sems["k_done"], b * HP + 1)
                else:
                    pe.wait_ge(sems["q_done"], b * HP + hp)
                c = slice(hp * P, hp * P + P)
                three(m_ps[:, 0:S], w_hi[:, 1, c], w_lo[:, 1, c], ct_hi[:], ct_lo[:]).then_inc(sems["k_ps"], 1)

            def q_part(b, hp):
                if hp == 0:
                    pe.wait_ge(sems["xt_done"], b + 1)
                    wait(pe, "q_done", b * HP)
                else:
                    pe.wait_ge(sems["k_done"], b * HP + hp + 1)
                c = slice(hp * P, hp * P + P)
                three(m_ps[:, 0:S], w_hi[:, 0, c], w_lo[:, 0, c], xt_hi[:], xt_lo[:]).then_inc(sems["q_ps"], 1)

            def scores(b, u, first, end):
                hp, rows = u // 2, slice(DK * (u % 2), DK * (u % 2) + DK)
                task = side(b, u - 1, first, end) if u > 0 else ("values", b, 0, 0)
                if task:
                    kind, tb, n, t = task
                    if kind == "values":
                        pe.wait_ge(sems["v_tmp_done"], tb * 4 + 2 * n + t + 1)
                    elif kind == "tokens":
                        pe.wait_ge(sems["xt_done"], tb + 1)
                    else:
                        pe.wait_ge(sems["x1_done"], tb * WP + n * ST + t + 1)
                if u % 2 == 0:
                    pe.wait_ge(sems["k_done" if u == 0 else "q_done"], b * HP + hp + 1)
                wait(pe, "exp_done", b * 2 * H + 2 * u - 2)
                for t in range(ST):
                    c = slice(t * P, t * P + P)
                    last = three(s_ps[2 * (u % 2) + t][:, 0:T], q_hi[rows, hp % 2, c], q_lo[rows, hp % 2, c],
                                 k_hi[rows, hp, :], k_lo[rows, hp, :])
                last.then_inc(sems["scores_ps"], 1)

            def transposes(b, u):
                pe.wait_ge(sems["probs_done"], b * ST * H + ST * u + ST)
                wait(pe, "pta_done", b * H + u)
                for k in range(2):
                    for t in range(ST):
                        last = nc.tensor.transpose(pta[:, (k * ST + t) * P:(k * ST + t + 1) * P],
                                                   probs[:, u % PRING, t, k * P:(k + 1) * P], ident[:])
                last.then_inc(sems["pta_ps"], 1)
                wait(pe, "ptb_done", b * H + u)
                for t in range(ST):
                    last = nc.tensor.transpose(ptb[:, t * P:(t + 1) * P], probs[:, u % PRING, t, 2 * P:3 * P], ident[:])
                last.then_inc(sems["ptb_ps"], 1)

            def weighted(b, u):
                if u % 8 == 0:
                    pe.wait_ge(sems["v_done"], b * 4 + u // 8 * ST + ST)
                wait(pe, "ot_done", b * H + u)
                pe.wait_ge(sems["ptb_done"], b * H + u + 1)
                for k in range(KT):
                    for part in (pt_hi, pt_lo):
                        last = nc.tensor.matmul(o_ps[:, 0:S], v_hl[:, k, u, :, :].rearrange("p a d -> p (a d)"),
                                                part[:, u % 2, k * S:(k + 1) * S],
                                                start=(k == 0 and part is pt_hi), stop=(k == KT - 1 and part is pt_lo))
                last.then_inc(sems["o_ps_done"], 1)

            def project_out(b, g, t, bank):
                pe.wait_ge(sems["ot_done"], b * H + g * WG + WG)
                for h in range(g * WG, g * WG + WG):
                    last = nc.tensor.matmul(bank[:, 0:D], ot[:, h, t * P:(t + 1) * P], wo0[:, h, :],
                                            start=(h == g * WG), stop=(h == g * WG + WG - 1))
                last.then_inc(sems["wo_ps"], 1)

            def step(b, i, first, last):
                if i < H:
                    scores(b, i, first, last)
                if i < H - 2:
                    (q_part if i % 2 else k_part)(b, i // 2 + 1)
                elif i < H and not last:
                    (k_part if i % 2 else q_part)(b + 1, 0)
                task = side(b, i, first, last)
                if task:
                    wait(pe, "exp_done", b * 2 * H + 2 * min(i, H) - (1 if i < H + 1 else 0))
                    if task[0] == "values":
                        values(*task[1:])
                    elif task[0] == "tokens":
                        xt(task[1])
                    else:
                        project_out(*task[1:], side_bank(i))
                if unit_at(b, i - 2, first) and i - 2 < H:
                    transposes(*unit_at(b, i - 2, first))
                if unit_at(b, i - 3, first) and i - 3 < H:
                    weighted(*unit_at(b, i - 3, first))

            def warm_up(to, rounds):
                with pe.Fori(0, rounds):
                    for i in range(4):
                        nc.tensor.transpose(to[:, i * P:(i + 1) * P], ident[:], ident[:])

            pe.wait_ge(sems["ident_made"], 2)
            pe.wait_ge(sems["stats_done"], 1)
            warm_up(o_ps, 4)
            xt(0)
            warm_up(o_ps, 1)
            pe.wait_ge(sems["wq_lo"], 1)
            q_part(0, 0)
            warm_up(o_ps, 1)
            pe.wait_ge(sems["wk_lo"], 1)
            k_part(0, 0)
            warm_up(o_ps, 1)
            pe.wait_ge(sems["wv_lo"], 1)
            values(0, 0, 0)
            warm_up(o_ps, 2)
            pe.wait_ge(sems["mk_lo"], 1)
            pe.wait_ge(sems["mv_lo"], 2)
            pe.wait_ge(sems["wo_loaded"], 32)
            attention_steps(pe, step)

            def grouped(ps, done, ready, src, use, free):
                for g in range(G4 + 1):
                    if g < G4:
                        pe.wait_ge(sem_of(ready), g + 1)
                        wait(pe, done, g - 1)
                        for i in range(4):
                            last = nc.tensor.transpose(bank[g % 2][:, i * P:(i + 1) * P], src(g, i), ident[:])
                        last.then_inc(sem_of(ps), 1)
                    if g >= 1:
                        pe.wait_ge(sem_of(done), g)
                        free(g - 1)
                        use(g - 1)

            def route(layer):
                def logits_of(g):
                    for i in range(4):
                        t = 4 * g + i
                        last = nc.tensor.matmul(bank[2][:, t * E:(t + 1) * E], xt4[:, g % 2, i, :], router[:, layer, :],
                                                start=True, stop=True)
                    last.then_inc(sem_of(f"logits_ps{layer}"), 1)
                grouped(f"xt4_ps{layer}", f"xt4_done{layer}", f"ln_out{2 * layer}", lambda g, i: rows[:, 4 * g + i, 0:D],
                        logits_of, lambda g: None)

            def ranks(layer):
                pe.wait_ge(sems["onehot_done"], layer + 1)
                nc.tensor.matmul(bank[3][:, 0:(NT + 1) * E], upper[:], onehot[:].rearrange("p t e -> p (t e)"), start=True, stop=False)
                for t in range(NT):
                    last = nc.tensor.matmul(bank[3][:, (t + 1) * E:(NT + 1) * E].rearrange("p (t e) -> p t e", e=E), ones[:],
                                            onehot[:, t:t + 1, :].broadcast_to([P, NT - t, E]), start=False, stop=(t == NT - 1))
                last.then_inc(sems["ranks_ps"], 1)

            def experts(layer):
                def transpose_in(j):
                    if isinstance(j.lap, int) and j.n >= SLOT_TILES:
                        return
                    pe.wait_ge(sem_of(f"xg_loaded_{j.c}"), moved(layer, j.c, j.lap + 1))
                    wait(pe, f"xgt_done{layer}", j.n - 1)
                    nc.tensor.transpose(bank[6 + j.c % 2][:, 0:P], xg[:, j.c, 0:D], ident[:]).then_inc(sem_of(f"tx_ps{layer}"), 1)

                def up(j, half, to):
                    for k in range(FK):
                        last = nc.tensor.matmul(to[:, k * P:(k + 1) * P], w_up[:, j.c % 2, (half * FK + k) * P:(half * FK + k + 1) * P], xgt[:, j.c % 2, :], start=True, stop=True)
                    return last

                def step(j):
                    up_too = not (isinstance(j.lap, int) and j.n >= SLOT_TILES)
                    down_too = not (isinstance(j.lap, int) and j.n == 0)
                    if up_too:
                        transpose_in(j.at(1))
                        pe.wait_ge(sem_of(f"staged_up{layer}"), j.n + 1)
                        pe.wait_ge(sem_of(f"xgt_done{layer}"), j.n + 1)
                        wait(pe, ("silu_done", "biased")[layer], j.n - 1)
                        up(j, 0, bank[j.c % 2]).then_inc(sem_of(f"a_ps{layer}"), 1)
                        if layer == 0:
                            wait(pe, "h_done0", j.n - 1)
                            up(j, 1, bank[4 + j.c % 2]).then_inc(sems["gate_ps"], 1)
                    if down_too:
                        i = j.at(-1)
                        pe.wait_ge(sem_of(f"staged_dn{layer}"), i.n + 1)
                        pe.wait_ge(sem_of(f"h_done{layer}"), i.n + 1)
                        wait(pe, ("yo_summed", "yo_done1")[layer], i.n - 1)
                        for k in range(FK):
                            last = nc.tensor.matmul(bank[2 + i.c % 2][:, 0:D], h_t[:, i.c % 2, k, :],
                                                    w_dn[:, i.c % 2, k, :],
                                                    start=(k == 0), stop=(k == FK - 1))
                        last.then_inc(sem_of(f"y_ps{layer}"), 1)
                transpose_in(Tile(0, 0))
                expert_steps(pe, step)

            def project4(lhs, which, to, name):
                for i in range(4):
                    last = nc.tensor.matmul(to[:, i * D:(i + 1) * D], lhs(i), w_attn1[:, which, :], start=True, stop=True)
                last.then_inc(sem_of(name), 1)

            pe.wait_ge(sems["r_loaded"], 16 * 12)
            ctx_tiles = ctx_t[:].rearrange("p b (t c) -> p (b t) c", c=P)
            pe.wait_ge(sems["consts_made"], 13)
            pe.wait_ge(sems["x1_done"], WP * B)

            def from_context(g):
                wait(pe, "v1_done", g - 1)
                nc.tensor.matmul(bank[6 + g % 2], w_attn1[:, 2, :], ctx_tiles[:, 4 * g:4 * g + 4, :].rearrange("p a c -> p (a c)"),
                                 start=True, stop=True).then_inc(sems["v1_ps"], 1)
                wait(pe, "kq_done", g - 1)
                project4(lambda i: ctx_tiles[:, 4 * g + i, :], 1, bank[4 + g % 2], "kq_ps")
            from_context(0)
            from_context(1)
            warm_up(bank[3], 4)
            route(0)
            ranks(0)
            from_context(2)
            from_context(3)
            warm_up(bank[2], 20)
            pe.wait_ge(sems["v1_done"], G4)
            pe.wait_ge(sems["w1_loaded"], 16)
            pe.wait_ge(sems["w2_loaded"], 16)
            experts(0)

            def project_q(g):
                for i in range(4):
                    last = nc.tensor.matmul(bank[4 + g % 2][:, i * D:(i + 1) * D], xt4[:, g % 2, i, :], w_attn1[:, 0, :],
                                            start=True, stop=True)
                last.then_inc(sems["kq_ps"], 1)
            pe.wait_ge(sems["yo_summed"], SLOT_TILES)
            warm_up(bank[3], 18)
            pe.wait_ge(sems["x2_loaded"], 16)
            warm_up(bank[3], 4)
            grouped("xta_ps", "xta_done", "ln_out1", lambda g, i: x_in[:, 4 * g + i, :],
                    project_q, lambda g: wait(pe, "z1_done", G4 + g - 1))
            warm_up(bank[3], 3)
            pe.wait_ge(sems["kq_done"], 2 * G4)
            for b in range(B):
                for t in range(ST):
                    last = nc.tensor.matmul(bank[2 + b // 4][:, (b % 4) * D:(b % 4 + 1) * D], k1[:, b * ST + t, :],
                                            q1[:, b * ST + t, :], start=(t == 0), stop=(t == ST - 1))
                if b % 4 == 3:
                    last.then_inc(sems["s1_ps"], 1)
            for g in range(G4):
                if g % 2 == 0:
                    pe.wait_ge(sems["s1_done"], g // 2 + 1)
                for i in range(4):
                    t = 4 * g + i
                    last = nc.tensor.matmul(bank[4 + g][:, i * D:(i + 1) * D], v1t[:, t, :], s1[:, t // ST, :],
                                            start=True, stop=True)
                last.then_inc(sems["o1_ps"], 1)
            for g in range(G4 + 1):
                if g < G4:
                    pe.wait_ge(sems["o1_done"], g + 1)
                    wait(pe, "ot1_done", g - 1)
                    for i in range(4):
                        last = nc.tensor.transpose(bank[g % 2][:, i * P:(i + 1) * P], z1[:, g % 2, i, :], ident[:])
                    last.then_inc(sems["ot1_ps"], 1)
                if g >= 1:
                    n = g - 1
                    pe.wait_ge(sems["ot1_done"], n + 1)
                    wait(pe, "x3_done", n - 1)
                    project4(lambda i: xt4[:, n % 2, i, :], 3, bank[2 + n % 2], "wo1_ps")
            pe.wait_ge(sems["x3_done"], G4)
            warm_up(bank[3], 7)
            route(1)
            ranks(1)
            pe.wait_ge(sems["l1_loaded"], 64)
            experts(1)


_P0, _P1 = "L0_xattn_", "L1_xattn_"


def _layout(i):
    import numpy as np
    return {
        "x": i["x"].reshape(B * S, D), "ctx": i["ctx_1024"].transpose(2, 0, 1),
        "wq0": i[_P0 + "wq_w"], "wk0": i[_P0 + "wk_w"], "wv0": i[_P0 + "wv_w"],
        "bq0": i[_P0 + "wq_b"].reshape(HP, P).T, "bk0": i[_P0 + "wk_b"].reshape(HP, P).T, "bv0": i[_P0 + "wv_b"][None],
        "mk0": i[_P0 + "mk"][0].T.reshape(HP, P, MEM).transpose(1, 0, 2), "mv0": i[_P0 + "mv"][0],
        "wo0": i[_P0 + "wo_w"].reshape(H, DK, D).transpose(1, 0, 2), "bo0": i[_P0 + "wo_b"][None],
        "wr0": i["L0_ffn_router_w"], "br0": i["L0_ffn_router_b"][None],
        "w1_0": i["L0_ffn_w1"].transpose(1, 0, 2), "w2_0": i["L0_ffn_w2"].reshape(E, FK, P, D).transpose(2, 0, 1, 3),
        "wq1": i[_P1 + "Wq"], "wk1": i[_P1 + "Wk"], "wv1": i[_P1 + "Wv"], "wo1": i[_P1 + "Wo"],
        "bq1": i[_P1 + "bq"][None], "bk1": i[_P1 + "bk"][None], "bv1": i[_P1 + "bv"][:, None], "bo1": i[_P1 + "bo"][None],
        "wr1": i["L1_ffn_Wr"], "br1": i["L1_ffn_br"][None],
        "w1_1": i["L1_ffn_W1"].transpose(1, 0, 2), "b1_1": i["L1_ffn_b1"].reshape(E, FK, P).transpose(2, 0, 1),
        "w2_1": i["L1_ffn_W2"].reshape(E, FK, P, D).transpose(2, 0, 1, 3), "b2_1": i["L1_ffn_b2"][None],
    }


def kernel(**inputs):
    import numpy as np
    import concourse.bacc as bacc
    from concourse.bass_utils import run_bass_kernel_spmd

    nc = bacc.Bacc("TRN2", target_bir_lowering=False, num_devices=1)
    arrays, io = {}, {}
    for name, a in _layout({k: np.asarray(v) for k, v in inputs.items()}).items():
        arrays["in_" + name] = np.ascontiguousarray(a)
        io[name] = nc.dram_tensor("in_" + name, a.shape, mybir.dt.from_np(a.dtype), kind="ExternalInput").ap()
    io["out"] = nc.dram_tensor("out", (B * S, D), F32, kind="ExternalOutput").ap()
    build(nc, io)
    r = run_bass_kernel_spmd(nc, [arrays], core_ids=[0])
    return r.results[0]["out"].reshape(B, S, D)
```
